# Optimizing a Trainium2 kernel written in Bass

```python
import numpy as np
import jax
import jax.numpy as jnp

def _softmax(x, axis=-1):
    return jax.nn.softmax(x, axis=axis)

def _gelu(x):
    return jax.nn.gelu(x, approximate=True)

def _silu(x):
    return jax.nn.silu(x)

def _sigmoid(x):
    return jax.nn.sigmoid(x)

def _layernorm(x, axis=-1, eps=1e-05):
    m = jnp.mean(x, axis=axis, keepdims=True)
    v = jnp.var(x, axis=axis, keepdims=True)
    return (x - m) / jnp.sqrt(v + eps)

def _scatter_add(tgt, idx, src, axis=0):
    return tgt.at[idx].add(src)

def _segment_sum(src, seg, n):
    return jax.ops.segment_sum(src, seg, n)
kernel_name = 'mk_gnn_preln_d4_gnn_r16_7fd9a1'

def setup_inputs(seed: int=0):
    np.random.seed(seed)
    _w = jnp.asarray

    def _rec_inputs():
        import jax
        import jax.numpy as jnp
        _gk = jax.random.key(seed)
        x = -0.0003713 + 1 * jax.random.normal(jax.random.fold_in(_gk, 1), (6250, 256), jnp.float32)
        src = jax.random.randint(jax.random.fold_in(_gk, 2), (100000,), 0, 6250, jnp.int32)
        dst = jnp.minimum((6250 * jax.random.uniform(jax.random.fold_in(_gk, 3), (100000,)) ** 2.0).astype(jnp.int32), 99999)
        _o = jnp.argsort(dst, stable=True)
        src = src[_o]
        dst = dst[_o]
        edge_type_2 = jax.random.randint(jax.random.fold_in(_gk, 13), (100000,), 0, 2, jnp.int32)
        return (x, src, dst, edge_type_2)
    x, src, dst, edge_type_2 = _rec_inputs()

    def _L0_gnn_setup():
        import jax, jax.numpy as jnp
        import numpy as np
        N_NODES = 3125
        N_EDGES = 50000
        IN_CH = 256
        HID_CH = 256
        OUT_CH = 256
        N_LAYERS = 3
        key = jax.random.key(seed)
        ks = jax.random.split(key, 8)
        s_in = 1.0 / np.sqrt(IN_CH)
        s_h = 1.0 / np.sqrt(HID_CH)
        return {'x': jax.random.normal(ks[0], (N_NODES, IN_CH), dtype=jnp.float32), 'W_in': jax.random.normal(ks[1], (IN_CH, HID_CH), dtype=jnp.float32) * s_in, 'b_in': jnp.zeros((HID_CH,), dtype=jnp.float32), 'W_agg': jax.random.normal(ks[2], (N_LAYERS, HID_CH, HID_CH), dtype=jnp.float32) * s_h, 'W_self': jax.random.normal(ks[3], (N_LAYERS, HID_CH, HID_CH), dtype=jnp.float32) * s_h, 'b_hid': jnp.zeros((N_LAYERS, HID_CH), dtype=jnp.float32), 'W_out': jax.random.normal(ks[4], (HID_CH, OUT_CH), dtype=jnp.float32) * s_h, 'b_out': jnp.zeros((OUT_CH,), dtype=jnp.float32), 'edge_index': jax.random.randint(ks[5], (2, N_EDGES), 0, N_NODES, dtype=jnp.int64)}
    _L0_gnn_all = _L0_gnn_setup()
    _L0_gnn_in = {k: v for k, v in _L0_gnn_all.items() if k in ('W_in', 'b_in', 'W_agg', 'W_self', 'b_hid', 'W_out', 'b_out')}
    del _L0_gnn_all

    def _L1_gnn_setup():
        import jax, jax.numpy as jnp
        import numpy as np
        N_NODES = 6250
        N_EDGES = 100000
        D_IN = 256
        HEADS = 8
        D_HEAD = 32
        NEG_SLOPE = 0.2
        BN_EPS = 1e-05
        key = jax.random.key(seed)
        ks = jax.random.split(key, 8)
        x = jax.random.normal(ks[0], (N_NODES, D_IN), dtype=jnp.float32)
        edge_index = jax.random.randint(ks[1], (2, N_EDGES), 0, N_NODES, dtype=jnp.int32)
        W = jax.random.normal(ks[2], (D_IN, HEADS * D_HEAD), dtype=jnp.float32) / np.sqrt(D_IN)
        att_src = jax.random.normal(ks[3], (HEADS, D_HEAD), dtype=jnp.float32) / np.sqrt(D_HEAD)
        att_dst = jax.random.normal(ks[4], (HEADS, D_HEAD), dtype=jnp.float32) / np.sqrt(D_HEAD)
        bias = jax.random.normal(ks[5], (HEADS * D_HEAD,), dtype=jnp.float32) * 0.01
        gamma = jnp.ones((HEADS * D_HEAD,), dtype=jnp.float32)
        beta = jnp.zeros((HEADS * D_HEAD,), dtype=jnp.float32)
        return {'x': x, 'edge_index': edge_index, 'W': W, 'att_src': att_src, 'att_dst': att_dst, 'bias': bias, 'gamma': gamma, 'beta': beta}
    _L1_gnn_all = _L1_gnn_setup()
    _L1_gnn_in = {k: v for k, v in _L1_gnn_all.items() if k in ('W', 'att_src', 'att_dst', 'bias', 'gamma', 'beta')}
    del _L1_gnn_all

    def _L2_gnn_setup():
        import jax, jax.numpy as jnp
        import numpy as np
        N = 3125
        E = 100000
        D = 256
        H = 256
        EPS = 1e-05

        def _gnn_layer(x, row, col, W, b, g, beta):
            n = x.shape[0]
            neigh = x[col]
            agg = jax.ops.segment_sum(neigh, row, num_segments=n)
            deg = jax.ops.segment_sum(jnp.ones((row.shape[0],), x.dtype), row, num_segments=n)
            deg = jnp.maximum(deg, 1.0)[:, None]
            h = (x + agg / deg) @ W.T + b
            mu = jnp.mean(h, axis=-1, keepdims=True)
            var = jnp.mean(jnp.square(h - mu), axis=-1, keepdims=True)
            hn = (h - mu) * jax.lax.rsqrt(var + EPS) * g + beta
            return jax.nn.silu(hn)
        key = jax.random.key(seed)
        ks = jax.random.split(key, 12)
        x = jax.random.normal(ks[0], (N, D), dtype=jnp.float32)
        edge_index = jax.random.randint(ks[1], (2, E), 0, N, dtype=jnp.int32)
        s0 = 1.0 / np.sqrt(D)
        s1 = 1.0 / np.sqrt(H)
        W0 = jax.random.uniform(ks[2], (H, D), jnp.float32, -s0, s0)
        b0 = jax.random.uniform(ks[3], (H,), jnp.float32, -s0, s0)
        g0 = jnp.ones((H,), jnp.float32)
        beta0 = jnp.zeros((H,), jnp.float32)
        W1 = jax.random.uniform(ks[4], (H, H), jnp.float32, -s1, s1)
        b1 = jax.random.uniform(ks[5], (H,), jnp.float32, -s1, s1)
        g1 = jnp.ones((H,), jnp.float32)
        beta1 = jnp.zeros((H,), jnp.float32)
        return {'x': x, 'edge_index': edge_index, 'W0': W0, 'b0': b0, 'g0': g0, 'beta0': beta0, 'W1': W1, 'b1': b1, 'g1': g1, 'beta1': beta1}
    _L2_gnn_all = _L2_gnn_setup()
    _L2_gnn_in = {k: v for k, v in _L2_gnn_all.items() if k in ('W0', 'b0', 'g0', 'beta0', 'W1', 'b1', 'g1', 'beta1')}
    del _L2_gnn_all

    def _L3_gnn_setup():
        import jax, jax.numpy as jnp
        import numpy as np
        N_NODES = 625
        N_EDGES = 20000
        D = 256
        D_OUT = 256
        NUM_REL = 2
        key = jax.random.key(seed)
        ks = jax.random.split(key, 16)
        s = 1.0 / np.sqrt(D)
        inp = {}
        inp['feat'] = jax.random.normal(ks[0], (N_NODES, D), dtype=jnp.float32)
        inp['src'] = jax.random.randint(ks[1], (N_EDGES,), 0, N_NODES, dtype=jnp.int32)
        inp['dst'] = jax.random.randint(ks[2], (N_EDGES,), 0, N_NODES, dtype=jnp.int32)
        inp['rel'] = jax.random.randint(ks[3], (N_EDGES,), 0, NUM_REL, dtype=jnp.int32)
        inp['W_rel'] = jax.random.normal(ks[4], (NUM_REL, D, D), dtype=jnp.float32) * s
        inp['b_rel'] = jax.random.normal(ks[5], (NUM_REL, D), dtype=jnp.float32) * s
        inp['W_ih'] = jax.random.normal(ks[6], (4 * D, D), dtype=jnp.float32) * s
        inp['b_ih'] = jax.random.normal(ks[7], (4 * D,), dtype=jnp.float32) * s
        inp['b_hh'] = jax.random.normal(ks[8], (4 * D,), dtype=jnp.float32) * s
        h = D // 2
        inp['W1'] = jax.random.normal(ks[9], (h, D), dtype=jnp.float32) * s
        inp['b1'] = jax.random.normal(ks[10], (h,), dtype=jnp.float32) * s
        inp['W2'] = jax.random.normal(ks[11], (h, h), dtype=jnp.float32) * (1.0 / np.sqrt(h))
        inp['b2'] = jax.random.normal(ks[12], (h,), dtype=jnp.float32) * (1.0 / np.sqrt(h))
        inp['W3'] = jax.random.normal(ks[13], (D_OUT, h), dtype=jnp.float32) * (1.0 / np.sqrt(h))
        inp['b3'] = jax.random.normal(ks[14], (D_OUT,), dtype=jnp.float32) * (1.0 / np.sqrt(h))
        return inp
    _L3_gnn_all = _L3_gnn_setup()
    _L3_gnn_in = {k: v for k, v in _L3_gnn_all.items() if k in ('W_rel', 'b_rel', 'W_ih', 'b_ih', 'b_hh', 'W1', 'b1', 'W2', 'b2', 'W3', 'b3')}
    del _L3_gnn_all
    return {'x': x, 'src': src, 'dst': dst, 'edge_type_2': edge_type_2, 'L0_gnn_W_in': _L0_gnn_in['W_in'], 'L0_gnn_b_in': _L0_gnn_in['b_in'], 'L0_gnn_W_agg': _L0_gnn_in['W_agg'], 'L0_gnn_W_self': _L0_gnn_in['W_self'], 'L0_gnn_b_hid': _L0_gnn_in['b_hid'], 'L0_gnn_W_out': _L0_gnn_in['W_out'], 'L0_gnn_b_out': _L0_gnn_in['b_out'], 'L1_gnn_W': _L1_gnn_in['W'], 'L1_gnn_att_src': _L1_gnn_in['att_src'], 'L1_gnn_att_dst': _L1_gnn_in['att_dst'], 'L1_gnn_bias': _L1_gnn_in['bias'], 'L1_gnn_gamma': _L1_gnn_in['gamma'], 'L1_gnn_beta': _L1_gnn_in['beta'], 'L2_gnn_W0': _L2_gnn_in['W0'], 'L2_gnn_b0': _L2_gnn_in['b0'], 'L2_gnn_g0': _L2_gnn_in['g0'], 'L2_gnn_beta0': _L2_gnn_in['beta0'], 'L2_gnn_W1': _L2_gnn_in['W1'], 'L2_gnn_b1': _L2_gnn_in['b1'], 'L2_gnn_g1': _L2_gnn_in['g1'], 'L2_gnn_beta1': _L2_gnn_in['beta1'], 'L3_gnn_W_rel': _L3_gnn_in['W_rel'], 'L3_gnn_b_rel': _L3_gnn_in['b_rel'], 'L3_gnn_W_ih': _L3_gnn_in['W_ih'], 'L3_gnn_b_ih': _L3_gnn_in['b_ih'], 'L3_gnn_b_hh': _L3_gnn_in['b_hh'], 'L3_gnn_W1': _L3_gnn_in['W1'], 'L3_gnn_b1': _L3_gnn_in['b1'], 'L3_gnn_W2': _L3_gnn_in['W2'], 'L3_gnn_b2': _L3_gnn_in['b2'], 'L3_gnn_W3': _L3_gnn_in['W3'], 'L3_gnn_b3': _L3_gnn_in['b3']}

def reference(x, src, dst, edge_type_2, L0_gnn_W_in, L0_gnn_b_in, L0_gnn_W_agg, L0_gnn_W_self, L0_gnn_b_hid, L0_gnn_W_out, L0_gnn_b_out, L1_gnn_W, L1_gnn_att_src, L1_gnn_att_dst, L1_gnn_bias, L1_gnn_gamma, L1_gnn_beta, L2_gnn_W0, L2_gnn_b0, L2_gnn_g0, L2_gnn_beta0, L2_gnn_W1, L2_gnn_b1, L2_gnn_g1, L2_gnn_beta1, L3_gnn_W_rel, L3_gnn_b_rel, L3_gnn_W_ih, L3_gnn_b_ih, L3_gnn_b_hh, L3_gnn_W1, L3_gnn_b1, L3_gnn_W2, L3_gnn_b2, L3_gnn_W3, L3_gnn_b3):
    import jax
    import jax.numpy as jnp

    def _L0_gnn_ref(x, W_in, b_in, W_agg, W_self, b_hid, W_out, b_out, edge_index):
        import jax, jax.numpy as jnp
        import numpy as np
        N_NODES = 3125
        N_EDGES = 50000
        IN_CH = 256
        HID_CH = 256
        OUT_CH = 256
        N_LAYERS = 3
        n = x.shape[0]
        dst = edge_index[0]
        src = edge_index[1]
        n_layers = W_agg.shape[0]
        h = x @ W_in + b_in
        deg = jax.ops.segment_sum(jnp.ones_like(dst, dtype=h.dtype), dst, num_segments=n)
        deg = jnp.maximum(deg, 1.0)[:, None]
        for l in range(n_layers):
            agg = jax.ops.segment_sum(h[src], dst, num_segments=n) / deg
            h = jax.nn.relu(agg @ W_agg[l] + h @ W_self[l] + b_hid[l])
        return h @ W_out + b_out

    def _L1_gnn_ref(x, edge_index, W, att_src, att_dst, bias, gamma, beta):
        import jax, jax.numpy as jnp
        import numpy as np
        N_NODES = 6250
        N_EDGES = 100000
        D_IN = 256
        HEADS = 8
        D_HEAD = 32
        NEG_SLOPE = 0.2
        BN_EPS = 1e-05
        N = x.shape[0]
        H, D = att_src.shape
        xh = (x @ W).reshape(N, H, D)
        a_src = jnp.einsum('nhd,hd->nh', xh, att_src)
        a_dst = jnp.einsum('nhd,hd->nh', xh, att_dst)
        loops = jnp.arange(N, dtype=edge_index.dtype)
        src = jnp.concatenate([edge_index[0], loops])
        dst = jnp.concatenate([edge_index[1], loops])
        e = jax.nn.leaky_relu(a_src[src] + a_dst[dst], NEG_SLOPE)
        m = jax.ops.segment_max(e, dst, num_segments=N)
        e = jnp.exp(e - m[dst])
        denom = jax.ops.segment_sum(e, dst, num_segments=N)
        alpha = e / denom[dst]
        msg = xh[src] * alpha[:, :, None]
        out = jax.ops.segment_sum(msg, dst, num_segments=N).reshape(N, H * D) + bias
        mean = jnp.mean(out, axis=0)
        var = jnp.var(out, axis=0)
        out = (out - mean) * jax.lax.rsqrt(var + BN_EPS) * gamma + beta
        return out + x

    def _L2_gnn_ref(x, edge_index, W0, b0, g0, beta0, W1, b1, g1, beta1):
        import jax, jax.numpy as jnp
        import numpy as np
        N = 3125
        E = 100000
        D = 256
        H = 256
        EPS = 1e-05

        def _gnn_layer(x, row, col, W, b, g, beta):
            n = x.shape[0]
            neigh = x[col]
            agg = jax.ops.segment_sum(neigh, row, num_segments=n)
            deg = jax.ops.segment_sum(jnp.ones((row.shape[0],), x.dtype), row, num_segments=n)
            deg = jnp.maximum(deg, 1.0)[:, None]
            h = (x + agg / deg) @ W.T + b
            mu = jnp.mean(h, axis=-1, keepdims=True)
            var = jnp.mean(jnp.square(h - mu), axis=-1, keepdims=True)
            hn = (h - mu) * jax.lax.rsqrt(var + EPS) * g + beta
            return jax.nn.silu(hn)
        row, col = (edge_index[0], edge_index[1])
        x = _gnn_layer(x, row, col, W0, b0, g0, beta0)
        x = _gnn_layer(x, row, col, W1, b1, g1, beta1)
        return x

    def _L3_gnn_ref(feat, src, dst, rel, W_rel, b_rel, W_ih, b_ih, b_hh, W1, b1, W2, b2, W3, b3):
        import jax, jax.numpy as jnp
        import numpy as np
        N_NODES = 625
        N_EDGES = 20000
        D = 256
        D_OUT = 256
        NUM_REL = 2
        n_nodes = feat.shape[0]
        S = feat[src]

        def edge_nn(x, W, b):
            h = jax.nn.relu(x @ W.T + b)
            return jax.nn.relu(h @ W.T + b)
        msgs = jnp.zeros_like(S)
        for r in range(W_rel.shape[0]):
            msgs = jnp.where((rel == r)[:, None], edge_nn(S, W_rel[r], b_rel[r]), msgs)
        agg = jax.ops.segment_sum(msgs, dst, num_segments=n_nodes)
        gates = agg @ W_ih.T + b_ih + b_hh
        i, f, g, o = jnp.split(gates, 4, axis=-1)
        c = jax.nn.sigmoid(i) * jnp.tanh(g)
        hn = jax.nn.sigmoid(o) * jnp.tanh(c)
        x = jax.nn.relu(hn @ W1.T + b1)
        x = jax.nn.relu(x @ W2.T + b2)
        return x @ W3.T + b3
    edge_index = jnp.stack([src, dst])
    h = jnp.maximum(_layernorm(x, axis=-1), 0.0)
    x = x + _L0_gnn_ref(h, L0_gnn_W_in, L0_gnn_b_in, L0_gnn_W_agg, L0_gnn_W_self, L0_gnn_b_hid, L0_gnn_W_out, L0_gnn_b_out, edge_index)
    h = jnp.maximum(_layernorm(x, axis=-1), 0.0)
    x = x + _L1_gnn_ref(h, edge_index, L1_gnn_W, L1_gnn_att_src, L1_gnn_att_dst, L1_gnn_bias, L1_gnn_gamma, L1_gnn_beta)
    h = jnp.maximum(_layernorm(x, axis=-1), 0.0)
    x = x + _L2_gnn_ref(h, edge_index, L2_gnn_W0, L2_gnn_b0, L2_gnn_g0, L2_gnn_beta0, L2_gnn_W1, L2_gnn_b1, L2_gnn_g1, L2_gnn_beta1)
    h = jnp.maximum(_layernorm(x, axis=-1), 0.0)
    x = x + _L3_gnn_ref(h, src, dst, edge_type_2, L3_gnn_W_rel, L3_gnn_b_rel, L3_gnn_W_ih, L3_gnn_b_ih, L3_gnn_b_hh, L3_gnn_W1, L3_gnn_b1, L3_gnn_W2, L3_gnn_b2, L3_gnn_W3, L3_gnn_b3)
    return x

_drawn_inputs = setup_inputs


def setup_inputs(seed=0):
    import zlib

    import numpy as np

    out = dict(_drawn_inputs(seed))
    spreads = {'L0_gnn_b_in': (0.0, 0.1),
     'L0_gnn_b_hid': (0.0, 0.1),
     'L0_gnn_b_out': (0.0, 0.1),
     'L1_gnn_gamma': (1.0, 0.2),
     'L1_gnn_beta': (0.0, 0.1),
     'L2_gnn_g0': (1.0, 0.2),
     'L2_gnn_beta0': (0.0, 0.1),
     'L2_gnn_g1': (1.0, 0.2),
     'L2_gnn_beta1': (0.0, 0.1)}
    factors = {'L1_gnn_bias': 64.0,
     'L2_gnn_b0': 2.747,
     'L2_gnn_b1': 2.883,
     'L3_gnn_b_rel': 4.548,
     'L3_gnn_b_ih': 34.613,
     'L3_gnn_b_hh': 30.394,
     'L3_gnn_b1': 3.833}
    for name, (base, spread) in spreads.items():
        noise = np.random.default_rng([zlib.crc32(name.encode()), seed]).standard_normal(out[name].shape)
        drawn = base * np.exp(spread * noise) if base else spread * noise
        out[name] = jnp.asarray(drawn.astype(out[name].dtype))
    for name, factor in factors.items():
        out[name] = (out[name] * factor).astype(out[name].dtype)
    return out
```

```python
from contextlib import ExitStack

import concourse.bass as bass
from concourse import mybir

F32 = mybir.dt.float32
I32 = mybir.dt.int32
I16 = mybir.dt.int16
BF16 = mybir.dt.bfloat16
ALU = mybir.AluOpType
ACT = mybir.ActivationFunctionType
AX = mybir.AxisListType.X

P = 128
LN_EPS = 1e-5
SLOPE = 0.2


def build(nc, io, out):
    N, D = io["x"].shape
    E = io["src"].shape[0]
    HEADS, DH = io["L1_gnn_att_src"].shape
    T = -(-N // P)
    NP = T * P
    C = -(-E // P)
    EP = C * P
    STEPS = C + T - 1
    U = 10
    HALF = U // 2
    TURNS = STEPS // U
    assert TURNS * U == STEPS
    SB = -(-(STEPS + HALF) // P)
    B = 7
    K = T // B
    assert K * B == T
    GW = D + HEADS
    NODE = 14
    assert 2 * NP <= 1 << NODE
    LAST = N - (T - 1) * P
    H2 = D // 2
    Q = D // P

    ctx = ExitStack()
    with ctx:
        def sb(name, shape, dt=F32):
            return ctx.enter_context(nc.sbuf_tensor(name, shape, dt))

        sems = {}

        def sem(name):
            if name not in sems:
                sems[name] = ctx.enter_context(nc.semaphore(name))
            return sems[name]

        def dram(name, shape, dt=F32):
            return nc.dram_tensor(name, shape, dt).ap()

        BY_DST, BY_SRC = 0, 1
        recs = [dram("recs_by_dst", (C, P), I32), dram("recs_by_src", (C, P), I32)]
        tile_row_dram = dram("tile_row_dram", (2, SB, P), I16)
        table = dram("table", (NP, D))
        gat_table = dram("gat_table", (NP, GW))
        rel_table = dram("rel_table", (2 * NP, D))
        res = dram("res", (NP, D))

        def tiled(ap):
            return ap.rearrange("(t p) c -> p t c", p=P)

        acc = sb("acc", [P, T, GW])
        own = sb("own", [P, T, D])
        idx_by_src = sb("idx_by_src", [P, SB * P], I16)
        idx_rel = sb("idx_rel", [P, SB * P], I16)
        idx_by_dst = sb("idx_by_dst", [P, SB * P], I16)
        node_loc = sb("node_loc", [P, 2, SB * P], BF16)
        tile_row = sb("tile_row", [1, 2, SB * P], I16)
        ring = sb("ring", [P, U, GW])
        idx_slot = sb("idx_slot", [P, 2 * U], I32)
        onehot = sb("onehot", [P, 2 * U, P])
        onehot_t = sb("onehot_t", [P, HALF, P])
        hbuf = sb("hbuf", [P, B, D])
        hT = sb("hT", [P, B * Q, P])
        tbuf = sb("tbuf", [P, B, GW])
        xb = sb("xb", [P, B, D])
        rb = sb("rb", [P, B, D])
        wbuf = sb("wbuf", [P, Q, 1152])
        gat_ring = [ring[:, 0:HALF, :], ring[:, HALF:U, :], tbuf[:, 0:HALF, :],
                    hbuf[:, :, :].rearrange("p j d -> p (j d)")[:, 0:HALF * GW].rearrange("p (u c) -> p u c", c=GW)]
        pbuf = sb("pbuf", [P, 1536])
        iota_row = sb("iota_row", [P, P])
        ident = sb("ident", [P, P])
        ones = sb("ones", [P, P])
        ones_last = sb("ones_last", [P, P])
        part = sb("part", [P, 1])
        rdeg = sb("rdeg", [P, T])
        st = sb("st", [P, B, 6])
        mv = sb("mv", [P, B, 2])
        sd = sb("sd", [P, B])
        rstd = sb("rstd", [P, B])
        nmr = sb("nmr", [P, B])
        a_own = sb("a_own", [P, T, HEADS])
        dst_tab = sb("dst_tab", [P, T, 2 * HEADS])
        w_self = sb("w_self", [P, T, HEADS])
        zlog = sb("zlog", [P, HALF, HEADS])
        zlog2 = sb("zlog2", [P, HALF, HEADS])
        amax = sb("amax", [P, HEADS])
        amax7 = sb("amax7", [P, HEADS])
        gdiag = sb("gdiag", [HEADS, HEADS])
        gmax = sb("gmax", [HEADS, 1])
        gmax_b = sb("gmax_b", [P, HEADS])
        den = sb("den", [P, B, HEADS])
        bn_sum = sb("bn_sum", [P, D])
        bn_a = sb("bn_a", [P, D])
        bn_b = sb("bn_b", [P, D])
        bn_mean = sb("bn_mean", [P, D])
        carrier = sb("carrier", [P, 8])
        acc_flat = acc[:, :, :].rearrange("p t c -> p (t c)")
        at = [0]

        def place(n, dt=F32):
            words = n if dt in (F32, I32) else -(-n // 2)
            ap = acc_flat[:, at[0]:at[0] + words]
            at[0] += words
            assert at[0] <= T * GW
            return ap if dt == F32 else ap.bitcast(dt)[:, 0:n]

        edges = place(3 * C, I32).rearrange("p (a c) -> p a c", a=3)
        rec_sb = [place(C, I32), place(C, I32)]
        key_tile = place(C, BF16)
        is_tile = place(C, I16)
        running = place(C)
        all_ones = place(C)
        position = place(C)
        pos_i = place(C, I32)
        counts, totals, ends, starts = (place(T) for _ in range(4))
        SLOTS = 17
        SORT_TURNS = C // (2 * SLOTS)
        assert SORT_TURNS * 2 * SLOTS == C
        pos_slot = place(2 * SLOTS, I32)
        rec_slot = place(2 * SLOTS, I32)
        bounds = place(C)
        junk = place(C)
        edge_rows = place(SB * P, I32).rearrange("p (s e) -> p s e", s=SB)
        edge_i = onehot[:, 0:SB, :].bitcast(I32)
        edge_f = rb[:, 0:SB, :].rearrange("p j (a e) -> p a j e", a=2)
        last_rec, last_tile = (edges[0:1, a, :] for a in range(2))
        bound_row = edges[0:1, 2, :].bitcast(F32)
        chunk_row = place(C)[0:1, :]
        step_no, chunk_f, chunk_c, tile_f, tile_base = (place(SB) for _ in range(5))
        chunk_i = place(SB, I32)
        tile_i = place(SB, I16)
        zrows = xb[:, 0, :]
        before = hbuf[:, 0, 0:P]

        psum = ctx.enter_context(nc.psum_tensor("psum", [P, 8, 512], F32))
        psT = psum[:, 0:4, :].rearrange("p b (f c) -> p (b f) c", c=P)
        GB = HALF
        ps_oh = psum[:, 5:7, :].rearrange("p b (f c) -> p (b f) c", c=P)
        ps_log = psum[:, 7, 0:HALF * 2 * HEADS].rearrange("p (u h) -> p u h", u=HALF)

        LOADS = {
            "in": ([("W_in", io["L0_gnn_W_in"]), ("agg", io["L0_gnn_W_agg"][0]), ("self", io["L0_gnn_W_self"][0])],
                   [("b_in", io["L0_gnn_b_in"]), ("b_hid", io["L0_gnn_b_hid"][0])]),
            "l0": ([("agg", io["L0_gnn_W_agg"][1]), ("self", io["L0_gnn_W_self"][1])], [("b_hid", io["L0_gnn_b_hid"][1])]),
            "l1": ([("agg", io["L0_gnn_W_agg"][2]), ("self", io["L0_gnn_W_self"][2])], [("b_hid", io["L0_gnn_b_hid"][2])]),
            "l2": ([("W_out", io["L0_gnn_W_out"]), ("W_gat", io["L1_gnn_W"])],
                   [("b_out", io["L0_gnn_b_out"]), ("att_src", io["L1_gnn_att_src"].rearrange("h d -> (h d)")),
                    ("att_dst", io["L1_gnn_att_dst"].rearrange("h d -> (h d)"))]),
            "ga": ([("W0", io["L2_gnn_W0"])],
                   [("bias", io["L1_gnn_bias"]), ("gamma", io["L1_gnn_gamma"]), ("beta", io["L1_gnn_beta"])]),
            "s0": ([("W1", io["L2_gnn_W1"])],
                   [("b", io["L2_gnn_b0"]), ("g", io["L2_gnn_g0"]), ("beta", io["L2_gnn_beta0"])]),
            "s1": ([("R0", io["L3_gnn_W_rel"][0]), ("R1", io["L3_gnn_W_rel"][1])],
                   [("b", io["L2_gnn_b1"]), ("g", io["L2_gnn_g1"]), ("beta", io["L2_gnn_beta1"]),
                    ("b0", io["L3_gnn_b_rel"][0]), ("b1", io["L3_gnn_b_rel"][1])]),
            "fi": ([("ih", io["L3_gnn_W_ih"]), ("W3", io["L3_gnn_W3"])],
                   [("bi", io["L3_gnn_b_ih"]), ("b1", io["L3_gnn_b1"]), ("b2", io["L3_gnn_b2"]), ("b3", io["L3_gnn_b3"])]),
        }
        W, R, NLOADS = {}, {}, {}
        for ph, (ws, rs) in LOADS.items():
            at = 0
            for name, ap in ws:
                if name == "W3":
                    continue
                W[ph, name] = at
                at += ap.shape[1]
            at = 0
            for name, ap in rs:
                R[ph, name] = at
                at += ap.shape[0]
            NLOADS[ph] = len(ws) + len(rs)
        W1_AT = 4 * D
        NLOADS["fi"] += 3
        w2 = onehot_t[:, 0, :]
        w3 = onehot[:, 0:2, :].rearrange("p a c -> p (a c)")
        bhh = ring[:, 0:4, 0:D]

        def row(ph, name, n=D):
            return pbuf[:, R[ph, name]:R[ph, name] + n]

        def over_batch(ap):
            return ap.unsqueeze(1).broadcast_to([P, B, ap.shape[1]])

        def heads(ap):
            return ap.rearrange("p (h d) -> p h d", h=HEADS)

        block = ctx.enter_context(nc.Block())
        PASSES = ["in", "l0", "l1", "l2", "ga", "s0", "s1"]
        STORED = {ph: (ph + "_stored", 16 * K) for ph in PASSES} | {"s1": ("s1_stored", 32 * K)}
        ACC_READ = {ph: ph + "_pre" for ph in PASSES} | {"ga": "ga_x2"}
        TRANSPOSED = {"in": ["in_u", "in_tab"], "l0": ["l0_tab"], "l1": ["l1_tab"], "l2": ["l2_u", "l2_tab"],
                      "ga": ["ga_tab"], "s0": ["s0_tab"], "s1": ["s1_u0", "s1_v0", "s1_u1", "s1_v1"],
                      "fi": ["fi_i", "fi_1", "fi_2", "fi_3"]}
        PRODUCTS = TRANSPOSED | {"fi": ["fi_i", "fi_g", "fi_o", "fi_1", "fi_2", "fi_3"]}
        TABLES = {ph: [ph + "_tab"] for ph in PASSES if ph != "s1"}
        NORMS = {"in": ["in"], "l2": ["l2"], "ga": ["ga"], "s0": ["s0"], "s1": ["s1", "s1b"]}
        LN_BIASED = {"in": ["in"], "l2": ["l2"], "ga": ["ga"], "s1": ["s1b"]}

        PRODUCT_UNITS = [u for names in PRODUCTS.values() for u in names]

        def count(units, k, unit, items=1, j=None):
            before = 0
            for names in units.values():
                if unit in names:
                    at = before * K + names.index(unit)
                    return k * (len(names) * items) + (at * items + (items if j is None else j + 1))
                before += len(names)

        ORDER = [BY_DST if ph in ("l2", "s1") else BY_SRC for ph in PASSES]
        GAT = PASSES.index("l2")
        HALVES, FIRST, TAIL = STEPS // HALF, 2, 4
        GAT_TURNS = (HALVES - FIRST - TAIL) // 4
        assert FIRST + 4 * GAT_TURNS + TAIL == HALVES
        ONEHOTS = [g * (STEPS + HALF) - (HALF if g > GAT else 0) for g in range(len(PASSES))]

        def filled(g, h):
            n = -(-(HALVES - h) // 4)
            return (TURNS * (g - (g > GAT)) if h < 2 else 0) + (n if g > GAT else 0)

        def slot_sem(r, u):
            return sem(f"gathered{r * HALF + u}") if r < 2 else sem(f"gathered_half{r}")

        def gat_halves(eng, half):
            for n in range(FIRST):
                half(n, n)
            with eng.Fori(0, GAT_TURNS) as i:
                for r in range(4):
                    half(i * 4 + (FIRST + r), (FIRST + r) % 4)
            for n in range(HALVES - TAIL, HALVES):
                half(n, n % 4)


        @block.sync
        def _(sp):
            def load_params(ph):
                ws, rs = LOADS[ph]
                done = sem(ph + "_params")
                for name, ap in ws:
                    n = ap.shape[1]
                    to, of = (w3, ap) if name == "W3" else (wbuf[:, :, W[ph, name]:W[ph, name] + n], ap.rearrange("(q p) n -> p q n", p=P))
                    if name != "W3":
                        sp.dma_start(to, of).then_inc(done, 16)
                for name, ap in rs:
                    n = ap.shape[0]
                    sp.dma_start(pbuf[:, R[ph, name]:R[ph, name] + n],
                                 ap.unsqueeze(0).broadcast_to([P, n])).then_inc(done, 16)

            def rows(ap, k, first=0):
                return tiled(ap)[:, bass.ds(k * B + first, B), :]

            sp.dma_start(res[0:N, :], io["x"]).then_inc(sem("x_copied"), 16)
            sp.wait_ge(sem("pads_set"), 1)
            for n, a in enumerate((io["src"], io["dst"], io["edge_type_2"])):
                whole = E // C
                most = whole // 16 * 16
                for p, q in ((0, most), (most, whole)):
                    sp.dma_start(edges[p:q, n, :], a[p * C:q * C].rearrange("(p c) -> p c", c=C)).then_inc(sem("edges"), 16)
                sp.dma_start(edges[whole:whole + 1, n, 0:E - whole * C], a[whole * C:E].unsqueeze(0)).then_inc(sem("edges"), 16)
            sp.dma_start(res[N:NP, :], zrows[0:NP - N, :]).then_inc(sem("x_copied"), 16)
            load_params("in")
            sp.wait_ge(sem("rec_by_dst"), 1)
            sp.dma_start(recs[BY_DST].rearrange("c e -> (c e)").rearrange("(p c) -> p c", c=C), rec_sb[BY_DST]).then_inc(sem("rec_stored"), 16)
            sp.wait_ge(sem("rec_stored"), 16)

            def chunk_ends(o):
                sp.dma_start(last_rec, recs[o][:, P - 1:P].rearrange("c o -> o c"), allow_slow_non_contiguous=True).then_inc(sem("last_rec"), 16)

            def step_tiles(o):
                sp.wait_ge(sem("tile_i"), o + 1)
                for s in range(SB):
                    sp.dma_start(tile_row_dram[o, s:s + 1, :].rearrange("o p -> p o"), tile_i[:, s:s + 1]).then_inc(sem("tile_out"), 16)
                sp.wait_ge(sem("tile_out"), 16 * SB * (o + 1))
                sp.dma_start(tile_row[0:1, o, :], tile_row_dram[o].rearrange("s p -> (s p)").unsqueeze(0)).then_inc(sem("tile_row"), 16)

            chunk_ends(BY_DST)
            sp.wait_ge(sem("x_copied"), 32)
            sp.dma_start(xb[:], rows(res, 0)).then_inc(sem("in_x"), 16)
            step_tiles(BY_DST)

            def first(k, more):
                if more:
                    sp.wait_ge(sem("in_h"), k + 1)
                    sp.dma_start(xb[:], rows(res, k + 1)).then_inc(sem("in_x"), 16)
                sp.wait_ge(sem("taken_act"), count(TABLES, k, "in_tab", B))
                sp.dma_start(rows(table, k), tbuf[:, :, 0:D]).then_inc(sem("in_stored"), 16)

            def table_out(ph):
                def step(k, more):
                    sp.wait_ge(sem("taken_act"), count(TABLES, k, ph + "_tab", B))
                    sp.dma_start(rows(table, k), tbuf[:, :, 0:D]).then_inc(sem(ph + "_stored"), 16)
                return step

            def batches(step):
                with sp.Fori(0, K - 1) as k:
                    step(k, True)
                step(K - 1, False)

            def settled(ph):
                sp.wait_ge(sem(STORED[ph][0]), STORED[ph][1])
                if ph != "s1":
                    sp.wait_ge(sem("taken_dve"), count(PRODUCTS, K - 1, ph + "_tab", B))

            batches(first)
            for h in range(2):
                sp.wait_ge(sem(f"scattered{h}"), 16 * SLOTS * SORT_TURNS)
            chunk_ends(BY_SRC)
            step_tiles(BY_SRC)
            for prev, ph in (("in", "l0"), ("l0", "l1")):
                settled(prev)
                load_params(ph)
                batches(table_out(ph))

            def l2(k, more):
                sp.wait_ge(sem("l2_res"), k + 1)
                sp.dma_start(rows(res, k), rb[:]).then_inc(sem("l2_rstored"), 16)
                if more:
                    sp.wait_ge(sem("l2_rstored"), k * 16 + 16)
                    sp.dma_start(rb[:], rows(res, k + 1)).then_inc(sem("l2_r"), 16)
                sp.wait_ge(sem("taken_act"), count(TABLES, k, "l2_tab", B))
                sp.dma_start(rows(gat_table, k), tbuf[:]).then_inc(sem("l2_stored"), 16)

            settled("l1")
            load_params("l2")
            sp.dma_start(rb[:], rows(res, 0)).then_inc(sem("l2_r"), 16)
            batches(l2)

            def ga_own(k, more):
                if more:
                    sp.wait_ge(sem("ga_self"), k + 1)
                    sp.dma_start(tbuf[:], rows(gat_table, k + 1)).then_inc(sem("ga_xh"), 16)

            def ga(k, more):
                sp.wait_ge(sem("ga_x2"), k + 1)
                sp.dma_start(rows(res, k), xb[:]).then_inc(sem("ga_rstored"), 16)
                if more:
                    sp.dma_start(rb[:], rows(res, k + 1)).then_inc(sem("ga_r"), 16)
                sp.wait_ge(sem("taken_act"), count(TABLES, k, "ga_tab", B))
                sp.dma_start(rows(table, k), tbuf[:, :, 0:D]).then_inc(sem("ga_stored"), 16)

            settled("l2")
            sp.wait_ge(sem("l2_rstored"), 16 * K)
            load_params("ga")
            sp.wait_ge(sem("mm"), U + STEPS * (GAT + 1))
            sp.dma_start(tbuf[:], rows(gat_table, 0)).then_inc(sem("ga_xh"), 16)
            sp.dma_start(rb[:], rows(res, 0)).then_inc(sem("ga_r"), 16)
            batches(ga_own)
            batches(ga)
            settled("ga")
            load_params("s0")
            batches(table_out("s0"))

            def s1(k, more):
                sp.wait_ge(sem("s1_x3"), k + 1)
                sp.dma_start(rows(res, k), xb[:]).then_inc(sem("s1_rstored"), 16)
                for r in range(2):
                    sp.wait_ge(sem(f"s1_m{r}"), k + 1)
                    sp.dma_start(rows(rel_table, k, r * T), tbuf[:, :, 0:D]).then_inc(sem("s1_stored"), 16)
                if more:
                    sp.dma_start(rb[:], rows(res, k + 1)).then_inc(sem("s1_r"), 16)

            settled("s0")
            load_params("s1")
            sp.wait_ge(sem("ga_rstored"), 16 * K)
            sp.dma_start(rb[:], rows(res, 0)).then_inc(sem("s1_r"), 16)
            batches(s1)
            settled("s1")
            load_params("fi")
            sp.wait_ge(sem("summed"), GB + len(PASSES) * STEPS)
            done = sem("fi_params")
            sp.dma_start(wbuf[:, :, W1_AT:W1_AT + H2], io["L3_gnn_W1"].rearrange("(q p) n -> p q n", p=P)).then_inc(done, 16)
            sp.dma_start(w2, io["L3_gnn_W2"]).then_inc(done, 16)
            sp.dma_start(w3, io["L3_gnn_W3"]).then_inc(done, 16)
            sp.dma_start(bhh, io["L3_gnn_b_hh"].rearrange("(a d) -> a d", d=D).unsqueeze(0).broadcast_to([P, 4, D])).then_inc(done, 16)

            out_t = out[0:(T - 1) * P, :].rearrange("(t p) c -> p t c", p=P)
            sp.wait_ge(sem("s1_rstored"), 16 * K)
            sp.dma_start(tbuf[:, :, 0:D], rows(res, 0)).then_inc(sem("fi_r"), 16)
            with sp.Fori(0, K - 1) as k:
                sp.wait_ge(sem("fi_y"), k + 1)
                sp.dma_start(out_t[:, bass.ds(k * B, B), :], tbuf[:, :, 0:D]).then_inc(sem("out_stored"), 16)
                sp.wait_ge(sem("out_stored"), k * 16 + 16)
                sp.dma_start(tbuf[:, :, 0:D], rows(res, k + 1)).then_inc(sem("fi_r"), 16)
            sp.wait_ge(sem("fi_y"), K)
            sp.dma_start(out_t[:, (K - 1) * B:T - 1, :], tbuf[:, 0:B - 1, 0:D]).then_inc(sem("out_stored"), 16)
            sp.dma_start(out[(T - 1) * P:N, :], tbuf[0:LAST, B - 1, 0:D]).then_inc(sem("out_stored"), 16)
            sp.wait_ge(sem("out_stored"), 16 * (K + 1))

        @block.gpsimd
        def _(pool):
            halves = [pool.alloc_register(f"halves{h}") for h in range(2)]
            sorts = [pool.alloc_register(f"sorts{h}") for h in range(2)]
            gat_puts = [pool.alloc_register(f"gat_puts{r}") for r in range(4)]
            for r in halves + sorts + gat_puts:
                pool.reg_mov(r, 0)
            exact = dict(allow_small_or_imprecise_dtypes=True)
            nc.gpsimd.iota(iota_row[:], [[1, P]], base=0, channel_multiplier=0, **exact).then_inc(sem("iota"), 1)
            nc.gpsimd.iota(part[:], [[0, 1]], base=0, channel_multiplier=1, **exact).then_inc(sem("iota"), 1)
            nc.gpsimd.iota(step_no, [[P, SB]], base=0, channel_multiplier=1, **exact).then_inc(sem("iota"), 1)
            nc.gpsimd.iota(chunk_row, [[1, C]], base=1, channel_multiplier=0, **exact).then_inc(sem("iota"), 1)

            def step_edges(o):
                pool.wait_ge(sem("chunk_i"), o + 1)
                for s in range(SB):
                    nc.gpsimd.indirect_dma_start(
                        out=edge_rows[:, s, :], out_offset=None, in_=recs[o],
                        in_offset=bass.IndirectOffsetOnAxis(ap=chunk_i[:, s:s + 1], axis=0)).then_inc(sem("edge_rows"), 16)

            step_edges(BY_DST)
            pool.wait_ge(sem("positions"), 1)
            scattered = recs[BY_SRC].rearrange("c e -> (c e)").unsqueeze(1)


            def scatter(i, first):
                for h in range(2):
                    half = slice(h * SLOTS, (h + 1) * SLOTS)
                    if not first:
                        pool.wait_ge(sem(f"scattered{h}"), i * (16 * SLOTS))
                    at_col = bass.ds(i * (2 * SLOTS) + h * SLOTS, SLOTS)
                    nc.gpsimd.tensor_copy(pos_slot[:, half], pos_i[:, at_col]).then_inc(sem("sort_slots"), 1)
                    nc.gpsimd.tensor_copy(rec_slot[:, half], rec_sb[BY_SRC][:, at_col]).then_inc(sem("sort_slots"), 1)
                    pool.wait_ge(sem("sort_slots"), i * 4 + (2 * h + 2))
                    pool.reg_add(sorts[h], sorts[h], 1)
                    for u in range(h * SLOTS, (h + 1) * SLOTS):
                        nc.gpsimd.indirect_dma_start(
                            out=scattered, out_offset=bass.IndirectOffsetOnAxis(ap=pos_slot[:, u:u + 1], axis=0),
                            in_=rec_slot[:, u:u + 1], in_offset=None).then_inc(sem(f"scattered{h}"), 16)

            scatter(0, True)
            with pool.Fori(1, SORT_TURNS) as i:
                scatter(i, False)
            step_edges(BY_SRC)
            for g, ph in enumerate(PASSES):
                pool.wait_ge(*((sem(ACC_READ[ph]), K) if g > 0 else (sem("edge_T_read"), 4)))
                if g == 0:
                    pool.wait_ge(sem("tile_out"), 16 * SB * 2)
                nc.gpsimd.memset(acc[:], 0.0).then_inc(sem("acc_zero"), 1)
                pool.wait_ge(sem(STORED[ph][0]), STORED[ph][1])
                if g == GAT:
                    def gather(n, r):
                        pool.wait_ge(sem("idx_ready"), n + (HALVES * g + 1))
                        pool.reg_add(gat_puts[r], gat_puts[r], 1)
                        for u in range(HALF):
                            nc.gpsimd.indirect_dma_start(
                                out=gat_ring[r][:, u, :], out_offset=None, in_=gat_table,
                                in_offset=bass.IndirectOffsetOnAxis(ap=idx_slot[:, r * HALF + u:r * HALF + u + 1], axis=0)
                            ).then_inc(slot_sem(r, u), 16)

                    gat_halves(pool, gather)
                    continue
                tab = rel_table if ph == "s1" else table
                with pool.Fori(0, TURNS) as i:
                    for h in range(2):
                        pool.wait_ge(sem("idx_ready"), i * 2 + (HALVES * g + h + 1))
                        pool.reg_add(halves[h], halves[h], 1)
                        for u in range(h * HALF, (h + 1) * HALF):
                            nc.gpsimd.indirect_dma_start(
                                out=ring[:, u, 0:D], out_offset=None, in_=tab,
                                in_offset=bass.IndirectOffsetOnAxis(ap=idx_slot[:, u:u + 1], axis=0)).then_inc(sem(f"gathered{u}"), 16)
            pool.wait_ge(sem("idx_ready"), sum((pool.snap(r) for r in halves[1:] + gat_puts), pool.snap(halves[0])))

            pool.wait_ge(sem("sort_slots"), pool.snap(sorts[0]) + pool.snap(sorts[1]))

        @block.tensor
        def _(pe):
            regs = [pe.alloc_register(f"pe_tile{u}") for u in range(HALF)]

            def transposed(k, unit, ready, src, kt=Q):
                if ready in PRODUCT_UNITS:
                    pe.wait_ge(sem("taken_dve"), count(PRODUCTS, k, ready, B))
                else:
                    pe.wait_ge(sem(ready), k + 1)
                for j in range(B):
                    for q in range(kt):
                        last = nc.tensor.transpose(psT[:, j * kt + q, :], src[:, j, q * P:(q + 1) * P], ident[:])
                last.then_inc(sem("acts_T"), 1)

            def product(k, unit, w, n, kt=Q, hT_of=None, after=None):
                pe.wait_ge(sem("acts_hT"), count(TRANSPOSED, k, hT_of or unit))
                if after:
                    pe.wait_ge(sem("taken_dve"), count(PRODUCTS, k, after, B))
                for j in range(B):
                    if j >= 4:
                        pe.wait_ge(sem("taken_dve"), count(PRODUCTS, k, unit, B, j - 4))
                    for q in range(kt):
                        last = nc.tensor.matmul(psum[:, 4 + j % 4, 0:n], hT[:, j * kt + q, :], w(q),
                                                start=(q == 0), stop=(q == kt - 1))
                    last.then_inc(sem("product"), 1)

            def cols(at, n):
                return lambda q: wbuf[:, q, at:at + n]

            def edge_pass(g, w):
                with pe.Fori(0, TURNS) as i:
                    for u in range(U):
                        pe.wait_ge(sem(f"gathered{u}"), i * 16 + 16 * (filled(g, u // HALF) + 1))
                        pe.wait_ge(sem("onehot"), i * U + (ONEHOTS[g] + u + 1))
                        pe.wait_ge(sem("summed"), i * U + (STEPS * g + u + 1))
                        nc.tensor.matmul(psum[:, u % GB, 0:w], onehot[:, u, :], ring[:, u, 0:w],
                                         start=True, stop=True).then_inc(sem("mm"), 1)

            HC = C // 2

            def chunk_bounds(o):
                pe.wait_ge(sem("bound_row"), o + 1)
                for b in range(2):
                    last = nc.tensor.matmul(psum[:, b, 0:HC], ones[0:1, :], bound_row[:, b * HC:(b + 1) * HC], start=True, stop=True)
                last.then_inc(sem("bound_mm"), 1)

            def step_tables(o):
                for a in range(2):
                    pe.wait_ge(sem("edge_f"), 2 * o + a + 1)
                    if a > 0:
                        pe.wait_ge(sem("edge_T_read"), 2 * o + 1)
                    for s in range(SB):
                        last = nc.tensor.transpose(psT[:, s, :], edge_f[:, a, s, :], ident[:])
                    last.then_inc(sem("edge_T"), 1)
                pe.wait_ge(sem("edge_T_read"), 2 * o + 2)

            pe.wait_ge(sem("consts"), 1)
            chunk_bounds(BY_DST)
            pe.wait_ge(sem("counts"), T)
            nc.tensor.matmul(psum[:, 2, 0:T], before, counts, start=True, stop=True)
            nc.tensor.matmul(psum[:, 3, 0:T], ones[:], counts, start=True, stop=True).then_inc(sem("count_mm"), 1)
            step_tables(BY_DST)
            pe.wait_ge(sem("in_params"), 16 * NLOADS["in"])
            with pe.Fori(0, K) as k:
                transposed(k, "in_u", "in_h", hbuf)
                product(k, "in_u", cols(W["in", "W_in"], D), D)
                transposed(k, "in_tab", "in_u", hbuf)
                product(k, "in_tab", cols(W["in", "agg"], 2 * D), 2 * D)
            chunk_bounds(BY_SRC)
            step_tables(BY_SRC)
            edge_pass(0, D + 1)
            for g, ph in ((1, "l0"), (2, "l1")):
                pe.wait_ge(sem(ph + "_params"), 16 * NLOADS[ph])
                with pe.Fori(0, K) as k:
                    transposed(k, ph + "_tab", ph + "_h", hbuf)
                    product(k, ph + "_tab", cols(W[ph, "agg"], 2 * D), 2 * D)
                edge_pass(g, D)
            pe.wait_ge(sem("l2_params"), 16 * NLOADS["l2"])
            pe.wait_ge(sem("w_att"), 2 * Q)
            with pe.Fori(0, K) as k:
                transposed(k, "l2_u", "l2_h", hbuf)
                product(k, "l2_u", cols(W["l2", "W_out"], D), D)
                transposed(k, "l2_tab", "l2_ln_h", hbuf)
                product(k, "l2_tab", cols(W["l2", "W_gat"], GW + HEADS), GW + HEADS)
            pe.wait_ge(sem("amax"), 1)
            nc.tensor.transpose(psum[0:HEADS, 0, 0:P], amax[:], ident[:]).then_inc(sem("amax_T"), 1)
            pe.wait_ge(sem("gdiag"), 1)
            nc.tensor.matmul(psum[:, 1, 0:HEADS], ones[0:HEADS, :], gdiag[:], start=True, stop=True).then_inc(sem("gmax_mm"), 1)
            g = GAT
            pe.wait_ge(sem("dst_tab"), 1)
            pe.wait_ge(sem("tile_row"), 32)

            def onehots_T(n, r):
                pe.wait_ge(sem("onehot"), n * HALF + (ONEHOTS[g] + HALF))
                for v in range(HALF):
                    last = nc.tensor.transpose(ps_oh[:, v, :], onehot[:, r * HALF + v, :], ident[:])
                last.then_inc(sem("oh_T"), 1)

            def logits(n):
                nc.tensor.load(regs, tile_row[0:1, BY_DST, bass.ds(n * HALF, HALF)])
                tiles = [nc.tensor.snap(r) for r in regs]
                pe.wait_ge(sem("oh_t"), n + 1)
                if isinstance(n, int) and n == 0:
                    pass
                else:
                    pe.wait_ge(sem("z_less"), n)
                for v in range(HALF):
                    last = nc.tensor.matmul(ps_log[:, v, :], onehot_t[:, v, :],
                                            dst_tab[:, bass.ds(tiles[v], 1), :].rearrange("p t h -> p (t h)"),
                                            start=True, stop=True)
                last.then_inc(sem("log_mm"), 1)

            def gat_half(n, r):
                ahead = not isinstance(n, int) or n + 2 < HALVES
                if ahead:
                    onehots_T(n + 2, (r + 2) % 4)
                for v in range(HALF):
                    pe.wait_ge(sem("msg"), n * HALF + (v + 1))
                    pe.wait_ge(sem("summed"), n * HALF + (STEPS * g + v + 1))
                    nc.tensor.matmul(psum[:, v, 0:GW], onehot[:, r * HALF + v, :], gat_ring[r][:, v, :],
                                     start=True, stop=True).then_inc(sem("mm"), 1)
                if ahead:
                    logits(n + 2)

            for n in range(2):
                onehots_T(n, n)
                logits(n)
            gat_halves(pe, gat_half)
            for name in ("bs", "bv"):
                def sums(k, w_last):
                    pe.wait_ge(sem(name + "_rows"), k + 1)
                    for j in range(B):
                        last = nc.tensor.matmul(psum[:, 0, 0:D], (w_last if j == B - 1 else ones)[:], hbuf[:, j, :],
                                                start=(j == 0), stop=(j == B - 1))
                    last.then_inc(sem(name + "_mm"), 1)
                with pe.Fori(0, K - 1) as k:
                    sums(k, ones)
                sums(K - 1, ones_last)
            for g, ph, w, h in ((4, "ga", "W0", "ga_ln_h"), (5, "s0", "W1", "s0_silu")):
                pe.wait_ge(sem(ph + "_params"), 16 * NLOADS[ph])
                with pe.Fori(0, K) as k:
                    transposed(k, ph + "_tab", h, hbuf)
                    product(k, ph + "_tab", cols(W[ph, w], D), D)
                edge_pass(g, D)
            pe.wait_ge(sem("s1_params"), 16 * NLOADS["s1"])
            with pe.Fori(0, K) as k:
                for r in range(2):
                    transposed(k, f"s1_u{r}", "s1_ln_h", hbuf)
                    product(k, f"s1_u{r}", cols(W["s1", f"R{r}"], D), D, after="s1_v0" if r else None)
                    transposed(k, f"s1_v{r}", f"s1_relu{r}", rb)
                    product(k, f"s1_v{r}", cols(W["s1", f"R{r}"], D), D)
            edge_pass(6, D)
            pe.wait_ge(sem("fi_params"), 16 * NLOADS["fi"])
            with pe.Fori(0, K) as k:
                transposed(k, "fi_i", "fi_agg", hbuf)
                product(k, "fi_i", cols(0, D), D)
                product(k, "fi_g", cols(2 * D, D), D, hT_of="fi_i", after="fi_i")
                product(k, "fi_o", cols(3 * D, D), D, hT_of="fi_i", after="fi_g")
                transposed(k, "fi_1", "fi_hn", hbuf)
                product(k, "fi_1", cols(W1_AT, H2), H2)
                transposed(k, "fi_2", "fi_relu1", hbuf, 1)
                product(k, "fi_2", lambda q: w2, H2, 1)
                transposed(k, "fi_3", "fi_relu2", hbuf, 1)
                product(k, "fi_3", lambda q: w3, D, 1)

        @block.scalar
        def _(act):
            def take_T(k, unit, kt=Q):
                act.wait_ge(sem("acts_T"), count(TRANSPOSED, k, unit))
                for f in range(0, B * kt, 4):
                    n = min(4, B * kt - f)
                    last = nc.scalar.copy(hT[:, f:f + n, :], psT[:, f:f + n, :])
                last.then_inc(sem("acts_hT"), 1)

            def take_table(k, ph, n=D):
                for j in range(B):
                    act.wait_ge(sem("product"), count(PRODUCTS, k, ph + "_tab", B, j))
                    nc.scalar.copy(tbuf[:, j, 0:n], psum[:, 4 + j % 4, 0:n]).then_inc(sem("taken_act"), 1)
                act.wait_ge(sem(ph + "_stored"), k * 16 + 16)

            def ln_relu(k, ph, done):
                act.wait_ge(sem("ln_ve"), count(NORMS, k, ph))
                nc.scalar.activation(sd[:], mv[:, :, 1], ACT.Sqrt).then_inc(sem("ln_sd"), 1)
                act.wait_ge(sem("ln_bias"), count(LN_BIASED, k, ph))
                for j in range(B):
                    last = nc.scalar.activation(hbuf[:, j, :], xb[:, j, :], ACT.Relu, bias=nmr[:, j:j + 1], scale=rstd[:, j:j + 1])
                last.then_inc(sem(done), 1)

            def on_batch(k, ready, to, of, func, done):
                if ready in PRODUCT_UNITS:
                    act.wait_ge(sem("taken_dve"), count(PRODUCTS, k, ready, B))
                else:
                    act.wait_ge(sem(ready), k + 1)
                nc.scalar.activation(to, of, func).then_inc(sem(done), 1)

            def put_indices(i, h, g, idx):
                act.wait_ge(sem("mm"), i * U + (STEPS * g + (h + 1) * HALF))
                nc.scalar.copy(idx_slot[:, h * HALF:(h + 1) * HALF],
                               idx[:, bass.ds(i * U + h * HALF, HALF)]).then_inc(sem("idx_ready"), 1)

            def edge_pass(g, idx):
                with act.Fori(0, TURNS) as i:
                    for h in range(2):
                        put_indices(i, h, g, idx)

            def step_tables(o):
                for a, to in enumerate((idx_by_src if o == BY_SRC else idx_rel, node_loc[:, o, :])):
                    act.wait_ge(sem("edge_T"), 2 * o + a + 1)
                    for f in range(0, SB, 4):
                        n = min(4, SB - f)
                        last = nc.scalar.copy(to[:, f * P:(f + n) * P], psT[:, f:f + n, :].rearrange("p f c -> p (f c)"))
                    last.then_inc(sem("edge_T_read"), 1)

            step_tables(BY_DST)
            with act.Fori(0, K) as k:
                ln_relu(k, "in", "in_h")
                take_T(k, "in_u")
                take_T(k, "in_tab")
                take_table(k, "in")
            step_tables(BY_SRC)
            edge_pass(0, idx_by_src)
            for g, ph in ((1, "l0"), (2, "l1")):
                with act.Fori(0, K) as k:
                    on_batch(k, ph + "_pre", hbuf[:], xb[:], ACT.Relu, ph + "_h")
                    take_T(k, ph + "_tab")
                    take_table(k, ph)
                edge_pass(g, idx_by_src)
            with act.Fori(0, K) as k:
                on_batch(k, "l2_pre", hbuf[:], xb[:], ACT.Relu, "l2_h")
                take_T(k, "l2_u")
                ln_relu(k, "l2", "l2_ln_h")
                take_T(k, "l2_tab")
                take_table(k, "l2", GW)
            g = GAT

            def gat_indices(n, r):
                if not isinstance(n, int) or n >= 4:
                    act.wait_ge(sem("mm"), n * HALF + (U + STEPS * g - 3 * HALF))
                nc.scalar.copy(idx_slot[:, r * HALF:(r + 1) * HALF],
                               idx_by_dst[:, bass.ds(n * HALF, HALF)]).then_inc(sem("idx_ready"), 1)

            def take_onehots(n):
                act.wait_ge(sem("oh_T"), n + 1)
                nc.scalar.copy(onehot_t[:, 0:4, :], ps_oh[:, 0:4, :])
                nc.scalar.copy(onehot_t[:, 4:HALF, :], ps_oh[:, 4:HALF, :]).then_inc(sem("oh_t"), 1)

            def weights(n, r):
                act.wait_ge(sem("z_clamped"), n + 1)
                nc.scalar.activation(gat_ring[r][:, :, D:GW], zlog2[:], ACT.Exp).then_inc(sem("edge_w"), 1)

            def gat_half(n, r):
                for ahead, f in ((3, lambda: gat_indices(n + 3, (r + 3) % 4)), (2, lambda: take_onehots(n + 2)),
                                 (1, lambda: weights(n + 1, (r + 1) % 4))):
                    if not isinstance(n, int) or n + ahead < HALVES:
                        f()

            for n in range(3):
                gat_indices(n, n)
            for n in range(2):
                take_onehots(n)
            weights(0, 0)
            gat_halves(act, gat_half)
            act.wait_ge(sem("zs_clamped"), 1)
            nc.scalar.activation(w_self[:], w_self[:], ACT.Exp).then_inc(sem("w_self"), 1)
            with act.Fori(0, K) as k:
                act.wait_ge(sem("bs_rows"), k + 1)
                nc.scalar.copy(acc[:, bass.ds(k * B, B), 0:D], hbuf[:]).then_inc(sem("ga_kept"), 1)
            with act.Fori(0, K) as k:
                on_batch(k, "bv_dev", hbuf[:], xb[:], ACT.Square, "bv_rows")
            act.wait_ge(sem("bn_ve"), 1)
            nc.scalar.activation(bn_b[:], bn_a[:], ACT.Sqrt).then_inc(sem("bn_sd"), 1)
            with act.Fori(0, K) as k:
                ln_relu(k, "ga", "ga_ln_h")
                take_T(k, "ga_tab")
                take_table(k, "ga")
            edge_pass(4, idx_by_src)

            def ln_silu(k, ph):
                act.wait_ge(sem("ln_ve"), count(NORMS, k, ph))
                nc.scalar.activation(sd[:], mv[:, :, 1], ACT.Sqrt).then_inc(sem("ln_sd"), 1)
                on_batch(k, ph + "_n", hbuf[:], xb[:], ACT.Silu, ph + "_silu")

            with act.Fori(0, K) as k:
                ln_silu(k, "s0")
                take_T(k, "s0_tab")
                take_table(k, "s0")
            edge_pass(5, idx_by_src)
            with act.Fori(0, K) as k:
                ln_silu(k, "s1")
                ln_relu(k, "s1b", "s1_ln_h")
                for r in range(2):
                    take_T(k, f"s1_u{r}")
                    on_batch(k, f"s1_u{r}", rb[:], rb[:], ACT.Relu, f"s1_relu{r}")
                    take_T(k, f"s1_v{r}")
                    on_batch(k, f"s1_v{r}", tbuf[:, :, 0:D], tbuf[:, :, 0:D], ACT.Relu, f"s1_m{r}")
            edge_pass(6, idx_rel)
            with act.Fori(0, K) as k:
                take_T(k, "fi_i")
                on_batch(k, "fi_i", xb[:], xb[:], ACT.Sigmoid, "fi_si")
                on_batch(k, "fi_g", rb[:], rb[:], ACT.Tanh, "fi_tg")
                on_batch(k, "fi_c", xb[:], xb[:], ACT.Tanh, "fi_tc")
                on_batch(k, "fi_o", rb[:], rb[:], ACT.Sigmoid, "fi_so")
                take_T(k, "fi_1")
                on_batch(k, "fi_1", hbuf[:, :, 0:H2], hbuf[:, :, 0:H2], ACT.Relu, "fi_relu1")
                take_T(k, "fi_2", 1)
                on_batch(k, "fi_2", hbuf[:, :, 0:H2], hbuf[:, :, 0:H2], ACT.Relu, "fi_relu2")
                take_T(k, "fi_3", 1)

        @block.vector
        def _(dve):
            V = nc.vector
            regs = [dve.alloc_register(f"dve_tile{u}") for u in range(U)]

            def then(ins, name, value=1):
                ins.then_inc(sem(name), 1)
                dve.wait_ge(sem(name), value)

            norms = {ph: dve.alloc_register("norms_" + ph) for names in NORMS.values() for ph in names}
            for r in norms.values():
                V.reg_mov(r, 0)
            sort_tiles = dve.alloc_register("sort_tiles")
            V.reg_mov(sort_tiles, 0)
            once_n = [0]

            def once(ins):
                once_n[0] += 1
                then(ins, "dve_once", once_n[0])

            def ln_stats(k, ph, src=xb):
                for j in range(B):
                    last = V.bn_stats(st[:, j, :], src[:, j, :])
                last.then_inc(sem("ln_st"), 1)
                dve.wait_ge(sem("ln_st"), count(NORMS, k, ph))
                V.reg_add(norms[ph], norms[ph], 1)
                for j in range(B):
                    last = V.bn_aggr(mv[:, j, :], st[:, j, :])
                then(last, "ln_mv", count(NORMS, k, ph))
                V.tensor_scalar_add(mv[:, :, 1], mv[:, :, 1], LN_EPS).then_inc(sem("ln_ve"), 1)
                dve.wait_ge(sem("ln_sd"), count(NORMS, k, ph))
                then(V.reciprocal(rstd[:], sd[:]), "ln_rs", count(NORMS, k, ph))

            def ln_bias(k, ph):
                V.scalar_tensor_tensor(out=nmr[:], in0=mv[:, :, 0], scalar=-1.0, in1=rstd[:], op0=ALU.mult,
                                       op1=ALU.mult).then_inc(sem("ln_bias"), 1)

            def take(k, unit, f):
                for j in range(B):
                    if unit.endswith("_tab"):
                        dve.wait_ge(sem("taken_act"), count(TABLES, k, unit, B, j))
                    else:
                        dve.wait_ge(sem("product"), count(PRODUCTS, k, unit, B, j))
                    f(j, psum[:, 4 + j % 4, :]).then_inc(sem("taken_dve"), 1)

            def copied(to, of):
                return V.tensor_scalar(to, of, 1.0, None, op0=ALU.mult)

            def own_at(k, j):
                return own[:, bass.ds(k * B + j, 1), :].rearrange("p t c -> p (t c)")

            def mean_and_own(k, ph):
                for j in range(B):
                    t = bass.ds(k * B + j, 1)
                    last = V.scalar_tensor_tensor(out=xb[:, j, :], in0=acc[:, t, 0:D].rearrange("p t c -> p (t c)"),
                                                  scalar=rdeg[:, t], in1=own_at(k, j), op0=ALU.mult, op1=ALU.add)
                last.then_inc(sem(ph + "_pre"), 1)

            def make_onehot(g, step, u):
                V.tensor_scalar(onehot[:, u, :], iota_row[:], node_loc[:, ORDER[g], bass.ds(step, 1)], None,
                                op0=ALU.is_equal).then_inc(sem("onehot"), 1)

            def add_sums(step, g, bank, tile, w):
                dve.wait_ge(sem("mm"), step + (U + STEPS * g + 1))
                dve.wait_ge(sem("summed"), step + (GB + STEPS * g))
                a = acc[:, bass.ds(tile, 1), 0:w].rearrange("p t c -> p (t c)")
                V.tensor_tensor(a, a, psum[:, bank, 0:w], ALU.add).then_inc(sem("summed"), 1)

            def norms_done(g):
                for ph in NORMS.get(PASSES[g], ()):
                    dve.wait_ge(sem("ln_mv"), V.snap(norms[ph]))
                    n = list(norms).index(ph)
                    V.memset(carrier[:, n:n + 1], 0.0)

            def edge_pass(g, w):
                norms_done(g)
                for u in range(HALF):
                    make_onehot(g, u, u)
                dve.wait_ge(sem("acc_zero"), g + 1)
                with dve.Fori(0, TURNS) as i:
                    V.load(regs, tile_row[0:1, ORDER[g], bass.ds(i * U, U)])
                    tiles = [V.snap(r) for r in regs]
                    for u in range(U):
                        make_onehot(g, i * U + (u + HALF), (u + HALF) % U)
                        add_sums(i * U + u, g, u % GB, tiles[u], w)
                dve.wait_ge(sem("summed"), GB + STEPS * (g + 1))

            V.memset(edges[:, 0:2, :], NP - 1)
            V.memset(edges[:, 2, :], 0)
            V.memset(zrows, 0.0).then_inc(sem("pads_set"), 1)
            V.memset(all_ones, 1.0)
            V.memset(position, 0.0)
            V.memset(ones[:], 1.0).then_inc(sem("mm"), U)
            V.memset(ring[:, :, D:D + 1], 1.0).then_inc(sem("summed"), GB)
            dve.wait_ge(sem("iota"), 4)
            V.tensor_scalar(ones_last[:], part[:].broadcast_to([P, P]), float(LAST), None, op0=ALU.is_lt)
            V.tensor_scalar(before, iota_row[:], part[:], None, op0=ALU.is_gt)
            V.tensor_scalar(ident[:], iota_row[:], part[:], None, op0=ALU.is_equal).then_inc(sem("consts"), 1)
            dve.wait_ge(sem("edges"), 16 * 9)
            src_sb, dst_sb, rel_sb = (edges[:, a, :] for a in range(3))

            def shifted(to, of, bits, op=ALU.logical_shift_left):
                once(V.tensor_scalar(to, of, bits, None, op0=op))

            shifted(rec_sb[BY_DST], dst_sb, NODE)
            once(V.scalar_tensor_tensor(out=rel_sb, in0=rel_sb, scalar=float(NP), in1=src_sb, op0=ALU.mult, op1=ALU.add))
            once(V.tensor_tensor(rec_sb[BY_DST], rec_sb[BY_DST], rel_sb, ALU.bitwise_or))
            shifted(rec_sb[BY_SRC], src_sb, NODE)
            once(V.tensor_tensor(rec_sb[BY_SRC], rec_sb[BY_SRC], dst_sb, ALU.bitwise_or))
            shifted(src_sb, src_sb, 7, ALU.logical_shift_right)
            V.tensor_copy(key_tile, src_sb).then_inc(sem("rec_by_dst"), 1)
            dve.wait_ge(sem("rec_by_dst"), 1)

            HC = C // 2

            def step_chunks(o):
                dve.wait_ge(sem("last_rec"), 16 * (o + 1))
                shifted(last_tile, last_rec, NODE + 7, ALU.logical_shift_right)
                V.tensor_tensor(bound_row, last_tile, chunk_row, ALU.add).then_inc(sem("bound_row"), 1)
                dve.wait_ge(sem("bound_mm"), o + 1)
                once(V.tensor_copy(bounds.rearrange("p (b c) -> p b c", b=2), psum[:, 0:2, 0:HC]))
                for s in range(SB):
                    once(V.tensor_scalar(junk, bounds, step_no[:, s:s + 1], 0.0, op0=ALU.is_le, op1=ALU.add,
                                         accum_out=chunk_f[:, s:s + 1]))
                once(V.tensor_scalar(chunk_c, chunk_f, float(C - 1), None, op0=ALU.min))
                V.tensor_copy(chunk_i, chunk_c).then_inc(sem("chunk_i"), 1)
                once(V.tensor_tensor(tile_f, step_no, chunk_c, ALU.subtract))
                V.tensor_copy(tile_i, tile_f).then_inc(sem("tile_i"), 1)
                once(V.tensor_scalar(tile_base, tile_f, float(P), None, op0=ALU.mult))

            def step_tables(o):
                dve.wait_ge(sem("edge_rows"), 16 * SB * (o + 1))
                shifted(edge_i, edge_rows, (1 << NODE) - 1, ALU.bitwise_and)
                once(V.tensor_copy(edge_f[:, 0, :, :], edge_i))
                shifted(edge_i, edge_rows, NODE, ALU.logical_shift_right)
                V.memset(junk[:, 0:1], 0.0).then_inc(sem("edge_f"), 1)
                for s in range(SB):
                    last = V.tensor_scalar(edge_f[:, 1, s, :], edge_i[:, s, :], tile_base[:, s:s + 1], None, op0=ALU.subtract)
                last.then_inc(sem("edge_f"), 1)
                dve.wait_ge(sem("edge_T_read"), 2 * o + 2)

            step_chunks(BY_DST)
            with dve.Fori(0, T) as t:
                then(V.tensor_scalar(is_tile, key_tile, iota_row[:, bass.ds(t, 1)], 0.0, op0=ALU.is_equal, op1=ALU.add,
                                     accum_out=counts[:, bass.ds(t, 1)]), "counts", t + 1)
            dve.wait_ge(sem("count_mm"), 1)
            once(V.tensor_copy(totals, psum[:, 3, 0:T]))
            once(V.tensor_tensor_scan(ends, ones[:, 0:T], totals, 0.0, op0=ALU.mult, op1=ALU.add))
            once(V.tensor_tensor(starts, ends, totals, ALU.subtract))
            once(V.tensor_tensor(starts, starts, psum[:, 2, 0:T], ALU.add))
            with dve.Fori(0, T) as t:
                then(V.tensor_scalar(is_tile, key_tile, iota_row[:, bass.ds(t, 1)], None, op0=ALU.is_equal), "is_tile", t + 1)
                V.tensor_tensor_scan(running, all_ones, is_tile, starts[:, bass.ds(t, 1)], op0=ALU.mult, op1=ALU.add).then_inc(sem("running"), 1)
                dve.wait_ge(sem("running"), t + 1)
                V.reg_add(sort_tiles, sort_tiles, 1)
                then(V.copy_predicated(position, is_tile, running), "position", t + 1)
            dve.wait_ge(sem("position"), V.snap(sort_tiles))
            V.tensor_scalar(pos_i, position, -1.0, None, op0=ALU.add).then_inc(sem("positions"), 1)
            step_tables(BY_DST)
            once(V.tensor_scalar(idx_by_dst[:], idx_rel[:], float(NP), float(-NP), op0=ALU.is_ge, op1=ALU.mult))
            once(V.tensor_tensor(idx_by_dst[:], idx_by_dst[:], idx_rel[:], ALU.add))

            def own_hid(ph):
                def f(k):
                    return lambda j, ps: V.tensor_tensor(own_at(k, j), ps[:, D:2 * D], row(ph, "b_hid"), ALU.add)
                return f

            dve.wait_ge(sem("in_params"), 16 * NLOADS["in"])
            with dve.Fori(0, K) as k:
                dve.wait_ge(sem("in_x"), k * 16 + 16)
                ln_stats(k, "in")
                ln_bias(k, "in")
                take(k, "in_u", lambda j, ps: V.tensor_tensor(hbuf[:, j, :], ps[:, 0:D], row("in", "b_in"), ALU.add))
                take(k, "in_tab", own_hid("in")(k))
            step_chunks(BY_SRC)
            step_tables(BY_SRC)
            dve.wait_ge(sem("tile_row"), 32)
            edge_pass(0, D + 1)
            once(V.tensor_scalar(rdeg[:], acc[:, :, D], 1.0, None, op0=ALU.max))
            once(V.reciprocal(rdeg[:], rdeg[:]))
            for g, ph in ((1, "l0"), (2, "l1")):
                dve.wait_ge(sem(ph + "_params"), 16 * NLOADS[ph])
                with dve.Fori(0, K) as k:
                    mean_and_own(k, ph)
                    take(k, ph + "_tab", own_hid(ph)(k))
                edge_pass(g, D)

            dve.wait_ge(sem("l2_params"), 16 * NLOADS["l2"])
            wg = W["l2", "W_gat"]
            for a, name in enumerate(("att_src", "att_dst")):
                for q in range(Q):
                    n = a * Q + q
                    once(V.tensor_tensor(xb[:, n, :], wbuf[:, q, wg:wg + D], row("l2", name), ALU.mult))
                    V.tensor_reduce(wbuf[:, q, wg + D + a * HEADS:wg + D + (a + 1) * HEADS], heads(xb[:, n, :]),
                                    axis=AX, op=ALU.add).then_inc(sem("w_att"), 1)
            dve.wait_ge(sem("w_att"), 2 * Q)

            def logits(k):
                def f(j, ps):
                    t = bass.ds(k * B + j, 1)
                    copied(a_own[:, t, :].rearrange("p t h -> p (t h)"), ps[:, D:GW])
                    return copied(dst_tab[:, t, 0:HEADS].rearrange("p t h -> p (t h)"), ps[:, GW:GW + HEADS])
                return f

            with dve.Fori(0, K) as k:
                mean_and_own(k, "l2")
                take(k, "l2_u", lambda j, ps: V.tensor_tensor(xb[:, j, :], ps[:, 0:D], row("l2", "b_out"), ALU.add))
                dve.wait_ge(sem("taken_dve"), count(PRODUCTS, k, "l2_u", B))
                dve.wait_ge(sem("l2_r"), k * 16 + 16)
                then(V.tensor_tensor(xb[:], xb[:], rb[:], ALU.add), "l2_x1", k + 1)
                ln_stats(k, "l2")
                ln_bias(k, "l2")
                dve.wait_ge(sem("l2_ln_h"), k + 1)
                V.tensor_tensor(rb[:], xb[:], hbuf[:], ALU.add).then_inc(sem("l2_res"), 1)
                take(k, "l2_tab", logits(k))
                dve.wait_ge(sem("l2_res"), k + 1)
            dve.wait_ge(sem("taken_dve"), count(PRODUCTS, K - 1, "l2_tab", B))
            V.tensor_reduce(amax[:], a_own[:, :, :].rearrange("p t h -> p h t"), axis=AX, op=ALU.max).then_inc(sem("amax"), 1)
            dve.wait_ge(sem("amax_T"), 1)
            once(V.tensor_reduce(gmax[:], psum[0:HEADS, 0, 0:P], axis=AX, op=ALU.max))
            V.tensor_scalar(gdiag[:], ident[0:HEADS, 0:HEADS], gmax[:], None, op0=ALU.mult).then_inc(sem("gdiag"), 1)
            dve.wait_ge(sem("gmax_mm"), 1)
            once(V.tensor_copy(gmax_b[:], psum[:, 1, 0:HEADS]))
            dmax = dst_tab[:, :, HEADS:2 * HEADS]
            dlog = dst_tab[:, :, 0:HEADS]
            once(V.tensor_tensor(dmax, dlog, gmax_b[:].unsqueeze(1).broadcast_to([P, T, HEADS]), ALU.add))
            V.scalar_tensor_tensor(out=dmax, in0=dmax, scalar=SLOPE, in1=dmax, op0=ALU.mult, op1=ALU.max).then_inc(sem("dst_tab"), 1)

            g = GAT
            norms_done(g)

            def gat_onehots(n, r):
                for v in range(HALF):
                    make_onehot(g, n * HALF + v, r * HALF + v)

            def gat_logits(n, r):
                if not isinstance(n, int) or n > 0:
                    dve.wait_ge(sem("edge_w"), n)
                if r < 2:
                    for v in range(HALF):
                        dve.wait_ge(slot_sem(r, v), n * 4 + (16 * (filled(g, r) + 1) - 4 * r))
                else:
                    dve.wait_ge(slot_sem(r, 0), n * (4 * HALF) + HALF * (16 - 4 * r))
                dve.wait_ge(sem("log_mm"), n + 1)
                then(V.tensor_tensor(zlog[:], ps_log[:, :, 0:HEADS], gat_ring[r][:, :, D:GW], ALU.add), "z", n + 1)
                then(V.scalar_tensor_tensor(out=zlog2[:], in0=zlog[:], scalar=SLOPE, in1=zlog[:], op0=ALU.mult, op1=ALU.max), "z_leaky", n + 1)
                then(V.tensor_tensor(zlog[:], zlog2[:], ps_log[:, :, HEADS:2 * HEADS], ALU.subtract), "z_less", n + 1)
                V.tensor_scalar(zlog2[:], zlog[:], 0.0, None, op0=ALU.min).then_inc(sem("z_clamped"), 1)

            def gat_half(n, r):
                first = isinstance(n, int) and n == 0
                if not first:
                    V.load(regs[0:HALF], tile_row[0:1, BY_DST, bass.ds((n - 1) * HALF, HALF)])
                    tiles = [V.snap(r) for r in regs[0:HALF]]
                dve.wait_ge(sem("edge_w"), n + 1)
                for v in range(HALF):
                    if not first:
                        add_sums((n - 1) * HALF + v, g, v, tiles[v], GW)
                    V.tensor_tensor(heads(gat_ring[r][:, v, 0:D]), heads(gat_ring[r][:, v, 0:D]),
                                    gat_ring[r][:, v, D:GW].unsqueeze(2).broadcast_to([P, HEADS, DH]), ALU.mult).then_inc(sem("msg"), 1)
                if not isinstance(n, int) or n + 1 < HALVES:
                    gat_logits(n + 1, (r + 1) % 4)
                if not isinstance(n, int) or n + 3 < HALVES:
                    gat_onehots(n + 3, (r + 3) % 4)

            for n in range(3):
                gat_onehots(n, n)
            dve.wait_ge(sem("acc_zero"), g + 1)
            gat_logits(0, 0)
            gat_halves(dve, gat_half)
            V.load(regs[0:HALF], tile_row[0:1, BY_DST, bass.ds((HALVES - 1) * HALF, HALF)])
            for v, r in enumerate(regs[0:HALF]):
                add_sums((HALVES - 1) * HALF + v, g, v, V.snap(r), GW)
            dve.wait_ge(sem("summed"), GB + STEPS * (g + 1))

            once(V.tensor_tensor(w_self[:], a_own[:], dlog, ALU.add))
            once(V.scalar_tensor_tensor(out=w_self[:], in0=w_self[:], scalar=SLOPE, in1=w_self[:], op0=ALU.mult, op1=ALU.max))
            once(V.tensor_tensor(w_self[:], w_self[:], dmax, ALU.subtract))
            V.tensor_scalar(w_self[:], w_self[:], 0.0, None, op0=ALU.min).then_inc(sem("zs_clamped"), 1)
            V.memset(bn_a[:], 0.0)
            once(V.memset(bn_sum[:], 0.0))
            dve.wait_ge(sem("ga_params"), 16 * NLOADS["ga"])
            dve.wait_ge(sem("w_self"), 1)

            def by_head(ap):
                return ap.rearrange("p j (h d) -> p j h d", h=HEADS)

            def over_dim(ap):
                return ap.unsqueeze(3).broadcast_to([P, B, HEADS, DH])

            with dve.Fori(0, K) as k:
                t = bass.ds(k * B, B)
                dve.wait_ge(sem("ga_xh"), k * 16 + 16)
                then(V.tensor_tensor(by_head(xb[:]), by_head(tbuf[:, :, 0:D]), over_dim(w_self[:, t, :]), ALU.mult), "ga_self", k + 1)
                V.tensor_tensor(xb[:], xb[:], acc[:, t, 0:D], ALU.add)
                then(V.tensor_tensor(den[:], acc[:, t, D:GW], w_self[:, t, :], ALU.add), "ga_den", k + 1)
                then(V.reciprocal(den[:], den[:]), "ga_rden", k + 1)
                then(V.tensor_tensor(by_head(xb[:]), by_head(xb[:]), over_dim(den[:]), ALU.mult), "ga_quot", k + 1)
                V.tensor_tensor(hbuf[:], xb[:], over_batch(row("ga", "bias")), ALU.add).then_inc(sem("bs_rows"), 1)
                dve.wait_ge(sem("bs_mm"), k + 1)
                then(V.tensor_tensor(bn_sum[:], bn_sum[:], psum[:, 0, 0:D], ALU.add), "bs_added", k + 1)
                dve.wait_ge(sem("ga_kept"), k + 1)
            once(V.tensor_scalar(bn_mean[:], bn_sum[:], 1.0 / N, None, op0=ALU.mult))
            with dve.Fori(0, K) as k:
                t = bass.ds(k * B, B)
                V.tensor_tensor(xb[:], acc[:, t, 0:D], over_batch(bn_mean[:]), ALU.subtract).then_inc(sem("bv_dev"), 1)
                dve.wait_ge(sem("bv_mm"), k + 1)
                then(V.tensor_tensor(bn_a[:], bn_a[:], psum[:, 0, 0:D], ALU.add), "bv_added", k + 1)
            V.tensor_scalar(bn_a[:], bn_a[:], 1.0 / N, LN_EPS, op0=ALU.mult, op1=ALU.add).then_inc(sem("bn_ve"), 1)
            dve.wait_ge(sem("bn_sd"), 1)
            once(V.reciprocal(bn_a[:], bn_b[:]))
            once(V.tensor_tensor(bn_a[:], bn_a[:], row("ga", "gamma"), ALU.mult))
            once(V.tensor_tensor(bn_b[:], bn_mean[:], bn_a[:], ALU.mult))
            once(V.tensor_tensor(bn_b[:], row("ga", "beta"), bn_b[:], ALU.subtract))
            with dve.Fori(0, K) as k:
                t = bass.ds(k * B, B)
                then(V.tensor_tensor(xb[:], acc[:, t, 0:D], over_batch(bn_a[:]), ALU.mult), "ga_scaled", k + 1)
                then(V.tensor_tensor(xb[:], xb[:], over_batch(bn_b[:]), ALU.add), "ga_shifted", k + 1)
                dve.wait_ge(sem("ga_r"), k * 16 + 16)
                then(V.tensor_tensor(xb[:], xb[:], rb[:], ALU.add), "ga_x2", k + 1)
                ln_stats(k, "ga")
                ln_bias(k, "ga")
                take(k, "ga_tab", lambda j, ps: copied(own_at(k, j), ps[:, 0:D]))
                dve.wait_ge(sem("ga_rstored"), k * 16 + 16)
            edge_pass(4, D)

            def ln_affine(k, ph):
                mean_and_own(k, ph)
                dve.wait_ge(sem(ph + "_pre"), k + 1)
                then(V.tensor_tensor(xb[:], xb[:], over_batch(row(ph, "b")), ALU.add), ph + "_z", k + 1)
                ln_stats(k, ph)
                for j in range(B):
                    last = V.tensor_scalar(xb[:, j, :], xb[:, j, :], mv[:, j, 0:1], rstd[:, j:j + 1], op0=ALU.subtract, op1=ALU.mult)
                then(last, ph + "_hat", k + 1)
                then(V.tensor_tensor(xb[:], xb[:], over_batch(row(ph, "g")), ALU.mult), ph + "_hg", k + 1)
                V.tensor_tensor(xb[:], xb[:], over_batch(row(ph, "beta")), ALU.add).then_inc(sem(ph + "_n"), 1)

            dve.wait_ge(sem("s0_params"), 16 * NLOADS["s0"])
            with dve.Fori(0, K) as k:
                ln_affine(k, "s0")
                take(k, "s0_tab", lambda j, ps: copied(own_at(k, j), ps[:, 0:D]))
            edge_pass(5, D)
            dve.wait_ge(sem("s1_params"), 16 * NLOADS["s1"])
            with dve.Fori(0, K) as k:
                ln_affine(k, "s1")
                dve.wait_ge(sem("s1_silu"), k + 1)
                dve.wait_ge(sem("s1_r"), k * 16 + 16)
                then(V.tensor_tensor(xb[:], hbuf[:], rb[:], ALU.add), "s1_x3", k + 1)
                ln_stats(k, "s1b")
                ln_bias(k, "s1b")
                for r in range(2):
                    take(k, f"s1_u{r}", lambda j, ps: V.tensor_tensor(rb[:, j, :], ps[:, 0:D], row("s1", f"b{r}"), ALU.add))
                    if r:
                        dve.wait_ge(sem("s1_stored"), k * 32 + 16)
                    take(k, f"s1_v{r}", lambda j, ps: V.tensor_tensor(tbuf[:, j, 0:D], ps[:, 0:D], row("s1", f"b{r}"), ALU.add))
                dve.wait_ge(sem("s1_stored"), k * 32 + 32)
                dve.wait_ge(sem("s1_rstored"), k * 16 + 16)
            edge_pass(6, D)

            dve.wait_ge(sem("fi_params"), 16 * NLOADS["fi"])
            once(V.tensor_tensor(pbuf[:, 0:4 * D].rearrange("p (a d) -> p a d", a=4),
                                 pbuf[:, 0:4 * D].rearrange("p (a d) -> p a d", a=4), bhh, ALU.add))

            def biased(to, at, n):
                return lambda j, ps: V.tensor_tensor(to[:, j, 0:n], ps[:, 0:n], pbuf[:, at:at + n], ALU.add)

            with dve.Fori(0, K) as k:
                copied(hbuf[:], acc[:, bass.ds(k * B, B), 0:D]).then_inc(sem("fi_agg"), 1)
                take(k, "fi_i", biased(xb, 0, D))
                take(k, "fi_g", biased(rb, 2 * D, D))
                dve.wait_ge(sem("fi_si"), k + 1)
                dve.wait_ge(sem("fi_tg"), k + 1)
                then(V.tensor_tensor(xb[:], xb[:], rb[:], ALU.mult), "fi_c", k + 1)
                take(k, "fi_o", biased(rb, 3 * D, D))
                dve.wait_ge(sem("fi_tc"), k + 1)
                dve.wait_ge(sem("fi_so"), k + 1)
                V.tensor_tensor(hbuf[:], rb[:], xb[:], ALU.mult).then_inc(sem("fi_hn"), 1)
                take(k, "fi_1", biased(hbuf, R["fi", "b1"], H2))
                take(k, "fi_2", biased(hbuf, R["fi", "b2"], H2))
                take(k, "fi_3", biased(xb, R["fi", "b3"], D))
                dve.wait_ge(sem("taken_dve"), count(PRODUCTS, k, "fi_3", B))
                dve.wait_ge(sem("fi_r"), k * 16 + 16)
                then(V.tensor_tensor(tbuf[:, :, 0:D], tbuf[:, :, 0:D], xb[:], ALU.add), "fi_y", k + 1)


_TRANSPOSED = ("L2_gnn_W0", "L2_gnn_W1", "L3_gnn_W_rel", "L3_gnn_W_ih", "L3_gnn_W1", "L3_gnn_W2", "L3_gnn_W3")


def kernel(**inputs):
    import numpy as _np
    import concourse.bacc as _bacc
    from concourse import mybir as _mybir
    from concourse.bass_utils import run_bass_kernel_spmd as _run

    nc = _bacc.Bacc("TRN2", target_bir_lowering=False, num_devices=1)
    arrays, io = {}, {}
    for name, value in inputs.items():
        a = _np.asarray(value)
        if name in _TRANSPOSED:
            a = a.swapaxes(-1, -2)
        a = _np.ascontiguousarray(a)
        arrays["in_" + name] = a
        io[name] = nc.dram_tensor("in_" + name, a.shape, _mybir.dt.from_np(a.dtype), kind="ExternalInput").ap()
    out = nc.dram_tensor("out_x", inputs["x"].shape, _mybir.dt.float32, kind="ExternalOutput").ap()
    build(nc, io, out)
    return _run(nc, [arrays], core_ids=[0]).results[0]["out_x"]
```

```python
from contextlib import ExitStack

import concourse.bass as bass
from concourse import mybir

F32 = mybir.dt.float32
I32 = mybir.dt.int32
I16 = mybir.dt.int16
BF16 = mybir.dt.bfloat16
ALU = mybir.AluOpType
ACT = mybir.ActivationFunctionType
AX = mybir.AxisListType.X

P = 128
LN_EPS = 1e-5
SLOPE = 0.2


def build(nc, io, out):
    N, D = io["x"].shape
    E = io["src"].shape[0]
    HEADS, DH = io["L1_gnn_att_src"].shape
    T = -(-N // P)
    NP = T * P
    C = -(-E // P)
    EP = C * P
    STEPS = C + T - 1
    U = 10
    HALF = U // 2
    TURNS = STEPS // U
    assert TURNS * U == STEPS
    SB = -(-(STEPS + HALF) // P)
    B = 7
    K = T // B
    assert K * B == T
    GW = D + HEADS
    NODE = 14
    assert 2 * NP <= 1 << NODE
    LAST = N - (T - 1) * P
    H2 = D // 2
    Q = D // P

    ctx = ExitStack()
    with ctx:
        def sb(name, shape, dt=F32):
            return ctx.enter_context(nc.sbuf_tensor(name, shape, dt))

        sems = {}

        def sem(name):
            if name not in sems:
                sems[name] = ctx.enter_context(nc.semaphore(name))
            return sems[name]

        def dram(name, shape, dt=F32):
            return nc.dram_tensor(name, shape, dt).ap()

        BY_DST, BY_SRC = 0, 1
        recs = [dram("recs_by_dst", (C, P), I32), dram("recs_by_src", (C, P), I32)]
        tile_row_dram = dram("tile_row_dram", (2, SB, P), I16)
        table = dram("table", (NP, D))
        gat_table = dram("gat_table", (NP, GW))
        rel_table = dram("rel_table", (2 * NP, D))
        res = dram("res", (NP, D))

        def tiled(ap):
            return ap.rearrange("(t p) c -> p t c", p=P)

        acc = sb("acc", [P, T, GW])
        own = sb("own", [P, T, D])
        idx_by_src = sb("idx_by_src", [P, SB * P], I16)
        idx_rel = sb("idx_rel", [P, SB * P], I16)
        idx_by_dst = sb("idx_by_dst", [P, SB * P], I16)
        node_loc = sb("node_loc", [P, 2, SB * P], BF16)
        tile_row = sb("tile_row", [1, 2, SB * P], I16)
        ring = sb("ring", [P, U, GW])
        idx_slot = sb("idx_slot", [P, 2 * U], I32)
        onehot = sb("onehot", [P, 2 * U, P])
        onehot_t = sb("onehot_t", [P, HALF, P])
        hbuf = sb("hbuf", [P, B, D])
        hT = sb("hT", [P, B * Q, P])
        tbuf = sb("tbuf", [P, B, GW])
        xb = sb("xb", [P, B, D])
        rb = sb("rb", [P, B, D])
        wbuf = sb("wbuf", [P, Q, 1152])
        gat_ring = [ring[:, 0:HALF, :], ring[:, HALF:U, :], tbuf[:, 0:HALF, :],
                    hbuf[:, :, :].rearrange("p j d -> p (j d)")[:, 0:HALF * GW].rearrange("p (u c) -> p u c", c=GW)]
        pbuf = sb("pbuf", [P, 1536])
        iota_row = sb("iota_row", [P, P])
        ident = sb("ident", [P, P])
        ones = sb("ones", [P, P])
        ones_last = sb("ones_last", [P, P])
        part = sb("part", [P, 1])
        rdeg = sb("rdeg", [P, T])
        st = sb("st", [P, B, 6])
        mv = sb("mv", [P, B, 2])
        sd = sb("sd", [P, B])
        rstd = sb("rstd", [P, B])
        nmr = sb("nmr", [P, B])
        a_own = sb("a_own", [P, T, HEADS])
        dst_tab = sb("dst_tab", [P, T, 2 * HEADS])
        w_self = sb("w_self", [P, T, HEADS])
        zlog = sb("zlog", [P, HALF, HEADS])
        zlog2 = sb("zlog2", [P, HALF, HEADS])
        amax = sb("amax", [P, HEADS])
        amax7 = sb("amax7", [P, HEADS])
        gdiag = sb("gdiag", [HEADS, HEADS])
        gmax = sb("gmax", [HEADS, 1])
        gmax_b = sb("gmax_b", [P, HEADS])
        den = sb("den", [P, B, HEADS])
        bn_sum = sb("bn_sum", [P, D])
        bn_a = sb("bn_a", [P, D])
        bn_b = sb("bn_b", [P, D])
        bn_mean = sb("bn_mean", [P, D])
        carrier = sb("carrier", [P, 8])
        acc_flat = acc[:, :, :].rearrange("p t c -> p (t c)")
        at = [0]

        def place(n, dt=F32):
            words = n if dt in (F32, I32) else -(-n // 2)
            ap = acc_flat[:, at[0]:at[0] + words]
            at[0] += words
            assert at[0] <= T * GW
            return ap if dt == F32 else ap.bitcast(dt)[:, 0:n]

        edges = place(3 * C, I32).rearrange("p (a c) -> p a c", a=3)
        rec_sb = [place(C, I32), place(C, I32)]
        key_tile = place(C, BF16)
        is_tile = place(C, I16)
        running = place(C)
        all_ones = place(C)
        position = place(C)
        pos_i = place(C, I32)
        counts, totals, ends, starts = (place(T) for _ in range(4))
        SLOTS = 17
        SORT_TURNS = C // (2 * SLOTS)
        assert SORT_TURNS * 2 * SLOTS == C
        pos_slot = place(2 * SLOTS, I32)
        rec_slot = place(2 * SLOTS, I32)
        bounds = place(C)
        junk = place(C)
        edge_rows = place(SB * P, I32).rearrange("p (s e) -> p s e", s=SB)
        edge_i = onehot[:, 0:SB, :].bitcast(I32)
        edge_f = rb[:, 0:SB, :].rearrange("p j (a e) -> p a j e", a=2)
        last_rec, last_tile = (edges[0:1, a, :] for a in range(2))
        bound_row = edges[0:1, 2, :].bitcast(F32)
        chunk_row = place(C)[0:1, :]
        step_no, chunk_f, chunk_c, tile_f, tile_base = (place(SB) for _ in range(5))
        chunk_i = place(SB, I32)
        tile_i = place(SB, I16)
        zrows = xb[:, 0, :]
        before = hbuf[:, 0, 0:P]

        psum = ctx.enter_context(nc.psum_tensor("psum", [P, 8, 512], F32))
        psT = psum[:, 0:4, :].rearrange("p b (f c) -> p (b f) c", c=P)
        BANKS = 4
        GB = HALF
        ps_oh = psum[:, 5:7, :].rearrange("p b (f c) -> p (b f) c", c=P)
        ps_log = psum[:, 7, 0:HALF * 2 * HEADS].rearrange("p (u h) -> p u h", u=HALF)

        LOADS = {
            "in": ([("W_in", io["L0_gnn_W_in"]), ("agg", io["L0_gnn_W_agg"][0]), ("self", io["L0_gnn_W_self"][0])],
                   [("b_in", io["L0_gnn_b_in"]), ("b_hid", io["L0_gnn_b_hid"][0])]),
            "l0": ([("agg", io["L0_gnn_W_agg"][1]), ("self", io["L0_gnn_W_self"][1])], [("b_hid", io["L0_gnn_b_hid"][1])]),
            "l1": ([("agg", io["L0_gnn_W_agg"][2]), ("self", io["L0_gnn_W_self"][2])], [("b_hid", io["L0_gnn_b_hid"][2])]),
            "l2": ([("W_out", io["L0_gnn_W_out"]), ("W_gat", io["L1_gnn_W"])],
                   [("b_out", io["L0_gnn_b_out"]), ("att_src", io["L1_gnn_att_src"].rearrange("h d -> (h d)")),
                    ("att_dst", io["L1_gnn_att_dst"].rearrange("h d -> (h d)"))]),
            "ga": ([("W0", io["L2_gnn_W0"])],
                   [("bias", io["L1_gnn_bias"]), ("gamma", io["L1_gnn_gamma"]), ("beta", io["L1_gnn_beta"])]),
            "s0": ([("W1", io["L2_gnn_W1"])],
                   [("b", io["L2_gnn_b0"]), ("g", io["L2_gnn_g0"]), ("beta", io["L2_gnn_beta0"])]),
            "s1": ([("R0", io["L3_gnn_W_rel"][0]), ("R1", io["L3_gnn_W_rel"][1])],
                   [("b", io["L2_gnn_b1"]), ("g", io["L2_gnn_g1"]), ("beta", io["L2_gnn_beta1"]),
                    ("b0", io["L3_gnn_b_rel"][0]), ("b1", io["L3_gnn_b_rel"][1])]),
            "fi": ([("ih", io["L3_gnn_W_ih"]), ("W3", io["L3_gnn_W3"])],
                   [("bi", io["L3_gnn_b_ih"]), ("b1", io["L3_gnn_b1"]), ("b2", io["L3_gnn_b2"]), ("b3", io["L3_gnn_b3"])]),
        }
        W, R, NLOADS = {}, {}, {}
        for ph, (ws, rs) in LOADS.items():
            at = 0
            for name, ap in ws:
                if name == "W3":
                    continue
                W[ph, name] = at
                at += ap.shape[1]
            at = 0
            for name, ap in rs:
                R[ph, name] = at
                at += ap.shape[0]
            NLOADS[ph] = len(ws) + len(rs)
        W1_AT = 4 * D
        NLOADS["fi"] += 3
        w2 = onehot_t[:, 0, :]
        w3 = onehot[:, 0:2, :].rearrange("p a c -> p (a c)")
        bhh = ring[:, 0:4, 0:D]
        hbuf2 = ring[:, 0:B, 0:D]
        tbuf2 = onehot[:, :, :].rearrange("p u e -> p (u e)")[:, 0:B * D].rearrange("p (j d) -> p j d", d=D)

        def row(ph, name, n=D):
            return pbuf[:, R[ph, name]:R[ph, name] + n]

        def over_batch(ap):
            return ap.unsqueeze(1).broadcast_to([P, B, ap.shape[1]])

        def heads(ap):
            return ap.rearrange("p (h d) -> p h d", h=HEADS)

        block = ctx.enter_context(nc.Block())
        PASSES = ["in", "l0", "l1", "l2", "ga", "s0", "s1"]
        STORES = [K] * (len(PASSES) - 1) + [2 * K]
        STORED = {ph: 1 + sum(STORES[:g]) for g, ph in enumerate(PASSES)}
        ALL_STORED = {ph: STORED[ph] + n for ph, n in zip(PASSES, STORES)}
        ACC_READ = {ph: (ph + "_pre", T) for ph in PASSES} | {"ga": ("ga_x2", K)}
        TRANSPOSED = {"in": ["in_u", "in_tab"], "l0": ["l0_tab"], "l1": ["l1_tab"], "l2": ["l2_u", "l2_tab"],
                      "ga": ["ga_tab"], "s0": ["s0_tab"], "s1": ["s1_u0", "s1_v0", "s1_v1"],
                      "fi": ["fi_i", "fi_1", "fi_2", "fi_3"]}
        PRODUCTS = TRANSPOSED | {"s1": ["s1_u0", "s1_u1", "s1_v0", "s1_v1"], "fi": ["fi_i", "fi_g", "fi_o", "fi_1", "fi_2", "fi_3"]}
        TABLES = {ph: [ph + "_tab"] for ph in PASSES if ph != "s1"}
        NORMS = {"in": ["in"], "l2": ["l2"], "ga": ["ga"], "s0": ["s0"], "s1": ["s1", "s1b"]}
        LN_BIASED = {"in": ["in"], "l2": ["l2"], "ga": ["ga"], "s1": ["s1b"]}

        PRODUCT_UNITS = [u for names in PRODUCTS.values() for u in names]

        FREE = BANKS - 1

        def count(units, k, unit, items=1, j=None):
            before = 0
            for names in units.values():
                if unit in names:
                    at = before * K + names.index(unit)
                    return k * (len(names) * items) + (at * items + (items if j is None else j + 1))
                before += len(names)

        ORDER = [BY_DST if ph in ("l2", "s1") else BY_SRC for ph in PASSES]
        GAT = PASSES.index("l2")
        HALVES, FIRST, TAIL = STEPS // HALF, 2, 4
        GAT_TURNS = (HALVES - FIRST - TAIL) // 4
        assert FIRST + 4 * GAT_TURNS + TAIL == HALVES
        ONEHOTS = [g * (STEPS + HALF) - (HALF if g > GAT else 0) for g in range(len(PASSES))]

        def filled(g, h):
            n = -(-(HALVES - h) // 4)
            return (TURNS * (g - (g > GAT)) if h < 2 else 0) + (n if g > GAT else 0)

        def slot_sem(r, u):
            return sem(f"gathered{r * HALF + u}") if r < 2 else sem(f"gathered_half{r}")

        def gat_halves(eng, half, tiles=None):
            def run(n0, count, at):
                got = tiles(n0, count) if tiles else None
                for m in range(count):
                    n = n0 + m
                    half(n, (at + m) % 4, *([got[m * HALF:(m + 1) * HALF]] if tiles else []))

            run(0, FIRST, 0)
            with eng.Fori(0, GAT_TURNS) as i:
                run(i * 4 + FIRST, 4, FIRST)
            run(HALVES - TAIL, TAIL, HALVES - TAIL)


        @block.sync
        def _(sp):
            def load_params(ph):
                ws, rs = LOADS[ph]
                done = sem(ph + "_params")
                for name, ap in ws:
                    n = ap.shape[1]
                    to, of = (w3, ap) if name == "W3" else (wbuf[:, :, W[ph, name]:W[ph, name] + n], ap.rearrange("(q p) n -> p q n", p=P))
                    if name != "W3":
                        sp.dma_start(to, of).then_inc(done, 16)
                for name, ap in rs:
                    n = ap.shape[0]
                    sp.dma_start(pbuf[:, R[ph, name]:R[ph, name] + n],
                                 ap.unsqueeze(0).broadcast_to([P, n])).then_inc(done, 16)

            def rows(ap, k, first=0):
                return tiled(ap)[:, bass.ds(k * B + first, B), :]

            sp.dma_start(res[0:N, :], io["x"]).then_inc(sem("x_copied"), 16)
            sp.wait_ge(sem("pads_set"), 1)
            for n, a in enumerate((io["src"], io["dst"], io["edge_type_2"])):
                whole = E // C
                most = whole // 16 * 16
                for p, q in ((0, most), (most, whole)):
                    sp.dma_start(edges[p:q, n, :], a[p * C:q * C].rearrange("(p c) -> p c", c=C)).then_inc(sem("edges"), 16)
                sp.dma_start(edges[whole:whole + 1, n, 0:E - whole * C], a[whole * C:E].unsqueeze(0)).then_inc(sem("edges"), 16)
            sp.dma_start(res[N:NP, :], zrows[0:NP - N, :]).then_inc(sem("stored"), 16)
            load_params("in")
            sp.wait_ge(sem("rec_by_dst"), 1)
            sp.dma_start(recs[BY_DST].rearrange("c e -> (c e)").rearrange("(p c) -> p c", c=C), rec_sb[BY_DST]).then_inc(sem("rec_stored"), 16)
            sp.wait_ge(sem("rec_stored"), 16)

            def chunk_ends(o):
                sp.dma_start(last_rec, recs[o][:, P - 1:P].rearrange("c o -> o c"), allow_slow_non_contiguous=True).then_inc(sem("last_rec"), 16)

            def step_tiles(o):
                sp.wait_ge(sem("tile_i"), o + 1)
                for s in range(SB):
                    sp.dma_start(tile_row_dram[o, s:s + 1, :].rearrange("o p -> p o"), tile_i[:, s:s + 1]).then_inc(sem("tile_out"), 16)
                sp.wait_ge(sem("tile_out"), 16 * SB * (o + 1))
                sp.dma_start(tile_row[0:1, o, :], tile_row_dram[o].rearrange("s p -> (s p)").unsqueeze(0)).then_inc(sem("tile_row"), 16)

            chunk_ends(BY_DST)
            sp.wait_ge(sem("x_copied"), 16)
            sp.wait_ge(sem("stored"), 16)
            sp.dma_start(xb[:], rows(res, 0)).then_inc(sem("in_x"), 16)
            step_tiles(BY_DST)

            def first(k, more):
                if more:
                    sp.wait_ge(sem("in_h"), k * B + B)
                    sp.dma_start(xb[:], rows(res, k + 1)).then_inc(sem("in_x"), 16)
                sp.wait_ge(sem("taken_act"), count(TABLES, k, "in_tab", B))
                sp.dma_start(rows(table, k), tbuf[:, :, 0:D]).then_inc(sem("stored"), 16)

            def table_out(ph):
                def step(k, more):
                    sp.wait_ge(sem("taken_act"), count(TABLES, k, ph + "_tab", B))
                    sp.dma_start(rows(table, k), tbuf[:, :, 0:D]).then_inc(sem("stored"), 16)
                return step

            def batches(step):
                with sp.Fori(0, K - 1) as k:
                    step(k, True)
                step(K - 1, False)

            def settled(ph):
                sp.wait_ge(sem("stored"), 16 * ALL_STORED[ph])
                if ph != "s1":
                    sp.wait_ge(sem("taken_dve"), FREE + count(PRODUCTS, K - 1, ph + "_tab", B))

            batches(first)
            for h in range(2):
                sp.wait_ge(sem(f"scattered{h}"), 16 * SLOTS * SORT_TURNS)
            chunk_ends(BY_SRC)
            step_tiles(BY_SRC)
            for prev, ph in (("in", "l0"), ("l0", "l1")):
                settled(prev)
                load_params(ph)
                batches(table_out(ph))

            def l2(k, more):
                sp.wait_ge(sem("l2_res"), k + 1)
                sp.dma_start(rows(res, k), rb[:]).then_inc(sem("l2_rstored"), 16)
                if more:
                    sp.wait_ge(sem("l2_rstored"), k * 16 + 16)
                    sp.dma_start(rb[:], rows(res, k + 1)).then_inc(sem("l2_r"), 16)
                sp.wait_ge(sem("taken_act"), count(TABLES, k, "l2_tab", B))
                sp.dma_start(rows(gat_table, k), tbuf[:]).then_inc(sem("stored"), 16)

            settled("l1")
            load_params("l2")
            sp.dma_start(rb[:], rows(res, 0)).then_inc(sem("l2_r"), 16)
            batches(l2)

            def ga_own(k, more):
                if more:
                    sp.wait_ge(sem("ga_self"), k + 1)
                    sp.dma_start(tbuf[:], rows(gat_table, k + 1)).then_inc(sem("ga_xh"), 16)

            def ga(k, more):
                sp.wait_ge(sem("ga_x2"), k + 1)
                sp.dma_start(rows(res, k), xb[:]).then_inc(sem("ga_rstored"), 16)
                if more:
                    sp.dma_start(rb[:], rows(res, k + 1)).then_inc(sem("ga_r"), 16)
                sp.wait_ge(sem("taken_act"), count(TABLES, k, "ga_tab", B))
                sp.dma_start(rows(table, k), tbuf[:, :, 0:D]).then_inc(sem("stored"), 16)

            settled("l2")
            sp.wait_ge(sem("l2_rstored"), 16 * K)
            load_params("ga")
            sp.wait_ge(sem("mm"), U + STEPS * (GAT + 1))
            sp.dma_start(tbuf[:], rows(gat_table, 0)).then_inc(sem("ga_xh"), 16)
            sp.dma_start(rb[:], rows(res, 0)).then_inc(sem("ga_r"), 16)
            batches(ga_own)
            batches(ga)
            settled("ga")
            load_params("s0")
            batches(table_out("s0"))

            def s1(k, more):
                sp.wait_ge(sem("s1_x3"), k + 1)
                sp.dma_start(rows(res, k), xb[:]).then_inc(sem("s1_rstored"), 16)
                for r in range(2):
                    sp.wait_ge(sem(f"s1_m{r}"), k * B + B)
                    sp.dma_start(rows(rel_table, k, r * T), tbuf2 if r else tbuf[:, :, 0:D]).then_inc(sem("stored"), 16)
                if more:
                    sp.dma_start(rb[:], rows(res, k + 1)).then_inc(sem("s1_r"), 16)

            settled("s0")
            load_params("s1")
            sp.wait_ge(sem("ga_rstored"), 16 * K)
            sp.dma_start(rb[:], rows(res, 0)).then_inc(sem("s1_r"), 16)
            batches(s1)
            settled("s1")
            load_params("fi")
            sp.wait_ge(sem("summed"), GB + len(PASSES) * STEPS)
            done = sem("fi_params")
            sp.dma_start(wbuf[:, :, W1_AT:W1_AT + H2], io["L3_gnn_W1"].rearrange("(q p) n -> p q n", p=P)).then_inc(done, 16)
            sp.dma_start(w2, io["L3_gnn_W2"]).then_inc(done, 16)
            sp.dma_start(w3, io["L3_gnn_W3"]).then_inc(done, 16)
            sp.dma_start(bhh, io["L3_gnn_b_hh"].rearrange("(a d) -> a d", d=D).unsqueeze(0).broadcast_to([P, 4, D])).then_inc(done, 16)

            out_t = out[0:(T - 1) * P, :].rearrange("(t p) c -> p t c", p=P)
            sp.wait_ge(sem("s1_rstored"), 16 * K)
            sp.dma_start(tbuf[:, :, 0:D], rows(res, 0)).then_inc(sem("fi_r"), 16)
            with sp.Fori(0, K - 1) as k:
                sp.wait_ge(sem("fi_y"), k + 1)
                sp.dma_start(out_t[:, bass.ds(k * B, B), :], tbuf[:, :, 0:D]).then_inc(sem("out_stored"), 16)
                sp.wait_ge(sem("out_stored"), k * 16 + 16)
                sp.dma_start(tbuf[:, :, 0:D], rows(res, k + 1)).then_inc(sem("fi_r"), 16)
            sp.wait_ge(sem("fi_y"), K)
            sp.dma_start(out_t[:, (K - 1) * B:T - 1, :], tbuf[:, 0:B - 1, 0:D]).then_inc(sem("out_stored"), 16)
            sp.dma_start(out[(T - 1) * P:N, :], tbuf[0:LAST, B - 1, 0:D]).then_inc(sem("out_stored"), 16)
            sp.wait_ge(sem("out_stored"), 16 * (K + 1))

        @block.gpsimd
        def _(pool):
            halves = [pool.alloc_register(f"halves{h}") for h in range(2)]
            sorts = [pool.alloc_register(f"sorts{h}") for h in range(2)]
            gat_puts = [pool.alloc_register(f"gat_puts{r}") for r in range(4)]
            for r in halves + sorts + gat_puts:
                pool.reg_mov(r, 0)
            exact = dict(allow_small_or_imprecise_dtypes=True)
            nc.gpsimd.iota(iota_row[:], [[1, P]], base=0, channel_multiplier=0, **exact).then_inc(sem("iota"), 1)
            nc.gpsimd.iota(part[:], [[0, 1]], base=0, channel_multiplier=1, **exact).then_inc(sem("iota"), 1)
            nc.gpsimd.iota(step_no, [[P, SB]], base=0, channel_multiplier=1, **exact).then_inc(sem("iota"), 1)
            nc.gpsimd.iota(chunk_row, [[1, C]], base=1, channel_multiplier=0, **exact).then_inc(sem("iota"), 1)

            def step_edges(o):
                pool.wait_ge(sem("chunk_i"), o + 1)
                for s in range(SB):
                    nc.gpsimd.indirect_dma_start(
                        out=edge_rows[:, s, :], out_offset=None, in_=recs[o],
                        in_offset=bass.IndirectOffsetOnAxis(ap=chunk_i[:, s:s + 1], axis=0)).then_inc(sem("edge_rows"), 16)

            step_edges(BY_DST)
            pool.wait_ge(sem("positions"), 1)
            scattered = recs[BY_SRC].rearrange("c e -> (c e)").unsqueeze(1)


            def scatter(i, first):
                for h in range(2):
                    half = slice(h * SLOTS, (h + 1) * SLOTS)
                    if not first:
                        pool.wait_ge(sem(f"scattered{h}"), i * (16 * SLOTS))
                    at_col = bass.ds(i * (2 * SLOTS) + h * SLOTS, SLOTS)
                    nc.gpsimd.tensor_copy(pos_slot[:, half], pos_i[:, at_col]).then_inc(sem("sort_slots"), 1)
                    nc.gpsimd.tensor_copy(rec_slot[:, half], rec_sb[BY_SRC][:, at_col]).then_inc(sem("sort_slots"), 1)
                    pool.wait_ge(sem("sort_slots"), i * 4 + (2 * h + 2))
                    pool.reg_add(sorts[h], sorts[h], 1)
                    for u in range(h * SLOTS, (h + 1) * SLOTS):
                        nc.gpsimd.indirect_dma_start(
                            out=scattered, out_offset=bass.IndirectOffsetOnAxis(ap=pos_slot[:, u:u + 1], axis=0),
                            in_=rec_slot[:, u:u + 1], in_offset=None).then_inc(sem(f"scattered{h}"), 16)

            scatter(0, True)
            with pool.Fori(1, SORT_TURNS) as i:
                scatter(i, False)
            step_edges(BY_SRC)
            for g, ph in enumerate(PASSES):
                pool.wait_ge(*((sem(ACC_READ[ph][0]), ACC_READ[ph][1]) if g > 0 else (sem("edge_T_read"), 4)))
                if g == 0:
                    pool.wait_ge(sem("tile_out"), 16 * SB * 2)
                nc.gpsimd.memset(acc[:], 0.0).then_inc(sem("acc_zero"), 1)
                pool.wait_ge(sem("stored"), 16 * ALL_STORED[ph])
                if g == GAT:
                    def gather(n, r):
                        pool.wait_ge(sem("idx_ready"), n + (HALVES * g + 1))
                        pool.reg_add(gat_puts[r], gat_puts[r], 1)
                        for u in range(HALF):
                            nc.gpsimd.indirect_dma_start(
                                out=gat_ring[r][:, u, :], out_offset=None, in_=gat_table,
                                in_offset=bass.IndirectOffsetOnAxis(ap=idx_slot[:, r * HALF + u:r * HALF + u + 1], axis=0)
                            ).then_inc(slot_sem(r, u), 16)

                    gat_halves(pool, gather)
                    continue
                tab = rel_table if ph == "s1" else table
                with pool.Fori(0, TURNS) as i:
                    for h in range(2):
                        pool.wait_ge(sem("idx_ready"), i * 2 + (HALVES * g + h + 1))
                        pool.reg_add(halves[h], halves[h], 1)
                        for u in range(h * HALF, (h + 1) * HALF):
                            nc.gpsimd.indirect_dma_start(
                                out=ring[:, u, 0:D], out_offset=None, in_=tab,
                                in_offset=bass.IndirectOffsetOnAxis(ap=idx_slot[:, u:u + 1], axis=0)).then_inc(sem(f"gathered{u}"), 16)
            pool.wait_ge(sem("idx_ready"), sum((pool.snap(r) for r in halves[1:] + gat_puts), pool.snap(halves[0])))

            pool.wait_ge(sem("sort_slots"), pool.snap(sorts[0]) + pool.snap(sorts[1]))

        @block.tensor
        def _(pe):
            regs = [pe.alloc_register(f"pe_tile{u}") for u in range(4 * HALF)]

            def unit(k, unit, w, n, ready=None, src=hbuf, kt=Q, hT_of=None):
                def transposed(j):
                    if ready in PRODUCT_UNITS:
                        pe.wait_ge(sem("taken_dve"), FREE + count(PRODUCTS, k, ready, B, j))
                    else:
                        pe.wait_ge(sem(ready), k * B + (j + 1))
                    pe.wait_ge(sem("acts_hT"), count(TRANSPOSED, k, unit, B, j))
                    for q in range(kt):
                        last = nc.tensor.transpose(psum[:, j % BANKS, q * P:(q + 1) * P], src[:, j, q * P:(q + 1) * P], ident[:])
                    last.then_inc(sem("acts_T"), 1)

                def product(j):
                    pe.wait_ge(sem("acts_hT"), FREE + count(TRANSPOSED, k, hT_of or unit, B, j))
                    pe.wait_ge(sem("taken_dve"), count(PRODUCTS, k, unit, B, j))
                    for q in range(kt):
                        last = nc.tensor.matmul(psum[:, 4 + j % BANKS, 0:n], hT[:, j * Q + q, :], w(q),
                                                start=(q == 0), stop=(q == kt - 1))
                    last.then_inc(sem("product"), 1)

                for j in range(B):
                    if not hT_of:
                        if j == 0:
                            transposed(0)
                        if j + 1 < B:
                            transposed(j + 1)
                    product(j)

            def cols(at, n):
                return lambda q: wbuf[:, q, at:at + n]

            def edge_pass(g, w):
                with pe.Fori(0, TURNS) as i:
                    for u in range(U):
                        pe.wait_ge(sem(f"gathered{u}"), i * 16 + 16 * (filled(g, u // HALF) + 1))
                        pe.wait_ge(sem("onehot"), i * U + (ONEHOTS[g] + u + 1))
                        pe.wait_ge(sem("summed"), i * U + (STEPS * g + u + 1))
                        nc.tensor.matmul(psum[:, u % GB, 0:w], onehot[:, u, :], ring[:, u, 0:w],
                                         start=True, stop=True).then_inc(sem("mm"), 1)

            HC = C // 2

            def chunk_bounds(o):
                pe.wait_ge(sem("bound_row"), o + 1)
                for b in range(2):
                    last = nc.tensor.matmul(psum[:, b, 0:HC], ones[0:1, :], bound_row[:, b * HC:(b + 1) * HC], start=True, stop=True)
                last.then_inc(sem("bound_mm"), 1)

            def step_tables(o):
                for a in range(2):
                    pe.wait_ge(sem("edge_f"), 2 * o + a + 1)
                    if a > 0:
                        pe.wait_ge(sem("edge_T_read"), 2 * o + 1)
                    for s in range(SB):
                        last = nc.tensor.transpose(psT[:, s, :], edge_f[:, a, s, :], ident[:])
                    last.then_inc(sem("edge_T"), 1)
                pe.wait_ge(sem("edge_T_read"), 2 * o + 2)

            pe.wait_ge(sem("consts"), 1)
            chunk_bounds(BY_DST)
            pe.wait_ge(sem("counts"), T)
            nc.tensor.matmul(psum[:, 2, 0:T], before, counts, start=True, stop=True)
            nc.tensor.matmul(psum[:, 3, 0:T], ones[:], counts, start=True, stop=True).then_inc(sem("count_mm"), 1)
            step_tables(BY_DST)
            pe.wait_ge(sem("in_params"), 16 * NLOADS["in"])
            with pe.Fori(0, K) as k:
                unit(k, "in_u", cols(W["in", "W_in"], D), D, "in_h")
                unit(k, "in_tab", cols(W["in", "agg"], 2 * D), 2 * D, "in_u")
            chunk_bounds(BY_SRC)
            step_tables(BY_SRC)
            edge_pass(0, D + 1)
            for g, ph in ((1, "l0"), (2, "l1")):
                pe.wait_ge(sem(ph + "_params"), 16 * NLOADS[ph])
                with pe.Fori(0, K) as k:
                    unit(k, ph + "_tab", cols(W[ph, "agg"], 2 * D), 2 * D, ph + "_h")
                edge_pass(g, D)
            pe.wait_ge(sem("l2_params"), 16 * NLOADS["l2"])
            pe.wait_ge(sem("w_att"), 2 * Q)
            with pe.Fori(0, K) as k:
                unit(k, "l2_u", cols(W["l2", "W_out"], D), D, "l2_h")
                unit(k, "l2_tab", cols(W["l2", "W_gat"], GW + HEADS), GW + HEADS, "l2_ln_h")
            pe.wait_ge(sem("amax"), 1)
            nc.tensor.transpose(psum[0:HEADS, 0, 0:P], amax[:], ident[:]).then_inc(sem("amax_T"), 1)
            pe.wait_ge(sem("gdiag"), 1)
            nc.tensor.matmul(psum[:, 1, 0:HEADS], ones[0:HEADS, :], gdiag[:], start=True, stop=True).then_inc(sem("gmax_mm"), 1)
            g = GAT
            pe.wait_ge(sem("dst_tab"), 1)
            pe.wait_ge(sem("tile_row"), 32)

            def onehots_T(n, r):
                pe.wait_ge(sem("onehot"), n * HALF + (ONEHOTS[g] + HALF))
                for v in range(HALF):
                    last = nc.tensor.transpose(ps_oh[:, v, :], onehot[:, r * HALF + v, :], ident[:])
                last.then_inc(sem("oh_T"), 1)

            def step_tiles(n, count):
                some = regs[0:count * HALF]
                nc.tensor.load(some, tile_row[0:1, BY_DST, bass.ds(n * HALF, count * HALF)])
                return some

            def logits(n, tiles):
                pe.wait_ge(sem("oh_t"), n + 1)
                if isinstance(n, int) and n == 0:
                    pass
                else:
                    pe.wait_ge(sem("z_less"), n)
                for v in range(HALF):
                    last = nc.tensor.matmul(ps_log[:, v, :], onehot_t[:, v, :],
                                            dst_tab[:, bass.ds(nc.tensor.snap(tiles[v]), 1), :].rearrange("p t h -> p (t h)"),
                                            start=True, stop=True)
                last.then_inc(sem("log_mm"), 1)

            def gat_half(n, r, tiles):
                ahead = not isinstance(n, int) or n + 2 < HALVES
                if ahead:
                    onehots_T(n + 2, (r + 2) % 4)
                for v in range(HALF):
                    pe.wait_ge(sem("msg"), n * HALF + (v + 1))
                    pe.wait_ge(sem("summed"), n * HALF + (STEPS * g + v + 1))
                    nc.tensor.matmul(psum[:, v, 0:GW], onehot[:, r * HALF + v, :], gat_ring[r][:, v, :],
                                     start=True, stop=True).then_inc(sem("mm"), 1)
                if ahead:
                    logits(n + 2, tiles)

            for n in range(2):
                onehots_T(n, n)
                logits(n, step_tiles(n, 1))
            gat_halves(pe, gat_half, lambda n, count: step_tiles(n + 2, count))
            for bank, (name, items, at) in enumerate((("bs", 1, lambda t, j: acc[:, bass.ds(t, 1), 0:D].rearrange("p t c -> p (t c)")),
                                                      ("bv", B, lambda t, j: hbuf[:, j, :]))):
                def sums(k):
                    for j in range(B):
                        pe.wait_ge(sem(name + "_rows"), k * items + (j + 1 if items > 1 else 1))
                        first, final = (isinstance(k, int) and k == m and j == n for m, n in ((0, 0), (K - 1, B - 1)))
                        nc.tensor.matmul(psum[:, bank, 0:D], (ones_last if final else ones)[:], at(k * B + j, j),
                                         start=first, stop=final).then_inc(sem(name + "_mm"), 1)
                sums(0)
                with pe.Fori(1, K - 1) as k:
                    sums(k)
                sums(K - 1)
            for g, ph, w, h in ((4, "ga", "W0", "ga_ln_h"), (5, "s0", "W1", "s0_silu")):
                pe.wait_ge(sem(ph + "_params"), 16 * NLOADS[ph])
                with pe.Fori(0, K) as k:
                    unit(k, ph + "_tab", cols(W[ph, w], D), D, h)
                edge_pass(g, D)
            pe.wait_ge(sem("s1_params"), 16 * NLOADS["s1"])
            with pe.Fori(0, K) as k:
                unit(k, "s1_u0", cols(W["s1", "R0"], D), D, "s1_ln_h")
                unit(k, "s1_u1", cols(W["s1", "R1"], D), D, hT_of="s1_u0")
                for r, src in enumerate((hbuf, hbuf2)):
                    unit(k, f"s1_v{r}", cols(W["s1", f"R{r}"], D), D, f"s1_relu{r}", src)
            edge_pass(6, D)
            pe.wait_ge(sem("fi_params"), 16 * NLOADS["fi"])
            with pe.Fori(0, K) as k:
                unit(k, "fi_i", cols(0, D), D, "fi_agg")
                unit(k, "fi_g", cols(2 * D, D), D, hT_of="fi_i")
                unit(k, "fi_o", cols(3 * D, D), D, hT_of="fi_i")
                unit(k, "fi_1", cols(W1_AT, H2), H2, "fi_hn")
                unit(k, "fi_2", lambda q: w2, H2, "fi_relu1", kt=1)
                unit(k, "fi_3", lambda q: w3, D, "fi_relu2", kt=1)

        @block.scalar
        def _(act):
            def take_T(k, unit, kt=Q, table=None, n=D):
                def rows(j):
                    if j == 0:
                        act.wait_ge(sem("stored"), k * 16 + 16 * STORED[table])
                    act.wait_ge(sem("product"), count(PRODUCTS, k, unit, B, j))
                    nc.scalar.copy(tbuf[:, j, 0:n], psum[:, 4 + j % BANKS, 0:n]).then_inc(sem("taken_act"), 1)

                for j in range(B):
                    act.wait_ge(sem("acts_T"), count(TRANSPOSED, k, unit, B, j))
                    nc.scalar.copy(hT[:, j * Q:j * Q + kt, :].rearrange("p q c -> p (q c)"),
                                   psum[:, j % BANKS, 0:kt * P]).then_inc(sem("acts_hT"), 1)
                    if table and j > 0:
                        rows(j - 1)
                if table:
                    rows(B - 1)

            def take_tab(k, ph, n=D):
                take_T(k, ph + "_tab", Q, ph, n)

            def ln_relu(k, ph, done):
                act.wait_ge(sem("ln_ve"), count(NORMS, k, ph))
                nc.scalar.activation(sd[:], mv[:, :, 1], ACT.Sqrt).then_inc(sem("ln_sd"), 1)
                act.wait_ge(sem("ln_bias"), count(LN_BIASED, k, ph))
                for j in range(B):
                    nc.scalar.activation(hbuf[:, j, :], xb[:, j, :], ACT.Relu, bias=nmr[:, j:j + 1],
                                         scale=rstd[:, j:j + 1]).then_inc(sem(done), 1)

            def on_tiles(k, ready, to, of, func, done, n=D):
                for j in range(B):
                    if ready in PRODUCT_UNITS:
                        act.wait_ge(sem("taken_dve"), FREE + count(PRODUCTS, k, ready, B, j))
                    else:
                        act.wait_ge(sem(ready), k * B + (j + 1))
                    nc.scalar.activation(to[:, j, 0:n], of[:, j, 0:n], func).then_inc(sem(done), 1)

            def put_indices(i, h, g, idx):
                act.wait_ge(sem("mm"), i * U + (STEPS * g + (h + 1) * HALF))
                nc.scalar.copy(idx_slot[:, h * HALF:(h + 1) * HALF],
                               idx[:, bass.ds(i * U + h * HALF, HALF)]).then_inc(sem("idx_ready"), 1)

            def edge_pass(g, idx):
                with act.Fori(0, TURNS) as i:
                    for h in range(2):
                        put_indices(i, h, g, idx)

            def step_tables(o):
                for a, to in enumerate((idx_by_src if o == BY_SRC else idx_rel, node_loc[:, o, :])):
                    act.wait_ge(sem("edge_T"), 2 * o + a + 1)
                    for f in range(0, SB, 4):
                        n = min(4, SB - f)
                        last = nc.scalar.copy(to[:, f * P:(f + n) * P], psT[:, f:f + n, :].rearrange("p f c -> p (f c)"))
                    last.then_inc(sem("edge_T_read"), 1)

            step_tables(BY_DST)
            with act.Fori(0, K) as k:
                ln_relu(k, "in", "in_h")
                take_T(k, "in_u")
                take_tab(k, "in")
            step_tables(BY_SRC)
            edge_pass(0, idx_by_src)
            for g, ph in ((1, "l0"), (2, "l1")):
                with act.Fori(0, K) as k:
                    on_tiles(k, ph + "_pre", hbuf, xb, ACT.Relu, ph + "_h")
                    take_tab(k, ph)
                edge_pass(g, idx_by_src)
            with act.Fori(0, K) as k:
                on_tiles(k, "l2_pre", hbuf, xb, ACT.Relu, "l2_h")
                take_T(k, "l2_u")
                ln_relu(k, "l2", "l2_ln_h")
                take_tab(k, "l2", GW)
            g = GAT

            def gat_indices(n, r):
                if not isinstance(n, int) or n >= 4:
                    act.wait_ge(sem("mm"), n * HALF + (U + STEPS * g - 3 * HALF))
                nc.scalar.copy(idx_slot[:, r * HALF:(r + 1) * HALF],
                               idx_by_dst[:, bass.ds(n * HALF, HALF)]).then_inc(sem("idx_ready"), 1)

            def take_onehots(n):
                act.wait_ge(sem("oh_T"), n + 1)
                nc.scalar.copy(onehot_t[:, 0:4, :], ps_oh[:, 0:4, :])
                nc.scalar.copy(onehot_t[:, 4:HALF, :], ps_oh[:, 4:HALF, :]).then_inc(sem("oh_t"), 1)

            def weights(n, r):
                act.wait_ge(sem("z_clamped"), n + 1)
                nc.scalar.activation(gat_ring[r][:, :, D:GW], zlog2[:], ACT.Exp).then_inc(sem("edge_w"), 1)

            def gat_half(n, r):
                for ahead, f in ((3, lambda: gat_indices(n + 3, (r + 3) % 4)), (2, lambda: take_onehots(n + 2)),
                                 (1, lambda: weights(n + 1, (r + 1) % 4))):
                    if not isinstance(n, int) or n + ahead < HALVES:
                        f()

            for n in range(3):
                gat_indices(n, n)
            for n in range(2):
                take_onehots(n)
            weights(0, 0)
            gat_halves(act, gat_half)
            act.wait_ge(sem("zs_clamped"), 1)
            nc.scalar.activation(w_self[:], w_self[:], ACT.Exp).then_inc(sem("w_self"), 1)

            def squares(k):
                act.wait_ge(sem("bv_dev"), k + 1)
                for j in range(B):
                    if not isinstance(k, int):
                        act.wait_ge(sem("bv_mm"), k * B + (j + 1 - B))
                    nc.scalar.activation(hbuf[:, j, :], xb[:, j, :], ACT.Square).then_inc(sem("bv_rows"), 1)

            squares(0)
            with act.Fori(1, K) as k:
                squares(k)
            act.wait_ge(sem("bn_ve"), 1)
            nc.scalar.activation(bn_b[:], bn_a[:], ACT.Sqrt).then_inc(sem("bn_sd"), 1)
            with act.Fori(0, K) as k:
                ln_relu(k, "ga", "ga_ln_h")
                take_tab(k, "ga")
            edge_pass(4, idx_by_src)

            def ln_silu(k, ph):
                act.wait_ge(sem("ln_ve"), count(NORMS, k, ph))
                nc.scalar.activation(sd[:], mv[:, :, 1], ACT.Sqrt).then_inc(sem("ln_sd"), 1)
                on_tiles(k, ph + "_n", hbuf, xb, ACT.Silu, ph + "_silu")

            with act.Fori(0, K) as k:
                ln_silu(k, "s0")
                take_tab(k, "s0")
            edge_pass(5, idx_by_src)
            with act.Fori(0, K) as k:
                ln_silu(k, "s1")
                ln_relu(k, "s1b", "s1_ln_h")
                take_T(k, "s1_u0")
                for r, (u, v) in enumerate(((hbuf, tbuf), (hbuf2, tbuf2))):
                    on_tiles(k, f"s1_u{r}", u, u, ACT.Relu, f"s1_relu{r}")
                for r, (u, v) in enumerate(((hbuf, tbuf), (hbuf2, tbuf2))):
                    take_T(k, f"s1_v{r}")
                    on_tiles(k, f"s1_v{r}", v, v, ACT.Relu, f"s1_m{r}")
            edge_pass(6, idx_rel)
            with act.Fori(0, K) as k:
                take_T(k, "fi_i")
                on_tiles(k, "fi_i", xb, xb, ACT.Sigmoid, "fi_si")
                on_tiles(k, "fi_g", rb, rb, ACT.Tanh, "fi_tg")
                on_tiles(k, "fi_c", xb, xb, ACT.Tanh, "fi_tc")
                on_tiles(k, "fi_o", rb, rb, ACT.Sigmoid, "fi_so")
                take_T(k, "fi_1")
                on_tiles(k, "fi_1", hbuf, hbuf, ACT.Relu, "fi_relu1", H2)
                take_T(k, "fi_2", 1)
                on_tiles(k, "fi_2", hbuf, hbuf, ACT.Relu, "fi_relu2", H2)
                take_T(k, "fi_3", 1)

        @block.vector
        def _(dve):
            V = nc.vector
            regs = [dve.alloc_register(f"dve_tile{u}") for u in range(4 * HALF)]

            def then(ins, name, value=1):
                ins.then_inc(sem(name), 1)
                dve.wait_ge(sem(name), value)

            norms = {ph: dve.alloc_register("norms_" + ph) for names in NORMS.values() for ph in names}
            for r in norms.values():
                V.reg_mov(r, 0)
            sort_tiles = dve.alloc_register("sort_tiles")
            V.reg_mov(sort_tiles, 0)
            once_n = [0]

            def once(ins):
                once_n[0] += 1
                then(ins, "dve_once", once_n[0])

            def ln_stats(k, ph, src=xb):
                for j in range(B):
                    last = V.bn_stats(st[:, j, :], src[:, j, :])
                last.then_inc(sem("ln_st"), 1)
                dve.wait_ge(sem("ln_st"), count(NORMS, k, ph))
                V.reg_add(norms[ph], norms[ph], 1)
                for j in range(B):
                    last = V.bn_aggr(mv[:, j, :], st[:, j, :])
                then(last, "ln_mv", count(NORMS, k, ph))
                V.tensor_scalar_add(mv[:, :, 1], mv[:, :, 1], LN_EPS).then_inc(sem("ln_ve"), 1)
                dve.wait_ge(sem("ln_sd"), count(NORMS, k, ph))
                then(V.reciprocal(rstd[:], sd[:]), "ln_rs", count(NORMS, k, ph))

            def ln_bias(k, ph):
                V.scalar_tensor_tensor(out=nmr[:], in0=mv[:, :, 0], scalar=-1.0, in1=rstd[:], op0=ALU.mult,
                                       op1=ALU.mult).then_inc(sem("ln_bias"), 1)

            def take(k, unit, f):
                for j in range(B):
                    if unit.endswith("_tab"):
                        dve.wait_ge(sem("taken_act"), count(TABLES, k, unit, B, j))
                    else:
                        dve.wait_ge(sem("product"), count(PRODUCTS, k, unit, B, j))
                    f(j, psum[:, 4 + j % BANKS, :]).then_inc(sem("taken_dve"), 1)

            def copied(to, of):
                return V.tensor_scalar(to, of, 1.0, None, op0=ALU.mult)

            def own_at(k, j):
                return own[:, bass.ds(k * B + j, 1), :].rearrange("p t c -> p (t c)")

            def mean_and_own(k, ph):
                for j in range(B):
                    t = bass.ds(k * B + j, 1)
                    V.scalar_tensor_tensor(out=xb[:, j, :], in0=acc[:, t, 0:D].rearrange("p t c -> p (t c)"), scalar=rdeg[:, t],
                                           in1=own_at(k, j), op0=ALU.mult, op1=ALU.add).then_inc(sem(ph + "_pre"), 1)

            def make_onehot(g, step, u):
                V.tensor_scalar(onehot[:, u, :], iota_row[:], node_loc[:, ORDER[g], bass.ds(step, 1)], None,
                                op0=ALU.is_equal).then_inc(sem("onehot"), 1)

            def add_sums(step, g, bank, tile, w):
                dve.wait_ge(sem("mm"), step + (U + STEPS * g + 1))
                dve.wait_ge(sem("summed"), step + (GB + STEPS * g))
                a = acc[:, bass.ds(V.snap(tile), 1), 0:w].rearrange("p t c -> p (t c)")
                V.tensor_tensor(a, a, psum[:, bank, 0:w], ALU.add).then_inc(sem("summed"), 1)

            def norms_done(g):
                for ph in NORMS.get(PASSES[g], ()):
                    dve.wait_ge(sem("ln_mv"), V.snap(norms[ph]))
                    n = list(norms).index(ph)
                    V.memset(carrier[:, n:n + 1], 0.0)

            def step_tiles(o, step, count):
                some = regs[0:count]
                V.load(some, tile_row[0:1, o, bass.ds(step, count)])
                return some

            def edge_pass(g, w):
                norms_done(g)
                for u in range(HALF):
                    make_onehot(g, u, u)
                dve.wait_ge(sem("acc_zero"), g + 1)
                with dve.Fori(0, TURNS) as i:
                    tiles = step_tiles(ORDER[g], i * U, U)
                    for u in range(U):
                        make_onehot(g, i * U + (u + HALF), (u + HALF) % U)
                        add_sums(i * U + u, g, u % GB, tiles[u], w)
                dve.wait_ge(sem("summed"), GB + STEPS * (g + 1))

            V.memset(edges[:, 0:2, :], NP - 1)
            V.memset(edges[:, 2, :], 0)
            V.memset(zrows, 0.0).then_inc(sem("pads_set"), 1)
            V.memset(all_ones, 1.0).then_inc(sem("acts_hT"), FREE)
            V.memset(position, 0.0).then_inc(sem("taken_dve"), FREE)
            V.memset(ones[:], 1.0).then_inc(sem("mm"), U)
            V.memset(ring[:, :, D:D + 1], 1.0).then_inc(sem("summed"), GB)
            dve.wait_ge(sem("iota"), 4)
            V.tensor_scalar(ones_last[:], part[:].broadcast_to([P, P]), float(LAST), None, op0=ALU.is_lt)
            V.tensor_scalar(before, iota_row[:], part[:], None, op0=ALU.is_gt)
            V.tensor_scalar(ident[:], iota_row[:], part[:], None, op0=ALU.is_equal).then_inc(sem("consts"), 1)
            dve.wait_ge(sem("edges"), 16 * 9)
            src_sb, dst_sb, rel_sb = (edges[:, a, :] for a in range(3))

            def shifted(to, of, bits, op=ALU.logical_shift_left):
                once(V.tensor_scalar(to, of, bits, None, op0=op))

            shifted(rec_sb[BY_DST], dst_sb, NODE)
            once(V.scalar_tensor_tensor(out=rel_sb, in0=rel_sb, scalar=float(NP), in1=src_sb, op0=ALU.mult, op1=ALU.add))
            once(V.tensor_tensor(rec_sb[BY_DST], rec_sb[BY_DST], rel_sb, ALU.bitwise_or))
            shifted(rec_sb[BY_SRC], src_sb, NODE)
            once(V.tensor_tensor(rec_sb[BY_SRC], rec_sb[BY_SRC], dst_sb, ALU.bitwise_or))
            shifted(src_sb, src_sb, 7, ALU.logical_shift_right)
            V.tensor_copy(key_tile, src_sb).then_inc(sem("rec_by_dst"), 1)
            dve.wait_ge(sem("rec_by_dst"), 1)

            HC = C // 2

            def step_chunks(o):
                dve.wait_ge(sem("last_rec"), 16 * (o + 1))
                shifted(last_tile, last_rec, NODE + 7, ALU.logical_shift_right)
                V.tensor_tensor(bound_row, last_tile, chunk_row, ALU.add).then_inc(sem("bound_row"), 1)
                dve.wait_ge(sem("bound_mm"), o + 1)
                once(V.tensor_copy(bounds.rearrange("p (b c) -> p b c", b=2), psum[:, 0:2, 0:HC]))
                for s in range(SB):
                    once(V.tensor_scalar(junk, bounds, step_no[:, s:s + 1], 0.0, op0=ALU.is_le, op1=ALU.add,
                                         accum_out=chunk_f[:, s:s + 1]))
                once(V.tensor_scalar(chunk_c, chunk_f, float(C - 1), None, op0=ALU.min))
                V.tensor_copy(chunk_i, chunk_c).then_inc(sem("chunk_i"), 1)
                once(V.tensor_tensor(tile_f, step_no, chunk_c, ALU.subtract))
                V.tensor_copy(tile_i, tile_f).then_inc(sem("tile_i"), 1)
                once(V.tensor_scalar(tile_base, tile_f, float(P), None, op0=ALU.mult))

            def step_tables(o):
                dve.wait_ge(sem("edge_rows"), 16 * SB * (o + 1))
                shifted(edge_i, edge_rows, (1 << NODE) - 1, ALU.bitwise_and)
                once(V.tensor_copy(edge_f[:, 0, :, :], edge_i))
                shifted(edge_i, edge_rows, NODE, ALU.logical_shift_right)
                V.memset(junk[:, 0:1], 0.0).then_inc(sem("edge_f"), 1)
                for s in range(SB):
                    last = V.tensor_scalar(edge_f[:, 1, s, :], edge_i[:, s, :], tile_base[:, s:s + 1], None, op0=ALU.subtract)
                last.then_inc(sem("edge_f"), 1)
                dve.wait_ge(sem("edge_T_read"), 2 * o + 2)

            step_chunks(BY_DST)
            with dve.Fori(0, T) as t:
                then(V.tensor_scalar(is_tile, key_tile, iota_row[:, bass.ds(t, 1)], 0.0, op0=ALU.is_equal, op1=ALU.add,
                                     accum_out=counts[:, bass.ds(t, 1)]), "counts", t + 1)
            dve.wait_ge(sem("count_mm"), 1)
            once(V.tensor_copy(totals, psum[:, 3, 0:T]))
            once(V.tensor_tensor_scan(ends, ones[:, 0:T], totals, 0.0, op0=ALU.mult, op1=ALU.add))
            once(V.tensor_tensor(starts, ends, totals, ALU.subtract))
            once(V.tensor_tensor(starts, starts, psum[:, 2, 0:T], ALU.add))
            with dve.Fori(0, T) as t:
                then(V.tensor_scalar(is_tile, key_tile, iota_row[:, bass.ds(t, 1)], None, op0=ALU.is_equal), "is_tile", t + 1)
                V.tensor_tensor_scan(running, all_ones, is_tile, starts[:, bass.ds(t, 1)], op0=ALU.mult, op1=ALU.add).then_inc(sem("running"), 1)
                dve.wait_ge(sem("running"), t + 1)
                V.reg_add(sort_tiles, sort_tiles, 1)
                then(V.copy_predicated(position, is_tile, running), "position", t + 1)
            dve.wait_ge(sem("position"), V.snap(sort_tiles))
            V.tensor_scalar(pos_i, position, -1.0, None, op0=ALU.add).then_inc(sem("positions"), 1)
            step_tables(BY_DST)
            once(V.tensor_scalar(idx_by_dst[:], idx_rel[:], float(NP), float(-NP), op0=ALU.is_ge, op1=ALU.mult))
            once(V.tensor_tensor(idx_by_dst[:], idx_by_dst[:], idx_rel[:], ALU.add))

            def own_hid(ph):
                def f(k):
                    return lambda j, ps: V.tensor_tensor(own_at(k, j), ps[:, D:2 * D], row(ph, "b_hid"), ALU.add)
                return f

            dve.wait_ge(sem("in_params"), 16 * NLOADS["in"])
            with dve.Fori(0, K) as k:
                dve.wait_ge(sem("in_x"), k * 16 + 16)
                ln_stats(k, "in")
                ln_bias(k, "in")
                take(k, "in_u", lambda j, ps: V.tensor_tensor(hbuf[:, j, :], ps[:, 0:D], row("in", "b_in"), ALU.add))
                take(k, "in_tab", own_hid("in")(k))
            step_chunks(BY_SRC)
            step_tables(BY_SRC)
            dve.wait_ge(sem("tile_row"), 32)
            edge_pass(0, D + 1)
            once(V.tensor_scalar(rdeg[:], acc[:, :, D], 1.0, None, op0=ALU.max))
            once(V.reciprocal(rdeg[:], rdeg[:]))
            for g, ph in ((1, "l0"), (2, "l1")):
                dve.wait_ge(sem(ph + "_params"), 16 * NLOADS[ph])
                with dve.Fori(0, K) as k:
                    mean_and_own(k, ph)
                    take(k, ph + "_tab", own_hid(ph)(k))
                edge_pass(g, D)

            dve.wait_ge(sem("l2_params"), 16 * NLOADS["l2"])
            wg = W["l2", "W_gat"]
            for a, name in enumerate(("att_src", "att_dst")):
                for q in range(Q):
                    n = a * Q + q
                    once(V.tensor_tensor(xb[:, n, :], wbuf[:, q, wg:wg + D], row("l2", name), ALU.mult))
                    V.tensor_reduce(wbuf[:, q, wg + D + a * HEADS:wg + D + (a + 1) * HEADS], heads(xb[:, n, :]),
                                    axis=AX, op=ALU.add).then_inc(sem("w_att"), 1)
            dve.wait_ge(sem("w_att"), 2 * Q)

            def logits(k):
                def f(j, ps):
                    t = bass.ds(k * B + j, 1)
                    copied(a_own[:, t, :].rearrange("p t h -> p (t h)"), ps[:, D:GW])
                    return copied(dst_tab[:, t, 0:HEADS].rearrange("p t h -> p (t h)"), ps[:, GW:GW + HEADS])
                return f

            with dve.Fori(0, K) as k:
                mean_and_own(k, "l2")
                dve.wait_ge(sem("l2_r"), k * 16 + 16)
                then(V.tensor_tensor(rb[:], rb[:], over_batch(row("l2", "b_out")), ALU.add), "l2_rb", k + 1)
                take(k, "l2_u", lambda j, ps: V.tensor_tensor(xb[:, j, :], ps[:, 0:D], rb[:, j, :], ALU.add))
                dve.wait_ge(sem("taken_dve"), FREE + count(PRODUCTS, k, "l2_u", B))
                ln_stats(k, "l2")
                ln_bias(k, "l2")
                dve.wait_ge(sem("l2_ln_h"), k * B + B)
                V.tensor_tensor(rb[:], xb[:], hbuf[:], ALU.add).then_inc(sem("l2_res"), 1)
                take(k, "l2_tab", logits(k))
                dve.wait_ge(sem("l2_res"), k + 1)
            dve.wait_ge(sem("taken_dve"), FREE + count(PRODUCTS, K - 1, "l2_tab", B))
            V.tensor_reduce(amax[:], a_own[:, :, :].rearrange("p t h -> p h t"), axis=AX, op=ALU.max).then_inc(sem("amax"), 1)
            dve.wait_ge(sem("amax_T"), 1)
            once(V.tensor_reduce(gmax[:], psum[0:HEADS, 0, 0:P], axis=AX, op=ALU.max))
            V.tensor_scalar(gdiag[:], ident[0:HEADS, 0:HEADS], gmax[:], None, op0=ALU.mult).then_inc(sem("gdiag"), 1)
            dve.wait_ge(sem("gmax_mm"), 1)
            once(V.tensor_copy(gmax_b[:], psum[:, 1, 0:HEADS]))
            dmax = dst_tab[:, :, HEADS:2 * HEADS]
            dlog = dst_tab[:, :, 0:HEADS]
            once(V.tensor_tensor(dmax, dlog, gmax_b[:].unsqueeze(1).broadcast_to([P, T, HEADS]), ALU.add))
            V.scalar_tensor_tensor(out=dmax, in0=dmax, scalar=SLOPE, in1=dmax, op0=ALU.mult, op1=ALU.max).then_inc(sem("dst_tab"), 1)

            g = GAT
            norms_done(g)

            def gat_onehots(n, r):
                for v in range(HALF):
                    make_onehot(g, n * HALF + v, r * HALF + v)

            def gat_logits(n, r):
                if not isinstance(n, int) or n > 0:
                    dve.wait_ge(sem("edge_w"), n)
                if r < 2:
                    for v in range(HALF):
                        dve.wait_ge(slot_sem(r, v), n * 4 + (16 * (filled(g, r) + 1) - 4 * r))
                else:
                    dve.wait_ge(slot_sem(r, 0), n * (4 * HALF) + HALF * (16 - 4 * r))
                dve.wait_ge(sem("log_mm"), n + 1)
                then(V.tensor_tensor(zlog[:], ps_log[:, :, 0:HEADS], gat_ring[r][:, :, D:GW], ALU.add), "z", n + 1)
                then(V.scalar_tensor_tensor(out=zlog2[:], in0=zlog[:], scalar=SLOPE, in1=zlog[:], op0=ALU.mult, op1=ALU.max), "z_leaky", n + 1)
                then(V.tensor_tensor(zlog[:], zlog2[:], ps_log[:, :, HEADS:2 * HEADS], ALU.subtract), "z_less", n + 1)
                V.tensor_scalar(zlog2[:], zlog[:], 0.0, None, op0=ALU.min).then_inc(sem("z_clamped"), 1)

            def gat_half(n, r, tiles):
                first = isinstance(n, int) and n == 0
                dve.wait_ge(sem("edge_w"), n + 1)
                for v in range(HALF):
                    if not first:
                        add_sums((n - 1) * HALF + v, g, v, tiles[v], GW)
                    V.tensor_tensor(heads(gat_ring[r][:, v, 0:D]), heads(gat_ring[r][:, v, 0:D]),
                                    gat_ring[r][:, v, D:GW].unsqueeze(2).broadcast_to([P, HEADS, DH]), ALU.mult).then_inc(sem("msg"), 1)
                if not isinstance(n, int) or n + 1 < HALVES:
                    gat_logits(n + 1, (r + 1) % 4)
                if not isinstance(n, int) or n + 3 < HALVES:
                    gat_onehots(n + 3, (r + 3) % 4)

            for n in range(3):
                gat_onehots(n, n)
            dve.wait_ge(sem("acc_zero"), g + 1)
            gat_logits(0, 0)
            def last_tiles(n, count):
                if isinstance(n, int) and n == 0:
                    return [None] * HALF + step_tiles(BY_DST, 0, (count - 1) * HALF)
                return step_tiles(BY_DST, (n - 1) * HALF, count * HALF)

            gat_halves(dve, gat_half, last_tiles)
            for v, tile in enumerate(step_tiles(BY_DST, (HALVES - 1) * HALF, HALF)):
                add_sums((HALVES - 1) * HALF + v, g, v, tile, GW)
            dve.wait_ge(sem("summed"), GB + STEPS * (g + 1))

            once(V.tensor_tensor(w_self[:], a_own[:], dlog, ALU.add))
            once(V.scalar_tensor_tensor(out=w_self[:], in0=w_self[:], scalar=SLOPE, in1=w_self[:], op0=ALU.mult, op1=ALU.max))
            once(V.tensor_tensor(w_self[:], w_self[:], dmax, ALU.subtract))
            V.tensor_scalar(w_self[:], w_self[:], 0.0, None, op0=ALU.min).then_inc(sem("zs_clamped"), 1)
            dve.wait_ge(sem("ga_params"), 16 * NLOADS["ga"])
            dve.wait_ge(sem("w_self"), 1)

            def by_head(ap):
                return ap.rearrange("p j (h d) -> p j h d", h=HEADS)

            def over_dim(ap):
                return ap.unsqueeze(3).broadcast_to([P, B, HEADS, DH])

            with dve.Fori(0, K) as k:
                t = bass.ds(k * B, B)
                dve.wait_ge(sem("ga_xh"), k * 16 + 16)
                then(V.tensor_tensor(by_head(xb[:]), by_head(tbuf[:, :, 0:D]), over_dim(w_self[:, t, :]), ALU.mult), "ga_self", k + 1)
                V.tensor_tensor(xb[:], xb[:], acc[:, t, 0:D], ALU.add)
                then(V.tensor_tensor(den[:], acc[:, t, D:GW], w_self[:, t, :], ALU.add), "ga_den", k + 1)
                then(V.reciprocal(den[:], den[:]), "ga_rden", k + 1)
                then(V.tensor_tensor(by_head(xb[:]), by_head(xb[:]), over_dim(den[:]), ALU.mult), "ga_quot", k + 1)
                V.tensor_tensor(acc[:, t, 0:D], xb[:], over_batch(row("ga", "bias")), ALU.add).then_inc(sem("bs_rows"), 1)
                dve.wait_ge(sem("bs_rows"), k + 1)
            dve.wait_ge(sem("bs_mm"), T)
            once(V.tensor_scalar(bn_mean[:], psum[:, 0, 0:D], 1.0 / N, None, op0=ALU.mult))

            def deviations(k):
                t = bass.ds(k * B, B)
                if not isinstance(k, int):
                    dve.wait_ge(sem("bv_rows"), k * B)
                V.tensor_tensor(xb[:], acc[:, t, 0:D], over_batch(bn_mean[:]), ALU.subtract).then_inc(sem("bv_dev"), 1)

            deviations(0)
            with dve.Fori(1, K) as k:
                deviations(k)
            dve.wait_ge(sem("bv_mm"), T)
            V.tensor_scalar(bn_a[:], psum[:, 1, 0:D], 1.0 / N, LN_EPS, op0=ALU.mult, op1=ALU.add).then_inc(sem("bn_ve"), 1)
            dve.wait_ge(sem("bn_sd"), 1)
            once(V.reciprocal(bn_a[:], bn_b[:]))
            once(V.tensor_tensor(bn_a[:], bn_a[:], row("ga", "gamma"), ALU.mult))
            once(V.tensor_tensor(bn_b[:], bn_mean[:], bn_a[:], ALU.mult))
            once(V.tensor_tensor(bn_b[:], row("ga", "beta"), bn_b[:], ALU.subtract))
            with dve.Fori(0, K) as k:
                t = bass.ds(k * B, B)
                then(V.tensor_tensor(xb[:], acc[:, t, 0:D], over_batch(bn_a[:]), ALU.mult), "ga_scaled", k + 1)
                then(V.tensor_tensor(xb[:], xb[:], over_batch(bn_b[:]), ALU.add), "ga_shifted", k + 1)
                dve.wait_ge(sem("ga_r"), k * 16 + 16)
                then(V.tensor_tensor(xb[:], xb[:], rb[:], ALU.add), "ga_x2", k + 1)
                ln_stats(k, "ga")
                ln_bias(k, "ga")
                take(k, "ga_tab", lambda j, ps: copied(own_at(k, j), ps[:, 0:D]))
                dve.wait_ge(sem("ga_rstored"), k * 16 + 16)
            edge_pass(4, D)

            def ln_affine(k, ph):
                mean_and_own(k, ph)
                dve.wait_ge(sem(ph + "_pre"), k * B + B)
                then(V.tensor_tensor(xb[:], xb[:], over_batch(row(ph, "b")), ALU.add), ph + "_z", k + 1)
                ln_stats(k, ph)
                for j in range(B):
                    last = V.tensor_scalar(xb[:, j, :], xb[:, j, :], mv[:, j, 0:1], rstd[:, j:j + 1], op0=ALU.subtract, op1=ALU.mult)
                then(last, ph + "_hat", k + 1)
                then(V.tensor_tensor(xb[:], xb[:], over_batch(row(ph, "g")), ALU.mult), ph + "_hg", k + 1)
                for j in range(B):
                    V.tensor_tensor(xb[:, j, :], xb[:, j, :], row(ph, "beta"), ALU.add).then_inc(sem(ph + "_n"), 1)

            dve.wait_ge(sem("s0_params"), 16 * NLOADS["s0"])
            with dve.Fori(0, K) as k:
                ln_affine(k, "s0")
                take(k, "s0_tab", lambda j, ps: copied(own_at(k, j), ps[:, 0:D]))
            edge_pass(5, D)
            dve.wait_ge(sem("s1_params"), 16 * NLOADS["s1"])
            with dve.Fori(0, K) as k:
                ln_affine(k, "s1")
                dve.wait_ge(sem("s1_silu"), k * B + B)
                dve.wait_ge(sem("s1_r"), k * 16 + 16)
                then(V.tensor_tensor(xb[:], hbuf[:], rb[:], ALU.add), "s1_x3", k + 1)
                ln_stats(k, "s1b")
                ln_bias(k, "s1b")
                for r, u in enumerate((hbuf, hbuf2)):
                    take(k, f"s1_u{r}", lambda j, ps: V.tensor_tensor(u[:, j, 0:D], ps[:, 0:D], row("s1", f"b{r}"), ALU.add))
                for r, v in enumerate((tbuf, tbuf2)):
                    dve.wait_ge(sem("stored"), k * 32 + (16 * STORED["s1"] + 16 * r))
                    take(k, f"s1_v{r}", lambda j, ps: V.tensor_tensor(v[:, j, 0:D], ps[:, 0:D], row("s1", f"b{r}"), ALU.add))
                dve.wait_ge(sem("s1_rstored"), k * 16 + 16)
            dve.wait_ge(sem("stored"), 16 * ALL_STORED["s1"])
            edge_pass(6, D)

            dve.wait_ge(sem("fi_params"), 16 * NLOADS["fi"])
            once(V.tensor_tensor(pbuf[:, 0:4 * D].rearrange("p (a d) -> p a d", a=4),
                                 pbuf[:, 0:4 * D].rearrange("p (a d) -> p a d", a=4), bhh, ALU.add))

            def biased(to, at, n):
                return lambda j, ps: V.tensor_tensor(to[:, j, 0:n], ps[:, 0:n], pbuf[:, at:at + n], ALU.add)

            with dve.Fori(0, K) as k:
                for j in range(B):
                    copied(hbuf[:, j, :], acc[:, bass.ds(k * B + j, 1), 0:D].rearrange("p t c -> p (t c)")).then_inc(sem("fi_agg"), 1)
                take(k, "fi_i", biased(xb, 0, D))
                take(k, "fi_g", biased(rb, 2 * D, D))
                for j in range(B):
                    dve.wait_ge(sem("fi_si"), k * B + (j + 1))
                    dve.wait_ge(sem("fi_tg"), k * B + (j + 1))
                    V.tensor_tensor(xb[:, j, :], xb[:, j, :], rb[:, j, :], ALU.mult).then_inc(sem("fi_c"), 1)
                dve.wait_ge(sem("fi_c"), k * B + B)
                take(k, "fi_o", biased(rb, 3 * D, D))
                for j in range(B):
                    dve.wait_ge(sem("fi_tc"), k * B + (j + 1))
                    dve.wait_ge(sem("fi_so"), k * B + (j + 1))
                    V.tensor_tensor(hbuf[:, j, :], rb[:, j, :], xb[:, j, :], ALU.mult).then_inc(sem("fi_hn"), 1)
                dve.wait_ge(sem("fi_hn"), k * B + B)
                take(k, "fi_1", biased(hbuf, R["fi", "b1"], H2))
                take(k, "fi_2", biased(hbuf, R["fi", "b2"], H2))
                take(k, "fi_3", biased(xb, R["fi", "b3"], D))
                dve.wait_ge(sem("taken_dve"), FREE + count(PRODUCTS, k, "fi_3", B))
                dve.wait_ge(sem("fi_r"), k * 16 + 16)
                then(V.tensor_tensor(tbuf[:, :, 0:D], tbuf[:, :, 0:D], xb[:], ALU.add), "fi_y", k + 1)


_TRANSPOSED = ("L2_gnn_W0", "L2_gnn_W1", "L3_gnn_W_rel", "L3_gnn_W_ih", "L3_gnn_W1", "L3_gnn_W2", "L3_gnn_W3")


def kernel(**inputs):
    import numpy as _np
    import concourse.bacc as _bacc
    from concourse import mybir as _mybir
    from concourse.bass_utils import run_bass_kernel_spmd as _run

    nc = _bacc.Bacc("TRN2", target_bir_lowering=False, num_devices=1)
    arrays, io = {}, {}
    for name, value in inputs.items():
        a = _np.asarray(value)
        if name in _TRANSPOSED:
            a = a.swapaxes(-1, -2)
        a = _np.ascontiguousarray(a)
        arrays["in_" + name] = a
        io[name] = nc.dram_tensor("in_" + name, a.shape, _mybir.dt.from_np(a.dtype), kind="ExternalInput").ap()
    out = nc.dram_tensor("out_x", inputs["x"].shape, _mybir.dt.float32, kind="ExternalOutput").ap()
    build(nc, io, out)
    return _run(nc, [arrays], core_ids=[0]).results[0]["out_x"]
```

```python
from contextlib import ExitStack

import concourse.bass as bass
from concourse import mybir

F32 = mybir.dt.float32
I32 = mybir.dt.int32
I16 = mybir.dt.int16
BF16 = mybir.dt.bfloat16
ALU = mybir.AluOpType
ACT = mybir.ActivationFunctionType
AX = mybir.AxisListType.X

P = 128
LN_EPS = 1e-5
SLOPE = 0.2


def build(nc, io, out):
    N, D = io["x"].shape
    E = io["src"].shape[0]
    HEADS, DH = io["L1_gnn_att_src"].shape
    T = -(-N // P)
    NP = T * P
    C = -(-E // P)
    EP = C * P
    STEPS = C + T - 1
    U = 10
    HALF = U // 2
    TURNS = STEPS // U
    assert TURNS * U == STEPS
    SB = -(-(STEPS + HALF) // P)
    B = 7
    K = T // B
    assert K * B == T
    GW = D + HEADS
    NODE = 14
    assert 2 * NP <= 1 << NODE
    LAST = N - (T - 1) * P
    H2 = D // 2
    Q = D // P

    ctx = ExitStack()
    with ctx:
        def sb(name, shape, dt=F32):
            return ctx.enter_context(nc.sbuf_tensor(name, shape, dt))

        sems = {}

        def sem(name):
            if name not in sems:
                sems[name] = ctx.enter_context(nc.semaphore(name))
            return sems[name]

        def dram(name, shape, dt=F32):
            return nc.dram_tensor(name, shape, dt).ap()

        BY_DST, BY_SRC = 0, 1
        recs = [dram("recs_by_dst", (C, P), I32), dram("recs_by_src", (C, P), I32)]
        tile_row_dram = dram("tile_row_dram", (2, SB, P), I16)
        SPARE = T
        tables = [dram(f"table{n}", (NP + P, D)) for n in range(2)]
        gat_table = dram("gat_table", (NP, GW))
        rel_table = dram("rel_table", (2 * NP, D))
        res = dram("res", (NP, D))
        res_end = dram("res_end", (NP, D))

        def tiled(ap):
            return ap.rearrange("(t p) c -> p t c", p=P)

        acc = sb("acc", [P, T + 1, GW])
        own = sb("own", [P, T + 2, D])
        idx_by_src = sb("idx_by_src", [P, SB * P], I16)
        idx_rel = sb("idx_rel", [P, SB * P], I16)
        idx_by_dst = sb("idx_by_dst", [P, SB * P], I16)
        node_loc = sb("node_loc", [P, 2, SB * P], BF16)
        HB = 8
        READ, WRITE, ROWS, WROTE = HALF, HALF + 1, HALF + 2, HB + HALF
        turn_row = sb("turn_row", [1, 2, TURNS * 2 * HB], I16)
        left_row = sb("left_row", [1, 2, 4 * T], I16)
        ring = sb("ring", [P, U, GW])
        idx_slot = sb("idx_slot", [P, 2 * U], I32)
        onehot = sb("onehot", [P, 2 * U, P])
        onehot_t = sb("onehot_t", [P, HALF, P])
        hbuf = sb("hbuf", [P, B, D])
        hT = sb("hT", [P, B * Q, P])
        tbuf = sb("tbuf", [P, B, GW])
        xb = sb("xb", [P, B, D])
        rb = sb("rb", [P, B, D])
        wbuf = sb("wbuf", [P, Q, 1152])
        gat_ring = [ring[:, 0:HALF, :], ring[:, HALF:U, :], tbuf[:, 0:HALF, :],
                    hbuf[:, :, :].rearrange("p j d -> p (j d)")[:, 0:HALF * GW].rearrange("p (u c) -> p u c", c=GW)]
        pbuf = sb("pbuf", [P, 1536])
        iota_row = sb("iota_row", [P, P])
        ident = sb("ident", [P, P])
        ones = sb("ones", [P, P])
        ones_last = sb("ones_last", [P, P])
        part = sb("part", [P, 1])
        rdeg = sb("rdeg", [P, T + 1])
        deg = sb("deg", [P, 2])
        st = sb("st", [P, B, 6])
        mv = sb("mv", [P, B, 2])
        sd = sb("sd", [P, B])
        rstd = sb("rstd", [P, B])
        nmr = sb("nmr", [P, B])
        a_own = sb("a_own", [P, T, HEADS])
        dst_tab = sb("dst_tab", [P, T, 2 * HEADS])
        w_self = sb("w_self", [P, T, HEADS])
        zlog = sb("zlog", [P, HALF, HEADS])
        zlog2 = sb("zlog2", [P, HALF, HEADS])
        z_under = sb("z_under", [P, HALF, HEADS])
        amax = sb("amax", [P, HEADS])
        gdiag = sb("gdiag", [HEADS, HEADS])
        gmax = sb("gmax", [HEADS, 1])
        gmax_b = sb("gmax_b", [P, HEADS])
        den = sb("den", [P, B, HEADS])
        bn_a = sb("bn_a", [P, D])
        bn_b = sb("bn_b", [P, D])
        bn_mean = sb("bn_mean", [P, D])
        carrier = sb("carrier", [P, 64])
        act_carrier = sb("act_carrier", [P, 64])
        acc_flat = acc[:, :, :].rearrange("p t c -> p (t c)")
        at = [0]

        def place(n, dt=F32):
            words = n if dt in (F32, I32) else -(-n // 2)
            ap = acc_flat[:, at[0]:at[0] + words]
            at[0] += words
            assert at[0] <= (T + 1) * GW
            return ap if dt == F32 else ap.bitcast(dt)[:, 0:n]

        edges = place(3 * C, I32).rearrange("p (a c) -> p a c", a=3)
        rec_sb = [place(C, I32), place(C, I32)]
        key_tile = place(C, BF16)
        is_tile = place(C, I16)
        running = place(C)
        all_ones = place(C)
        position = place(C)
        pos_i = place(C, I32)
        counts, totals, ends, starts = (place(T) for _ in range(4))
        SLOTS = 17
        SORT_TURNS = C // (2 * SLOTS)
        assert SORT_TURNS * 2 * SLOTS == C
        pos_slot = place(2 * SLOTS, I32)
        rec_slot = place(2 * SLOTS, I32)
        bounds = place(C)
        junk = place(C)
        edge_rows = place(SB * P, I32).rearrange("p (s e) -> p s e", s=SB)
        edge_i = onehot[:, 0:SB, :].bitcast(I32)
        edge_f = rb[:, 0:SB, :].rearrange("p j (a e) -> p a j e", a=2)
        last_rec, last_tile = (edges[0:1, a, :] for a in range(2))
        bound_row = edges[0:1, 2, :].bitcast(F32)
        chunk_row = place(C)[0:1, :]
        step_no, chunk_f, chunk_c, tile_f, tile_base = (place(SB) for _ in range(5))
        chunk_i = place(SB, I32)
        tile_i = place(SB, I16)
        tile_row = place(SB * P, I16)[0:1, :]
        come, done, tiles_read, tiles_same = (place(TURNS + T + 1)[0:1, :] for _ in range(4))
        zrows = xb[:, 0, :]
        before = hbuf[:, 0, 0:P]

        psum = ctx.enter_context(nc.psum_tensor("psum", [P, 8, 512], F32))
        psT = psum[:, 0:4, :].rearrange("p b (f c) -> p (b f) c", c=P)
        BANKS = 4
        BANK_T, BANK_P = 5, 6
        GB = HALF
        ps_oh = psum[:, 5:7, :].rearrange("p b (f c) -> p (b f) c", c=P)
        ps_log = psum[:, 7, 0:HALF * 2 * HEADS].rearrange("p (u h) -> p u h", u=HALF)

        LOADS = {
            "in": ([("W_in", io["L0_gnn_W_in"]), ("agg", io["L0_gnn_W_agg"][0]), ("self", io["L0_gnn_W_self"][0])],
                   [("b_in", io["L0_gnn_b_in"]), ("b_hid", io["L0_gnn_b_hid"][0])]),
            "l0": ([("agg", io["L0_gnn_W_agg"][1]), ("self", io["L0_gnn_W_self"][1])], [("b_hid", io["L0_gnn_b_hid"][1])]),
            "l1": ([("agg", io["L0_gnn_W_agg"][2]), ("self", io["L0_gnn_W_self"][2])], [("b_hid", io["L0_gnn_b_hid"][2])]),
            "l2": ([("W_out", io["L0_gnn_W_out"]), ("W_gat", io["L1_gnn_W"])],
                   [("b_out", io["L0_gnn_b_out"]), ("att_src", io["L1_gnn_att_src"].rearrange("h d -> (h d)")),
                    ("att_dst", io["L1_gnn_att_dst"].rearrange("h d -> (h d)"))]),
            "ga": ([("W0", io["L2_gnn_W0"])],
                   [("bias", io["L1_gnn_bias"]), ("gamma", io["L1_gnn_gamma"]), ("beta", io["L1_gnn_beta"]), ("b_next", io["L2_gnn_b0"])]),
            "s0": ([("W1", io["L2_gnn_W1"])],
                   [("b_next", io["L2_gnn_b1"]), ("g", io["L2_gnn_g0"]), ("beta", io["L2_gnn_beta0"])]),
            "s1": ([("R0", io["L3_gnn_W_rel"][0]), ("R1", io["L3_gnn_W_rel"][1])],
                   [("g", io["L2_gnn_g1"]), ("beta", io["L2_gnn_beta1"]),
                    ("b0", io["L3_gnn_b_rel"][0]), ("b1", io["L3_gnn_b_rel"][1])]),
            "fi": ([("ih", io["L3_gnn_W_ih"])],
                   [("b3", io["L3_gnn_b3"])]),
        }
        W, R, NLOADS = {}, {}, {}
        for ph, (ws, rs) in LOADS.items():
            at = 0
            for name, ap in ws:
                W[ph, name] = at
                at += ap.shape[1]
            at = 0
            for name, ap in rs:
                R[ph, name] = at
                at += ap.shape[0]
            NLOADS[ph] = len(ws) + len(rs)
        W1_AT = 4 * D
        w2 = onehot_t[:, 0, :]
        w3 = tbuf[:, 3, 0:D]
        bias_at = [D + n for n in (0, 4 * Q, 8 * Q, 8 * Q + 1)]
        b_ih, b_hh, b_1, b_2 = (pbuf[:, a:a + n] for a, n in zip(bias_at, (4 * Q, 4 * Q, 1, 1)))
        NLOADS["fi"] += 7
        fi_sums, fi_state, fi_1, fi_2 = hbuf[:, 0, :], hbuf[:, 1, :], hbuf[:, 2, 0:P], hbuf[:, 3, 0:P]
        fi_i, fi_g, fi_o, fi_cell, fi_3 = (xb[:, n, :] for n in range(5))
        b_rel = pbuf[:, 4 * D:4 * D + 2 * Q]
        NLOADS["s1"] += 2
        MSG_BANKS = {"u0": BANK_P, "u1": 7, "v0": BANK_T, "v1": BANK_P}
        msg_u = [hT[:, (1 + r) * Q:(2 + r) * Q, :] for r in range(2)]
        def row(ph, name, n=D):
            return pbuf[:, R[ph, name]:R[ph, name] + n]

        def over_batch(ap):
            return ap.unsqueeze(1).broadcast_to([P, B, ap.shape[1]])

        def heads(ap):
            return ap.rearrange("p (h d) -> p h d", h=HEADS)

        block = ctx.enter_context(nc.Block())
        PASSES = ["in", "l0", "l1", "l2", "ga", "s0", "s1"]
        SLOT_PHASES = ["l0", "l1", "s0", "s1", "fi"]
        STORES = [0 if ph in SLOT_PHASES else K for ph in PASSES]
        STORED = {ph: 1 + sum(STORES[:g]) for g, ph in enumerate(PASSES)}
        ALL_STORED = {ph: STORED[ph] + n for ph, n in zip(PASSES, STORES)}
        ACC_READ = {ph: (ph + "_pre", T) for ph in PASSES if ph not in SLOT_PHASES} | {"ga": ("ga_x2", T)}
        ZEROED = [g for g, ph in enumerate(PASSES) if ph not in SLOT_PHASES]
        TABLE_OF = [tables[n] for n in (0, 1, 0, 0, 0, 1, 0)]
        TRANSPOSED = {"in": ["in_u", "in_tab"], "l2": ["l2_u", "l2_tab"],
                      "ga": ["ga_tab"]}
        PRODUCTS = TRANSPOSED
        TABLES = {ph: [ph + "_tab"] for ph in PASSES if ph not in SLOT_PHASES}
        NORMS = {"in": ["in"], "l2": ["l2"], "ga": ["ga"]}
        LN_BIASED = {"in": ["in"], "l2": ["l2"], "ga": ["ga"]}

        PRODUCT_UNITS = [u for names in PRODUCTS.values() for u in names]

        FREE = BANKS - 1

        def count(units, k, unit, items=1, j=None):
            before = 0
            for names in units.values():
                if unit in names:
                    at = before * K + names.index(unit)
                    return k * (len(names) * items) + (at * items + (items if j is None else j + 1))
                before += len(names)

        ORDER = [BY_DST if ph in ("l2", "s1") else BY_SRC for ph in PASSES]
        GAT = PASSES.index("l2")
        HALVES, FIRST, FINAL = STEPS // HALF, 2, 4
        GAT_TURNS = (HALVES - FIRST - FINAL) // 4
        assert FIRST + 4 * GAT_TURNS + FINAL == HALVES
        ONEHOTS = [g * (STEPS + HALF) - (HALF if g > GAT else 0) for g in range(len(PASSES))]

        def filled(g, h):
            n = -(-(HALVES - h) // 4)
            return (TURNS * (g - (g > GAT)) if h < 2 else 0) + (n if g > GAT else 0)

        def slot_sem(r, u):
            return sem(f"gathered{r * HALF + u}") if r < 2 else sem(f"gathered_half{r}")

        def by_halves(eng, half, tiles=None):
            def run(n0, count, at):
                got = tiles(n0, count) if tiles else None
                for m in range(count):
                    n = n0 + m
                    half(n, (at + m) % 4, *([got[m]] if tiles else []))

            run(0, FIRST, 0)
            with eng.Fori(0, GAT_TURNS) as i:
                run(i * 4 + FIRST, 4, FIRST)
            run(HALVES - FINAL, FINAL, HALVES - FINAL)


        TAIL = 3
        BY_TURNS = T - TAIL
        NS = TURNS + BY_TURNS + TAIL
        SLOT_T = {"l0": ["tab"], "l1": ["tab"], "s0": ["tab"], "s1": ["h"], "fi": ["i"]}
        SLOT_P = {"l0": ["tab"], "l1": ["tab"], "s0": ["tab"], "s1": ["u0", "u1", "v0", "v1"], "fi": ["ig", "o"]}
        SLOT_LN = {"s0": ["z"], "s1": ["z", "x"]}
        SLOT_AFFINE = {"s0": ["z"], "s1": ["z"]}

        def slot_count(units, ph, n, unit=None):
            names = units[ph] if units else [None]
            before = sum(len(units.get(p, [])) if units else 1 for p in SLOT_PHASES[:SLOT_PHASES.index(ph)]) * NS
            return n * len(names) + (before + names.index(unit) + 1)

        LAYERS = ["1", "2", "3"]
        BANK_LAYERS = 7

        def layer_count(n, unit):
            return n * len(LAYERS) + (LAYERS.index(unit) + 1)

        def slot_done(name, ph, n):
            return n + 1 if name.startswith(ph + "_") else slot_count(None, ph, n)

        def more_slots(eng, reg, o, slot, skip, regs=None, first=0):
            eng.load([reg], left_row[0:1, o, 4 * T - 1:4 * T])
            with eng.If(eng.snap(reg) < BY_TURNS):
                with eng.Fori(0, BY_TURNS) as m:
                    if regs:
                        eng.load(regs, left_row[0:1, o, bass.ds(m * 4 + first, len(regs))])
                    slot(m + TURNS, *([eng.snap(r, min_val=0, max_val=BY_TURNS if first else SPARE + n) for n, r in enumerate(regs)] if regs else [None, None]))
            with eng.Else():
                skip()
            for j in range(TAIL):
                slot(TURNS + BY_TURNS + j, BY_TURNS + j, BY_TURNS + j)

        def both(*fs):
            def f(*args):
                for g in fs:
                    g(*args)
            return f

        def batches(eng, step):
            with eng.Fori(0, K - 1) as k:
                step(k, True)
            step(K - 1, False)

        @block.sync
        def _(sp):
            def load_params(ph):
                ws, rs = LOADS[ph]
                done = sem(ph + "_params")
                for name, ap in ws:
                    n = ap.shape[1]
                    sp.dma_start(wbuf[:, :, W[ph, name]:W[ph, name] + n], ap.rearrange("(q p) n -> p q n", p=P)).then_inc(done, 16)
                for name, ap in rs:
                    n = ap.shape[0]
                    sp.dma_start(pbuf[:, R[ph, name]:R[ph, name] + n],
                                 ap.unsqueeze(0).broadcast_to([P, n])).then_inc(done, 16)

            def rows(ap, k):
                return tiled(ap)[:, bass.ds(k * B, B), :]

            sp.dma_start(res[0:N, :], io["x"]).then_inc(sem("x_copied"), 16)
            sp.wait_ge(sem("pads_set"), 1)
            for n, a in enumerate((io["src"], io["dst"], io["edge_type_2"])):
                whole = E // C
                most = whole // 16 * 16
                for p, q in ((0, most), (most, whole)):
                    sp.dma_start(edges[p:q, n, :], a[p * C:q * C].rearrange("(p c) -> p c", c=C)).then_inc(sem("edges"), 16)
                sp.dma_start(edges[whole:whole + 1, n, 0:E - whole * C], a[whole * C:E].unsqueeze(0)).then_inc(sem("edges"), 16)
            sp.dma_start(res[N:NP, :], zrows[0:NP - N, :]).then_inc(sem("stored"), 16)
            load_params("in")
            sp.wait_ge(sem("rec_by_dst"), 1)
            sp.dma_start(recs[BY_DST].rearrange("c e -> (c e)").rearrange("(p c) -> p c", c=C), rec_sb[BY_DST]).then_inc(sem("rec_stored"), 16)
            sp.wait_ge(sem("rec_stored"), 16)

            def chunk_ends(o):
                sp.dma_start(last_rec, recs[o][:, P - 1:P].rearrange("c o -> o c"), allow_slow_non_contiguous=True).then_inc(sem("last_rec"), 16)

            def step_tiles(o):
                sp.wait_ge(sem("tile_i"), o + 1)
                for s in range(SB):
                    sp.dma_start(tile_row_dram[o, s:s + 1, :].rearrange("o p -> p o"), tile_i[:, s:s + 1]).then_inc(sem("tile_out"), 16)
                sp.wait_ge(sem("tile_out"), 16 * SB * (o + 1))
                sp.dma_start(tile_row, tile_row_dram[o].rearrange("s p -> (s p)").unsqueeze(0)).then_inc(sem("tile_row"), 16)

            chunk_ends(BY_DST)
            sp.wait_ge(sem("x_copied"), 16)
            sp.wait_ge(sem("stored"), 16)
            sp.dma_start(xb[:], rows(res, 0)).then_inc(sem("in_x"), 16)
            step_tiles(BY_DST)

            def first(k, more):
                if more:
                    sp.wait_ge(sem("in_h"), k * B + B)
                    sp.dma_start(xb[:], rows(res, k + 1)).then_inc(sem("in_x"), 16)
                sp.wait_ge(sem("taken_act"), count(TABLES, k, "in_tab", B))
                sp.dma_start(rows(tables[0], k), tbuf[:, :, 0:D]).then_inc(sem("stored"), 16)

            def settled(ph):
                if ph in SLOT_PHASES:
                    sp.wait_ge(sem("slot_taken"), 1 + slot_count(SLOT_P, ph, NS - 1, SLOT_P[ph][-1]))
                    return
                sp.wait_ge(sem("stored"), 16 * ALL_STORED[ph])
                if ph != "s1":
                    sp.wait_ge(sem("taken_dve"), FREE + count(PRODUCTS, K - 1, ph + "_tab", B))

            slot_regs = [sp.alloc_register(f"sp_slot{n}") for n in range(2)]

            def slots_out(ph):
                g, s = PASSES.index(ph) - 1, SLOT_PHASES.index(ph)

                def out(n, tile, stored, at):
                    sp.wait_ge(sem("slot_rows"), slot_count(None, ph, n))
                    sp.dma_start(tiled(TABLE_OF[g + 1])[:, bass.ds(tile, 1), :], tbuf[:, 0:1, 0:D]).then_inc(sem(stored), 16)
                    sp.wait_ge(sem(stored), at)
                    sp.sem_inc(sem("slot_out"), 1)

                sp.wait_ge(sem("turn_row"), ORDER[g] + 1)
                with sp.Fori(0, TURNS) as i:
                    sp.load(slot_regs[0:1], turn_row[0:1, ORDER[g], bass.ds(i * (2 * HB) + READ, 1)])
                    out(i, sp.snap(slot_regs[0], min_val=0, max_val=SPARE), "slot_stored", i * 16 + 16 * ((TURNS + TAIL) * s + 1))

                def slot(n, tile, _):
                    if isinstance(n, int):
                        out(n, tile, "slot_stored", 16 * ((TURNS + TAIL) * s + n - BY_TURNS + 1))
                    else:
                        out(n, tile, "left_stored", n * 16 + 16 * (BY_TURNS * s + 1 - TURNS))

                more_slots(sp, slot_regs[0], ORDER[g], slot, lambda: sp.sem_inc(sem("slot_out"), BY_TURNS), slot_regs)

            batches(sp, first)
            for h in range(2):
                sp.wait_ge(sem(f"scattered{h}"), 16 * SLOTS * SORT_TURNS)
            chunk_ends(BY_SRC)
            step_tiles(BY_SRC)
            for prev, ph in (("in", "l0"), ("l0", "l1")):
                settled(prev)
                load_params(ph)
                slots_out(ph)

            def l2(k, more):
                sp.wait_ge(sem("l2_res"), k + 1)
                sp.dma_start(rows(res, k), rb[:]).then_inc(sem("l2_rstored"), 16)
                if more:
                    sp.wait_ge(sem("l2_rstored"), k * 16 + 16)
                    sp.dma_start(rb[:], rows(res, k + 1)).then_inc(sem("l2_r"), 16)
                sp.wait_ge(sem("taken_act"), count(TABLES, k, "l2_tab", B))
                sp.dma_start(rows(gat_table, k), tbuf[:]).then_inc(sem("stored"), 16)

            settled("l1")
            load_params("l2")
            sp.dma_start(rb[:], rows(res, 0)).then_inc(sem("l2_r"), 16)
            batches(sp, l2)

            def ga_own(k, more):
                if more:
                    sp.wait_ge(sem("ga_own"), k * 4 + 1)
                    sp.dma_start(tbuf[:], rows(gat_table, k + 1)).then_inc(sem("ga_xh"), 16)

            def ga(k, more):
                sp.wait_ge(sem("ga_x2"), k * B + B)
                sp.dma_start(rows(res, k), xb[:]).then_inc(sem("ga_rstored"), 16)
                if more:
                    sp.dma_start(rb[:], rows(res, k + 1)).then_inc(sem("ga_r"), 16)
                sp.wait_ge(sem("taken_act"), count(TABLES, k, "ga_tab", B))
                sp.dma_start(rows(tables[0], k), tbuf[:, :, 0:D]).then_inc(sem("stored"), 16)

            settled("l2")
            sp.wait_ge(sem("l2_rstored"), 16 * K)
            load_params("ga")
            sp.wait_ge(sem("mm"), U + STEPS * (GAT + 1))
            sp.dma_start(tbuf[:], rows(gat_table, 0)).then_inc(sem("ga_xh"), 16)
            sp.dma_start(rb[:], rows(res, 0)).then_inc(sem("ga_r"), 16)
            batches(sp, ga_own)
            batches(sp, ga)
            settled("ga")
            load_params("s0")
            slots_out("s0")

            settled("s0")
            load_params("s1")
            for r in range(2):
                sp.dma_start(b_rel[:, r * Q:(r + 1) * Q], io["L3_gnn_b_rel"][r].rearrange("(q p) -> p q", p=P),
                             allow_slow_non_contiguous=True).then_inc(sem("s1_params"), 16)
            sp.wait_ge(sem("ga_rstored"), 16 * K)
            g = PASSES.index("s1") - 1

            def residual(n, tile, where, at):
                sp.dma_start(rb[:, 0:1, :], tiled(res)[:, bass.ds(tile, 1), :]).then_inc(sem(where + "_res"), 16)
                sp.wait_ge(sem(where + "_res"), at)
                sp.sem_inc(sem("s1_res"), 1)
                sp.wait_ge(sem("s1_x3"), n + 1)
                sp.dma_start(tiled(res_end)[:, bass.ds(tile, 1), :], xb[:, 1:2, :]).then_inc(sem(where + "_x3"), 16)
                sp.wait_ge(sem(where + "_x3"), at)
                sp.sem_inc(sem("s1_xout"), 1)

            def messages(n, tile, where, at):
                sp.wait_ge(sem("slot_taken"), 1 + slot_count(SLOT_P, "s1", n, "v1"))
                for r in range(2):
                    rows_r = rel_table[r * NP:(r + 1) * NP, :]
                    sp.dma_start(tiled(rows_r)[:, bass.ds(tile, 1), :], tbuf[:, r:r + 1, 0:D]).then_inc(sem(where + "_rel"), 16)
                sp.wait_ge(sem(where + "_rel"), at * 2)
                sp.sem_inc(sem("slot_out"), 1)

            def slot_tile(reg, i):
                sp.load(slot_regs[reg:reg + 1], turn_row[0:1, ORDER[g], bass.ds(i * (2 * HB) + ROWS, 1)])
                return sp.snap(slot_regs[reg], min_val=0, max_val=BY_TURNS)

            for n in range(2):
                residual(n, slot_tile(0, n), "s1_turns", n * 16 + 16)
            with sp.Fori(2, TURNS) as i:
                residual(i, slot_tile(0, i), "s1_turns", i * 16 + 16)
                messages(i - 2, slot_tile(1, i - 2), "s1_turns", i * 16 - 16)
            for n in (TURNS - 2, TURNS - 1):
                messages(n, slot_tile(1, n), "s1_turns", n * 16 + 16)

            def left_messages(n, tile, *_):
                for f in (residual, messages):
                    if isinstance(n, int):
                        f(n, tile, "s1_turns", 16 * (n - BY_TURNS + 1))
                    else:
                        f(n, tile, "s1_left", n * 16 + 16 * (1 - TURNS))

            def no_messages():
                for name in ("s1_res", "s1_xout", "slot_out"):
                    sp.sem_inc(sem(name), BY_TURNS)

            more_slots(sp, slot_regs[0], ORDER[g], left_messages, no_messages, slot_regs[0:1], 2)
            settled("s1")
            load_params("fi")
            done = sem("fi_params")
            sp.dma_start(wbuf[:, :, W1_AT:W1_AT + H2], io["L3_gnn_W1"].rearrange("(q p) n -> p q n", p=P)).then_inc(done, 16)
            sp.dma_start(w2, io["L3_gnn_W2"]).then_inc(done, 16)
            sp.dma_start(w3, io["L3_gnn_W3"]).then_inc(done, 16)
            for to, of in ((b_ih, io["L3_gnn_b_ih"]), (b_hh, io["L3_gnn_b_hh"]), (b_1, io["L3_gnn_b1"]), (b_2, io["L3_gnn_b2"])):
                sp.dma_start(to, of.rearrange("(a p) -> p a", p=P), allow_slow_non_contiguous=True).then_inc(done, 16)

            out_t = out[0:(T - 1) * P, :].rearrange("(t p) c -> p t c", p=P)
            g = len(PASSES) - 1

            def result(n, tile, where, at):
                sp.dma_start(rb[:, 1:2, :], tiled(res_end)[:, bass.ds(tile, 1), :]).then_inc(sem(where + "_res"), 16)
                sp.wait_ge(sem(where + "_res"), at)
                sp.sem_inc(sem("slot_res"), 1)
                sp.wait_ge(sem("fi_y"), slot_done("fi_y", "fi", n))
                if isinstance(tile, int) and tile == T - 1:
                    sp.dma_start(out[(T - 1) * P:N, :], tbuf[0:LAST, 0, 0:D]).then_inc(sem(where + "_out"), 16)
                else:
                    sp.dma_start(out_t[:, bass.ds(tile, 1), :], tbuf[:, 0:1, 0:D]).then_inc(sem(where + "_out"), 16)
                sp.wait_ge(sem(where + "_out"), at)
                sp.sem_inc(sem("slot_out"), 1)

            with sp.Fori(0, TURNS) as i:
                sp.load(slot_regs[0:1], turn_row[0:1, ORDER[g], bass.ds(i * (2 * HB) + ROWS, 1)])
                result(i, sp.snap(slot_regs[0], min_val=0, max_val=BY_TURNS), "turns", i * 16 + 16)

            def left_result(n, tile, *_):
                if isinstance(n, int):
                    result(n, tile, "turns", 16 * (n - BY_TURNS + 1))
                else:
                    result(n, tile, "left", n * 16 + 16 * (1 - TURNS))

            def no_results():
                for name in ("slot_res", "slot_out"):
                    sp.sem_inc(sem(name), BY_TURNS)

            more_slots(sp, slot_regs[0], ORDER[g], left_result, no_results, slot_regs[0:1], 2)

        @block.gpsimd
        def _(pool):
            halves = [pool.alloc_register(f"halves{r}") for r in range(4)]
            sorts = [pool.alloc_register(f"sorts{h}") for h in range(2)]
            for r in halves + sorts:
                pool.reg_mov(r, 0)
            exact = dict(allow_small_or_imprecise_dtypes=True)
            nc.gpsimd.iota(iota_row[:], [[1, P]], base=0, channel_multiplier=0, **exact).then_inc(sem("iota"), 1)
            nc.gpsimd.iota(part[:], [[0, 1]], base=0, channel_multiplier=1, **exact).then_inc(sem("iota"), 1)
            nc.gpsimd.iota(step_no, [[P, SB]], base=0, channel_multiplier=1, **exact).then_inc(sem("iota"), 1)
            nc.gpsimd.iota(chunk_row, [[1, C]], base=1, channel_multiplier=0, **exact).then_inc(sem("iota"), 1)

            def step_edges(o):
                pool.wait_ge(sem("chunk_i"), o + 1)
                for s in range(SB):
                    nc.gpsimd.indirect_dma_start(
                        out=edge_rows[:, s, :], out_offset=None, in_=recs[o],
                        in_offset=bass.IndirectOffsetOnAxis(ap=chunk_i[:, s:s + 1], axis=0)).then_inc(sem("edge_rows"), 16)

            step_edges(BY_DST)
            pool.wait_ge(sem("positions"), 1)
            scattered = recs[BY_SRC].rearrange("c e -> (c e)").unsqueeze(1)


            def scatter(i, first):
                for h in range(2):
                    half = slice(h * SLOTS, (h + 1) * SLOTS)
                    if not first:
                        pool.wait_ge(sem(f"scattered{h}"), i * (16 * SLOTS))
                    at_col = bass.ds(i * (2 * SLOTS) + h * SLOTS, SLOTS)
                    nc.gpsimd.tensor_copy(pos_slot[:, half], pos_i[:, at_col]).then_inc(sem("sort_slots"), 1)
                    nc.gpsimd.tensor_copy(rec_slot[:, half], rec_sb[BY_SRC][:, at_col]).then_inc(sem("sort_slots"), 1)
                    pool.wait_ge(sem("sort_slots"), i * 4 + (2 * h + 2))
                    pool.reg_add(sorts[h], sorts[h], 1)
                    for u in range(h * SLOTS, (h + 1) * SLOTS):
                        nc.gpsimd.indirect_dma_start(
                            out=scattered, out_offset=bass.IndirectOffsetOnAxis(ap=pos_slot[:, u:u + 1], axis=0),
                            in_=rec_slot[:, u:u + 1], in_offset=None).then_inc(sem(f"scattered{h}"), 16)

            scatter(0, True)
            with pool.Fori(1, SORT_TURNS) as i:
                scatter(i, False)
            step_edges(BY_SRC)
            for g, ph in enumerate(PASSES):
                if g == 0:
                    pool.wait_ge(sem("edge_T_read"), 4)
                    pool.wait_ge(sem("turn_row"), 2)
                elif g in ZEROED:
                    pool.wait_ge(sem(ACC_READ[ph][0]), ACC_READ[ph][1])
                if g in ZEROED:
                    nc.gpsimd.memset(acc[:], 0.0).then_inc(sem("acc_zero"), 1)
                if ph in SLOT_PHASES:
                    pool.wait_ge(sem("slot_out"), 1 + slot_count(None, ph, NS - 1))
                else:
                    pool.wait_ge(sem("stored"), 16 * ALL_STORED[ph])
                tab = {GAT: gat_table, len(PASSES) - 1: rel_table}.get(g, TABLE_OF[g][0:NP, :])

                def gather(n, r):
                    pool.wait_ge(sem("idx_ready"), n + (HALVES * g + 1))
                    if g != GAT:
                        pool.wait_ge(sem("mm"), n * HALF + (STEPS * g + HALF))
                    pool.reg_add(halves[r], halves[r], 1)
                    for u in range(HALF):
                        to = gat_ring[r][:, u, :] if g == GAT else ring[:, r % 2 * HALF + u, 0:D]
                        nc.gpsimd.indirect_dma_start(
                            out=to, out_offset=None, in_=tab,
                            in_offset=bass.IndirectOffsetOnAxis(ap=idx_slot[:, r * HALF + u:r * HALF + u + 1], axis=0)
                        ).then_inc(slot_sem(r, u) if g == GAT else sem(f"gathered{r % 2 * HALF + u}"), 16)

                by_halves(pool, gather)
            pool.wait_ge(sem("idx_ready"), sum((pool.snap(r) for r in halves[1:]), pool.snap(halves[0])))

            pool.wait_ge(sem("sort_slots"), pool.snap(sorts[0]) + pool.snap(sorts[1]))

        @block.tensor
        def _(pe):
            regs = [pe.alloc_register(f"pe_tile{u}") for u in range(4 * HB)]

            def unit(k, unit, w, n, ready):
                def transposed(j):
                    if ready in PRODUCT_UNITS:
                        pe.wait_ge(sem("taken_dve"), FREE + count(PRODUCTS, k, ready, B, j))
                    else:
                        pe.wait_ge(sem(ready), k * B + (j + 1))
                    pe.wait_ge(sem("acts_hT"), count(TRANSPOSED, k, unit, B, j))
                    for q in range(Q):
                        last = nc.tensor.transpose(psum[:, j % BANKS, q * P:(q + 1) * P], hbuf[:, j, q * P:(q + 1) * P], ident[:])
                    last.then_inc(sem("acts_T"), 1)

                def product(j):
                    pe.wait_ge(sem("acts_hT"), FREE + count(TRANSPOSED, k, unit, B, j))
                    pe.wait_ge(sem("taken_dve"), count(PRODUCTS, k, unit, B, j))
                    for q in range(Q):
                        last = nc.tensor.matmul(psum[:, 4 + j % BANKS, 0:n], hT[:, j * Q + q, :], w(q),
                                                start=(q == 0), stop=(q == Q - 1))
                    last.then_inc(sem("product"), 1)

                for j in range(B):
                    if j == 0:
                        transposed(0)
                    if j + 1 < B:
                        transposed(j + 1)
                    product(j)

            def cols(at, n):
                return lambda q: wbuf[:, q, at:at + n]

            def slot_T(ph, unit, ready, src, kt=Q):
                def f(n, *_):
                    pe.wait_ge(sem(ready), (1 if ready == "slot_h" else 0) + slot_done(ready, ph, n))
                    pe.wait_ge(sem("slot_hT"), slot_count(SLOT_T, ph, n, unit))
                    if len(SLOT_P[ph]) > 1:
                        pe.wait_ge(sem("slot_taken"), slot_count(SLOT_P, ph, n, SLOT_P[ph][0]))
                    for q in range(kt):
                        last = nc.tensor.transpose(psum[:, BANK_T, q * P:(q + 1) * P], src[:, q * P:(q + 1) * P], ident[:])
                    last.then_inc(sem("slot_T"), 1)
                return f

            def slot_P(ph, unit, w, cols_n):
                def f(n, *_):
                    pe.wait_ge(sem("slot_hT"), 1 + slot_count(SLOT_T, ph, n, unit))
                    pe.wait_ge(sem("slot_taken"), slot_count(SLOT_P, ph, n, unit))
                    for q in range(Q):
                        last = nc.tensor.matmul(psum[:, BANK_P, 0:cols_n], hT[:, q, :], w(q), start=(q == 0), stop=(q == Q - 1))
                    last.then_inc(sem("slot_P"), 1)
                return f

            def message_P(unit, block=0):
                r = int(unit[1])
                at = W["s1", f"R{r}"]

                def u(n, *_):
                    if block == 0:
                        pe.wait_ge(sem("slot_hT"), 1 + slot_count(SLOT_T, "s1", n, "h"))
                        pe.wait_ge(sem("slot_taken"), slot_count(SLOT_P, "s1", n, "u0"))
                    for q in range(Q):
                        last = nc.tensor.matmul(psum[:, MSG_BANKS[unit], block * P:(block + 1) * P],
                                                wbuf[:, q, at + block * P:at + (block + 1) * P], hT[:, q, :], start=(q == 0), stop=(q == Q - 1))
                    if block == Q - 1:
                        last.then_inc(sem("slot_P"), 1)

                def v(n, *_):
                    pe.wait_ge(sem("slot_taken"), slot_count(SLOT_P, "s1", n, unit) - 1)
                    to = psum[:, MSG_BANKS[unit], 0:D]
                    nc.tensor.matmul(to, ones[0:1, :], row("s1", f"b{r}")[0:1, :], start=True, stop=False)
                    for q in range(Q):
                        last = nc.tensor.matmul(to, msg_u[r][:, q, :], wbuf[:, q, at:at + D], start=False, stop=(q == Q - 1))
                    last.then_inc(sem("slot_P"), 1)

                return u if unit[0] == "u" else v

            def gates_P(bank, gates, block):
                def f(n, *_):
                    if block == 0:
                        pe.wait_ge(sem("slot_hT"), 1 + slot_count(SLOT_T, "fi", n, "i"))
                        pe.wait_ge(sem("slot_taken"), slot_count(SLOT_P, "fi", n, SLOT_P["fi"][0]))
                    at = gates[block // Q] * D + block % Q * P
                    for q in range(Q):
                        last = nc.tensor.matmul(psum[:, bank, block * P:(block + 1) * P], wbuf[:, q, at:at + P], hT[:, q, :],
                                                start=(q == 0), stop=(q == Q - 1))
                    if block == len(gates) * Q - 1:
                        last.then_inc(sem("slot_P"), 1)
                return f

            def layer_P(unit, pairs, cols_n):
                def f(n, *_):
                    if unit == "1":
                        pe.wait_ge(sem("fi_state"), n + 1)
                    pe.wait_ge(sem("layer_taken"), layer_count(n, unit))
                    for q, (a, b) in enumerate(pairs):
                        last = nc.tensor.matmul(psum[:, BANK_LAYERS, 0:cols_n], a, b, start=(q == 0), stop=(q == len(pairs) - 1))
                    last.then_inc(sem("layer_P"), 1)
                return f

            def edge_pass(g, w, ph=None, front={}, back={}, far={}):
                if ph:
                    pe.wait_ge(sem(ph + "_params"), 16 * NLOADS[ph])
                    pe.wait_ge(sem("turn_row"), ORDER[g] + 1)

                def turn(i, lag):
                    for u in range(U):
                        if u in front:
                            front[u](i)
                        if lag > 0 and u in back:
                            back[u](i - 1)
                        if lag > 1 and u in far:
                            far[u](i - 2)
                        pe.wait_ge(sem(f"gathered{u}"), i * 16 + 16 * (filled(g, u // HALF) + 1))
                        pe.wait_ge(sem("onehot"), i * U + (ONEHOTS[g] + u + 1))
                        pe.wait_ge(sem("summed"), i * U + (STEPS * g + u + 1))
                        nc.tensor.matmul(psum[:, u % GB, 0:w], onehot[:, u, :], ring[:, u, 0:w],
                                         start=True, stop=True).then_inc(sem("mm"), 1)

                lags = 2 if far else 1
                for i in range(lags):
                    turn(i, i)
                with pe.Fori(lags, TURNS) as i:
                    turn(i, lags)
                if ph:
                    for n, stage in ((TURNS - 1, back), (TURNS - 2, far), (TURNS - 1, far)):
                        for u in sorted(stage):
                            stage[u](n)

                    def skip():
                        names = [name for name, units in (("slot_T", SLOT_T), ("slot_P", SLOT_P)) for _ in units[ph]]
                        if ph == "fi":
                            pe.wait_ge(sem("layer_taken"), 1 + layer_count(TURNS - 1, LAYERS[-1]))
                            names += ["layer_P"] * len(LAYERS)
                        pe.wait_ge(sem("slot_taken"), 1 + slot_count(SLOT_P, ph, TURNS - 1, SLOT_P[ph][-1]))
                        for n, name in enumerate(names):
                            nc.tensor.matmul(psum[:, 7, 511 - n:512 - n], ident[:], ident[:, 0:1], start=True,
                                             stop=True).then_inc(sem(name), BY_TURNS)

                    def all_of(n, *tiles):
                        for stage in (front, back, far):
                            for u in sorted(stage):
                                stage[u](n)

                    more_slots(pe, regs[0], ORDER[g], all_of, skip)

            HC = C // 2

            def chunk_bounds(o):
                pe.wait_ge(sem("bound_row"), o + 1)
                for b in range(2):
                    last = nc.tensor.matmul(psum[:, b, 0:HC], ones[0:1, :], bound_row[:, b * HC:(b + 1) * HC], start=True, stop=True)
                last.then_inc(sem("bound_mm"), 1)

            def step_tables(o):
                for a in range(2):
                    pe.wait_ge(sem("edge_f"), 2 * o + a + 1)
                    if a > 0:
                        pe.wait_ge(sem("edge_T_read"), 2 * o + 1)
                    for s in range(SB):
                        last = nc.tensor.transpose(psT[:, s, :], edge_f[:, a, s, :], ident[:])
                    last.then_inc(sem("edge_T"), 1)
                pe.wait_ge(sem("edge_T_read"), 2 * o + 2)

            pe.wait_ge(sem("consts"), 1)
            chunk_bounds(BY_DST)
            pe.wait_ge(sem("counts"), T)
            nc.tensor.matmul(psum[:, 2, 0:T], before, counts, start=True, stop=True)
            nc.tensor.matmul(psum[:, 3, 0:T], ones[:], counts, start=True, stop=True).then_inc(sem("count_mm"), 1)
            step_tables(BY_DST)
            pe.wait_ge(sem("in_params"), 16 * NLOADS["in"])
            with pe.Fori(0, K) as k:
                unit(k, "in_u", cols(W["in", "W_in"], D), D, "in_h")
                unit(k, "in_tab", cols(W["in", "agg"], 2 * D), 2 * D, "in_u")
            chunk_bounds(BY_SRC)
            step_tables(BY_SRC)
            for g, (w, ph) in enumerate(((D + 1, "l0"), (D, "l1"))):
                edge_pass(g, w, ph, {}, {1: slot_T(ph, "tab", "slot_h", hbuf[:, 0, :]),
                                         3: slot_P(ph, "tab", cols(W[ph, "agg"], 2 * D), 2 * D)})
            edge_pass(2, D)
            pe.wait_ge(sem("l2_params"), 16 * NLOADS["l2"])
            pe.wait_ge(sem("w_att"), 2 * Q)
            with pe.Fori(0, K) as k:
                unit(k, "l2_u", cols(W["l2", "W_out"], D), D, "l2_h")
                unit(k, "l2_tab", cols(W["l2", "W_gat"], GW + HEADS), GW + HEADS, "l2_ln_h")
            pe.wait_ge(sem("amax"), 1)
            nc.tensor.transpose(psum[0:HEADS, 0, 0:P], amax[:], ident[:]).then_inc(sem("amax_T"), 1)
            pe.wait_ge(sem("gdiag"), 1)
            nc.tensor.matmul(psum[:, 1, 0:HEADS], ones[0:HEADS, :], gdiag[:], start=True, stop=True).then_inc(sem("gmax_mm"), 1)
            g = GAT
            pe.wait_ge(sem("dst_tab"), 1)

            def onehots_T(n, r):
                pe.wait_ge(sem("onehot"), n * HALF + (ONEHOTS[g] + HALF))
                for v in range(HALF):
                    last = nc.tensor.transpose(ps_oh[:, v, :], onehot[:, r * HALF + v, :], ident[:])
                last.then_inc(sem("oh_T"), 1)

            def step_tiles(n, count):
                nc.tensor.load(regs[0:count * HB], turn_row[0:1, BY_DST, bass.ds(n * HB, count * HB)])
                return [regs[m * HB:m * HB + HALF] for m in range(count)]

            def logits(n, tiles):
                pe.wait_ge(sem("oh_t"), n + 1)
                if isinstance(n, int) and n == 0:
                    pass
                else:
                    pe.wait_ge(sem("z_less"), n)
                for v in range(HALF):
                    last = nc.tensor.matmul(ps_log[:, v, :], onehot_t[:, v, :],
                                            dst_tab[:, bass.ds(nc.tensor.snap(tiles[v], min_val=0, max_val=T - 1), 1), :].rearrange("p t h -> p (t h)"),
                                            start=True, stop=True)
                last.then_inc(sem("log_mm"), 1)

            def gat_half(n, r, tiles):
                ahead = not isinstance(n, int) or n + 2 < HALVES
                if ahead:
                    onehots_T(n + 2, (r + 2) % 4)
                for v in range(HALF):
                    pe.wait_ge(sem("msg"), n * HALF + (v + 1))
                    pe.wait_ge(sem("summed"), n * HALF + (STEPS * g + v + 1))
                    nc.tensor.matmul(psum[:, v, 0:GW], onehot[:, r * HALF + v, :], gat_ring[r][:, v, :],
                                     start=True, stop=True).then_inc(sem("mm"), 1)
                if ahead:
                    logits(n + 2, tiles)

            for n in range(2):
                onehots_T(n, n)
                logits(n, step_tiles(n, 1)[0])
            by_halves(pe, gat_half, lambda n, count: step_tiles(n + 2, count) if not isinstance(n, int) or n + 2 + count <= HALVES else
                       step_tiles(n + 2, count - 2) + [None] * 2)
            for bank, (name, items, at) in enumerate((("bs", 1, lambda t, j: acc[:, bass.ds(t, 1), 0:D].rearrange("p t c -> p (t c)")),
                                                      ("bv", B, lambda t, j: hbuf[:, j, :]))):
                def sums(k):
                    for j in range(B):
                        pe.wait_ge(sem(name + "_rows"), k * items + (j + 1 if items > 1 else 1))
                        first, final = (isinstance(k, int) and k == m and j == n for m, n in ((0, 0), (K - 1, B - 1)))
                        nc.tensor.matmul(psum[:, bank, 0:D], (ones_last if final else ones)[:], at(k * B + j, j),
                                         start=first, stop=final).then_inc(sem(name + "_mm"), 1)
                sums(0)
                with pe.Fori(1, K - 1) as k:
                    sums(k)
                sums(K - 1)
            pe.wait_ge(sem("ga_params"), 16 * NLOADS["ga"])
            with pe.Fori(0, K) as k:
                unit(k, "ga_tab", cols(W["ga", "W0"], D), D, "ga_ln_h")
            edge_pass(4, D, "s0", {}, {1: slot_T("s0", "tab", "slot_h", hbuf[:, 0, :]), 3: slot_P("s0", "tab", cols(W["s0", "W1"], D), D)})
            edge_pass(5, D, "s1", far={1: slot_T("s1", "h", "slot_h", hbuf[:, 0, :]), 3: message_P("u0", 0), 4: message_P("u0", 1),
                                       5: message_P("u1", 0), 6: message_P("u1", 1), 8: message_P("v0"), 9: message_P("v1")})
            edge_pass(6, D, "fi", {1: slot_T("fi", "i", "fi_sums", fi_sums)} | {3 + b: gates_P(BANK_P, (0, 2), b) for b in range(2 * Q)}
                      | {3 + 2 * Q + b: gates_P(BANK_T, (3,), b) for b in range(Q)},
                      {4: layer_P("1", [(wbuf[:, q, W1_AT:W1_AT + H2], fi_state[:, q * P:(q + 1) * P]) for q in range(Q)], P),
                       6: layer_P("2", [(w2, fi_1)], P), 8: layer_P("3", [(fi_2, w3)], D)})

        @block.scalar
        def _(act):
            def take_T(k, unit, kt=Q, table=None, n=D, also=None):
                def rows(j):
                    if j == 0:
                        act.wait_ge(sem("stored"), k * 16 + 16 * STORED[table])
                    act.wait_ge(sem("product"), count(PRODUCTS, k, unit, B, j))
                    nc.scalar.copy(tbuf[:, j, 0:n], psum[:, 4 + j % BANKS, 0:n]).then_inc(sem("taken_act"), 1)

                for j in range(B + 2):
                    if j < B:
                        act.wait_ge(sem("acts_T"), count(TRANSPOSED, k, unit, B, j))
                        nc.scalar.copy(hT[:, j * Q:j * Q + kt, :].rearrange("p q c -> p (q c)"),
                                       psum[:, j % BANKS, 0:kt * P]).then_inc(sem("acts_hT"), 1)
                    if table and 1 <= j <= B:
                        rows(j - 1)
                    if also and j >= 2:
                        also(j - 2)

            def take_tab(k, ph, n=D, also=None):
                take_T(k, ph + "_tab", Q, ph, n, also)

            def ln_relu(k, ph, done):
                act.wait_ge(sem("ln_ve"), count(NORMS, k, ph))
                nc.scalar.activation(sd[:], mv[:, :, 1], ACT.Sqrt).then_inc(sem("ln_sd"), 1)
                act.wait_ge(sem("ln_bias"), count(LN_BIASED, k, ph))
                for j in range(B):
                    nc.scalar.activation(hbuf[:, j, :], xb[:, j, :], ACT.Relu, bias=nmr[:, j:j + 1],
                                         scale=rstd[:, j:j + 1]).then_inc(sem(done), 1)

            def on_tiles(k, ready, to, of, func, done, n=D, tiles=range(B)):
                for j in tiles:
                    if ready in PRODUCT_UNITS:
                        act.wait_ge(sem("taken_dve"), FREE + count(PRODUCTS, k, ready, B, j))
                    else:
                        act.wait_ge(sem(ready), k * B + (j + 1))
                    nc.scalar.activation(to[:, j, 0:n], of[:, j, 0:n], func).then_inc(sem(done), 1)

            def put_indices(n, r, g, idx):
                static = isinstance(n, int) and n < 4
                act.wait_ge(sem("mm"), U + STEPS * g if static else n * HALF + (U + STEPS * g - 3 * HALF))
                nc.scalar.copy(idx_slot[:, r * HALF:(r + 1) * HALF], idx[:, bass.ds(n * HALF, HALF)]).then_inc(sem("idx_ready"), 1)

            def slot_take_T(ph, unit):
                def f(n, *_):
                    act.wait_ge(sem("slot_T"), slot_count(SLOT_T, ph, n, unit))
                    nc.scalar.copy(hT[:, 0:Q, :].rearrange("p q c -> p (q c)"), psum[:, BANK_T, 0:Q * P]).then_inc(sem("slot_hT"), 1)
                return f

            def slot_sqrt(ph, norm):
                j = SLOT_LN[ph].index(norm)

                def f(n, *_):
                    act.wait_ge(sem("slot_ve"), slot_count(SLOT_LN, ph, n, norm))
                    nc.scalar.activation(sd[:, j:j + 1], mv[:, j, 1:2], ACT.Sqrt).then_inc(sem("slot_sd"), 1)
                return f

            def slot_act(ph, ready, to, of, func, done):
                def f(n, *_):
                    act.wait_ge(sem(ready), slot_count(SLOT_AFFINE, ph, n, "z") if ready == "slot_n" else slot_done(ready, ph, n))
                    nc.scalar.activation(to, of, func).then_inc(sem(done), 1)
                return f

            def gates(unit, bank, kinds):
                def f(n, *_):
                    act.wait_ge(sem("slot_P"), slot_count(SLOT_P, "fi", n, unit))
                    for b, (gate, func, to) in enumerate(kinds):
                        for m in range(Q):
                            last = nc.scalar.activation(to[:, m * P:(m + 1) * P], psum[:, bank, (b * Q + m) * P:(b * Q + m + 1) * P], func,
                                                        bias=b_ih[:, gate * Q + m:gate * Q + m + 1])
                    last.then_inc(sem("slot_taken"), 1)
                return f

            def layer(unit, to, b):
                def f(n, *_):
                    act.wait_ge(sem("layer_P"), layer_count(n, unit))
                    nc.scalar.activation(to, psum[:, BANK_LAYERS, 0:P], ACT.Relu, bias=b).then_inc(sem("layer_taken"), 1)
                return f

            def slot_table(ph, unit, w=D):
                def f(n, *_):
                    act.wait_ge(sem("slot_out"), slot_count(None, ph, n))
                    act.wait_ge(sem("slot_P"), slot_count(SLOT_P, ph, n, unit))
                    nc.scalar.copy(tbuf[:, 0, 0:w], psum[:, BANK_P, 0:w]).then_inc(sem("slot_rows"), 1)
                return f

            left = act.alloc_register("act_left")
            columns = iter(range(64))

            def edge_pass(g, idx, ph=None, slot=([], []), sems=()):
                if ph:
                    act.wait_ge(sem("turn_row"), ORDER[g] + 1)
                for n in range(4):
                    put_indices(n, n, g, idx)

                def turn(i, at):
                    for h in range(2):
                        for behind, f in slot[h]:
                            if not isinstance(i, int) or i >= behind:
                                f(i - behind)
                        if not isinstance(i, int) or 2 * i + 4 + h < HALVES:
                            put_indices(i * 2 + (4 + h), at + h, g, idx)

                for i in range(2):
                    turn(i, i % 2 * 2)
                with act.Fori(1, TURNS // 2 - 1) as i:
                    turn(i * 2, 0)
                    turn(i * 2 + 1, 2)
                for i in range(TURNS // 2 * 2 - 2, TURNS):
                    turn(i, i % 2 * 2)
                if ph:
                    for i in range(TURNS, TURNS + 2):
                        for behind, f in slot[0] + slot[1]:
                            if i - behind < TURNS:
                                f(i - behind)

                    def skip():
                        if ph == "fi":
                            act.wait_ge(sem("layer_taken"), 1 + layer_count(TURNS - 1, LAYERS[-1]))
                        for name, times in sems:
                            at = next(columns)
                            nc.scalar.copy(act_carrier[:, at:at + 1], part[:]).then_inc(sem(name), BY_TURNS * times)

                    def all_of(n, *tiles):
                        for now in range(3):
                            for behind, f in slot[0] + slot[1]:
                                if behind == now:
                                    f(n)

                    more_slots(act, left, ORDER[g], all_of, skip)

            def step_tables(o):
                for a, to in enumerate((idx_by_src if o == BY_SRC else idx_rel, node_loc[:, o, :])):
                    act.wait_ge(sem("edge_T"), 2 * o + a + 1)
                    for f in range(0, SB, 4):
                        n = min(4, SB - f)
                        last = nc.scalar.copy(to[:, f * P:(f + n) * P], psT[:, f:f + n, :].rearrange("p f c -> p (f c)"))
                    last.then_inc(sem("edge_T_read"), 1)

            step_tables(BY_DST)
            with act.Fori(0, K) as k:
                ln_relu(k, "in", "in_h")
                take_T(k, "in_u")
                take_tab(k, "in")
            step_tables(BY_SRC)
            for g, ph in enumerate(("l0", "l1")):
                edge_pass(g, idx_by_src, ph, ([(1, slot_take_T(ph, "tab")), (0, slot_act(ph, "slot_pre", hbuf[:, 0, :], xb[:, 0, :], ACT.Relu, "slot_h")),
                                               (1, slot_table(ph, "tab"))], []),
                          (("slot_h", 1), ("slot_hT", 1), ("slot_rows", 1)))
            edge_pass(2, idx_by_src)
            relu = lambda k, tiles=range(B): on_tiles(k, "l2_pre", hbuf, xb, ACT.Relu, "l2_h", tiles=tiles)

            def l2(k, more):
                take_T(k, "l2_u")
                ln_relu(k, "l2", "l2_ln_h")
                take_tab(k, "l2", GW, (lambda j: relu(k + 1, [j])) if more else None)

            relu(0)
            batches(act, l2)
            g = GAT

            def take_onehots(n):
                act.wait_ge(sem("oh_T"), n + 1)
                nc.scalar.copy(onehot_t[:, 0:4, :], ps_oh[:, 0:4, :])
                nc.scalar.copy(onehot_t[:, 4:HALF, :], ps_oh[:, 4:HALF, :]).then_inc(sem("oh_t"), 1)

            def weights(n, r):
                act.wait_ge(sem("z_less"), n + 1)
                nc.scalar.activation(z_under[:], zlog[:], ACT.Relu, scale=-1.0).then_inc(sem("z_under"), 1)
                act.wait_ge(sem("z_under"), n + 1)
                nc.scalar.activation(gat_ring[r][:, :, D:GW], z_under[:], ACT.Exp, scale=-1.0).then_inc(sem("edge_w"), 1)

            def gat_half(n, r):
                for ahead, f in ((3, lambda: put_indices(n + 3, (r + 3) % 4, g, idx_by_dst)), (2, lambda: take_onehots(n + 2)),
                                 (1, lambda: weights(n + 1, (r + 1) % 4))):
                    if not isinstance(n, int) or n + ahead < HALVES:
                        f()

            for n in range(3):
                put_indices(n, n, g, idx_by_dst)
            for n in range(2):
                take_onehots(n)
            weights(0, 0)
            by_halves(act, gat_half)
            act.wait_ge(sem("zs_clamped"), 1)
            nc.scalar.activation(w_self[:], w_self[:], ACT.Exp).then_inc(sem("w_self"), 1)

            def squares(k):
                act.wait_ge(sem("bv_dev"), k + 1)
                for j in range(B):
                    if not isinstance(k, int):
                        act.wait_ge(sem("bv_mm"), k * B + (j + 1 - B))
                    nc.scalar.activation(hbuf[:, j, :], xb[:, j, :], ACT.Square).then_inc(sem("bv_rows"), 1)

            squares(0)
            with act.Fori(1, K) as k:
                squares(k)
            act.wait_ge(sem("bn_ve"), 1)
            nc.scalar.activation(bn_b[:], bn_a[:], ACT.Sqrt).then_inc(sem("bn_sd"), 1)
            with act.Fori(0, K) as k:
                ln_relu(k, "ga", "ga_ln_h")
                take_tab(k, "ga")
            edge_pass(4, idx_by_src, "s0", ([(1, slot_take_T("s0", "tab")), (0, slot_sqrt("s0", "z")), (1, slot_table("s0", "tab"))],
                                            [(0, slot_act("s0", "slot_n", hbuf[:, 0, :], xb[:, 0, :], ACT.Silu, "slot_h"))]),
                      (("slot_sd", 1), ("slot_h", 1), ("slot_hT", 1), ("slot_rows", 1)))

            def normalized(n, *_):
                act.wait_ge(sem("s1_nmr"), n + 1)
                nc.scalar.activation(hbuf[:, 0, :], xb[:, 1, :], ACT.Relu, bias=nmr[:, 1:2], scale=rstd[:, 1:2]).then_inc(sem("slot_h"), 1)

            def message(unit):
                r = int(unit[1])

                def f(n, *_):
                    if unit[0] == "v":
                        act.wait_ge(sem("slot_out"), slot_count(None, "s1", n))
                    act.wait_ge(sem("slot_P"), slot_count(SLOT_P, "s1", n, unit))
                    ps = psum[:, MSG_BANKS[unit], :]
                    if unit[0] == "u":
                        for q in range(Q):
                            last = nc.scalar.activation(msg_u[r][:, q, :], ps[:, q * P:(q + 1) * P], ACT.Relu, bias=b_rel[:, r * Q + q:r * Q + q + 1])
                    else:
                        last = nc.scalar.activation(tbuf[:, r, 0:D], ps[:, 0:D], ACT.Relu)
                    last.then_inc(sem("slot_taken"), 1)
                return f

            edge_pass(5, idx_by_src, "s1", ([(1, slot_act("s1", "slot_n", xb[:, 0, :], xb[:, 0, :], ACT.Silu, "s1_silu")), (2, slot_take_T("s1", "h")),
                                             (2, message("u0"))],
                                            [(1, slot_sqrt("s1", "x")), (0, slot_sqrt("s1", "z")), (2, message("u1")), (1, normalized),
                                             (2, message("v0")), (2, message("v1"))]),
                      (("slot_h", 1), ("slot_hT", 1), ("slot_sd", 2), ("s1_silu", 1), ("slot_taken", len(SLOT_P["s1"]))))
            act.wait_ge(sem("fi_bias"), 1)
            edge_pass(6, idx_rel, "fi", ([(1, slot_act("fi", "fi_cell", fi_cell, fi_cell, ACT.Tanh, "fi_tanh")), (0, slot_take_T("fi", "i"))],
                                         [(1, layer("1", fi_1, b_1)), (0, gates("ig", BANK_P, ((0, ACT.Sigmoid, fi_i), (2, ACT.Tanh, fi_g)))),
                                          (1, layer("2", fi_2, b_2)), (0, gates("o", BANK_T, ((3, ACT.Sigmoid, fi_o),)))]),
                      (("fi_tanh", 1), ("slot_hT", 1), ("slot_taken", len(SLOT_P["fi"])), ("layer_taken", 2)))

        @block.vector
        def _(dve):
            V = nc.vector
            regs = [dve.alloc_register(f"dve_tile{u}") for u in range(4 * HB)]

            def then(ins, name, value=1):
                ins.then_inc(sem(name), 1)
                dve.wait_ge(sem(name), value)

            norms = {ph: dve.alloc_register("norms_" + ph) for names in NORMS.values() for ph in names}
            for r in norms.values():
                V.reg_mov(r, 0)
            slot_norms = dve.alloc_register("slot_norms")
            V.reg_mov(slot_norms, 0)
            sort_tiles = dve.alloc_register("sort_tiles")
            V.reg_mov(sort_tiles, 0)
            once_n = [0]

            def once(ins):
                once_n[0] += 1
                then(ins, "dve_once", once_n[0])

            def tile_stats(j):
                V.bn_stats(st[:, j, :], xb[:, j, :]).then_inc(sem("ln_st"), 1)

            def ln_rstd(k, ph):
                dve.wait_ge(sem("ln_st"), count(NORMS, k, ph, B))
                V.reg_add(norms[ph], norms[ph], 1)
                for j in range(B):
                    last = V.bn_aggr(mv[:, j, :], st[:, j, :])
                then(last, "ln_mv", count(NORMS, k, ph))
                V.tensor_scalar_add(mv[:, :, 1], mv[:, :, 1], LN_EPS).then_inc(sem("ln_ve"), 1)
                dve.wait_ge(sem("ln_sd"), count(NORMS, k, ph))
                then(V.reciprocal(rstd[:], sd[:]), "ln_rs", count(NORMS, k, ph))

            def ln_stats(k, ph):
                for j in range(B):
                    tile_stats(j)
                ln_rstd(k, ph)

            def ln_bias(k, ph):
                V.scalar_tensor_tensor(out=nmr[:], in0=mv[:, :, 0], scalar=-1.0, in1=rstd[:], op0=ALU.mult,
                                       op1=ALU.mult).then_inc(sem("ln_bias"), 1)

            def take(k, unit, f, also=None):
                for j in range(B):
                    if unit.endswith("_tab"):
                        dve.wait_ge(sem("taken_act"), count(TABLES, k, unit, B, j))
                    else:
                        dve.wait_ge(sem("product"), count(PRODUCTS, k, unit, B, j))
                    f(j, psum[:, 4 + j % BANKS, :]).then_inc(sem("taken_dve"), 1)
                    if also:
                        also(j)

            def copied(to, of):
                return V.tensor_scalar(to, of, 1.0, None, op0=ALU.mult)

            def own_at(k, j):
                return own[:, bass.ds(k * B + j, 1), :].rearrange("p t c -> p (t c)")

            def mean_and_own(k, ph, tiles=range(B)):
                for j in tiles:
                    t = bass.ds(k * B + j, 1)
                    V.scalar_tensor_tensor(out=xb[:, j, :], in0=acc[:, t, 0:D].rearrange("p t c -> p (t c)"), scalar=rdeg[:, t],
                                           in1=own_at(k, j), op0=ALU.mult, op1=ALU.add).then_inc(sem(ph + "_pre"), 1)

            def make_onehots(g, step, u):
                V.tensor_tensor(onehot[:, u:u + HALF, :], iota_row[:].unsqueeze(1).broadcast_to([P, HALF, P]),
                                node_loc[:, ORDER[g], bass.ds(step, HALF)].unsqueeze(2).broadcast_to([P, HALF, P]),
                                ALU.is_equal).then_inc(sem("onehot"), HALF)

            def add_sums(step, g, bank, tile, w, wait=True):
                if wait:
                    dve.wait_ge(sem("mm"), step + (U + STEPS * g + 1))
                dve.wait_ge(sem("summed"), step + (GB + STEPS * g))
                a = acc[:, bass.ds(V.snap(tile, min_val=0, max_val=T - 1), 1), 0:w].rearrange("p t c -> p (t c)")
                V.tensor_tensor(a, a, psum[:, bank, 0:w], ALU.add).then_inc(sem("summed"), 1)

            def norms_done(g):
                for ph in NORMS.get(PASSES[g], ()):
                    dve.wait_ge(sem("ln_mv"), V.snap(norms[ph]))
                    n = list(norms).index(ph)
                    V.memset(carrier[:, n:n + 1], 0.0)

            def step_tiles(o, n, count):
                V.load(regs[0:count * HB], turn_row[0:1, o, bass.ds(n * HB, count * HB)])
                return [regs[m * HB:m * HB + HALF] for m in range(count)]

            def tile_of(buf, t):
                return buf[:, bass.ds(t, 1), :].rearrange("p t c -> p (t c)")

            def slot_pre(ph, g, degrees=False):
                def f(n, r, w):
                    dve.wait_ge(sem("summed"), summed_at[0])
                    if ph != "s1":
                        dve.wait_ge(sem("slot_h"), slot_count(None, ph, n))
                    if degrees:
                        then(V.tensor_scalar(deg[:, 0:1], acc[:, bass.ds(r, 1), D], 1.0, None, op0=ALU.max), "deg", n * 3 + 1)
                        then(V.reciprocal(deg[:, 1:2], deg[:, 0:1]), "deg", n * 3 + 2)
                        then(copied(rdeg[:, bass.ds(r, 1)], deg[:, 1:2]), "deg", n * 3 + 3)
                    V.scalar_tensor_tensor(out=xb[:, 0, :], in0=tile_of(acc, r)[:, 0:D], scalar=rdeg[:, bass.ds(r, 1)],
                                           in1=tile_of(own, r), op0=ALU.mult, op1=ALU.add).then_inc(sem("slot_pre"), 1)
                return f

            def slot_ln(ph, norm):
                j = SLOT_LN[ph].index(norm)

                def f(n, r, w):
                    if norm == "z":
                        dve.wait_ge(sem("slot_pre"), slot_count(None, ph, n))
                    else:
                        dve.wait_ge(sem("s1_x3"), n + 1)
                    at = slot_count(SLOT_LN, ph, n, norm)
                    V.bn_stats(st[:, j, :], xb[:, j, :]).then_inc(sem("slot_st"), 1)
                    dve.wait_ge(sem("slot_st"), at)
                    V.reg_add(slot_norms, slot_norms, 1)
                    V.memset(carrier[:, 6:7], 0.0)
                    then(V.bn_aggr(mv[:, j, :], st[:, j, :]), "slot_mv", at)
                    V.tensor_scalar_add(mv[:, j, 1:2], mv[:, j, 1:2], LN_EPS).then_inc(sem("slot_ve"), 1)
                return f

            def slot_affine(ph, norm, g, b):
                def f(n, r, w):
                    dve.wait_ge(sem("slot_sd"), slot_count(SLOT_LN, ph, n, norm))
                    at = slot_count(SLOT_AFFINE, ph, n, norm)
                    then(V.reciprocal(rstd[:, 0:1], sd[:, 0:1]), "slot_hat", at * 2 - 1)
                    x = xb[:, 0, :]
                    then(V.scalar_tensor_tensor(out=x, in0=x, scalar=mv[:, 0, 0:1], in1=g, op0=ALU.subtract, op1=ALU.mult), "slot_hat", at * 2)
                    V.scalar_tensor_tensor(out=x, in0=x, scalar=rstd[:, 0:1], in1=b, op0=ALU.mult, op1=ALU.add).then_inc(sem("slot_n"), 1)
                return f

            def slot_zero(ph):
                def f(n, r, w):
                    dve.wait_ge(sem("slot_pre"), slot_count(None, ph, n))
                    a = tile_of(acc.bitcast(I32), r)
                    V.tensor_scalar(a, a, 0, None, op0=ALU.bitwise_and).then_inc(sem("slot_zero"), 1)
                return f

            def slot_own(ph, unit, at, b):
                def f(n, r, w):
                    dve.wait_ge(sem("slot_rows"), slot_count(None, ph, n))
                    V.tensor_tensor(tile_of(own, w), psum[:, BANK_P, at:at + D], b, ALU.add).then_inc(sem("slot_taken"), 1)
                return f

            summed_at = [None]
            columns = iter(range(16, 64))

            def edge_pass(g, w, ph=None, front={}, back={}, sems=()):
                norms_done(g)
                make_onehots(g, 0, 0)
                if g in ZEROED:
                    dve.wait_ge(sem("acc_zero"), ZEROED.index(g) + 1)
                else:
                    last = PASSES[g]
                    dve.wait_ge(sem("slot_zero"), 1 + slot_count(None, last, NS - 1))
                    dve.wait_ge(sem("slot_taken"), 1 + slot_count(SLOT_P, last, NS - 1, SLOT_P[last][-1]))
                if ph:
                    dve.wait_ge(sem(ph + "_params"), 16 * NLOADS[ph])

                def turn(i, last):
                    tiles = step_tiles(ORDER[g], i * 2, 2)
                    for u in range(U):
                        if u in front:
                            summed_at[0] = i * U + (GB + STEPS * g + u)
                            front[u](i, V.snap(regs[READ], min_val=0, max_val=SPARE), None)
                        if last and u in back:
                            back[u](i - 1, None, V.snap(regs[WROTE], min_val=0, max_val=SPARE + 1))
                        if u % HALF == 0:
                            make_onehots(g, i * U + (u + HALF), (u + HALF) % U)
                        add_sums(i * U + u, g, u % GB, (tiles[0] + tiles[1])[u], w)

                turn(0, False)
                with dve.Fori(1, TURNS) as i:
                    turn(i, True)
                dve.wait_ge(sem("summed"), GB + STEPS * (g + 1))
                if ph:
                    summed_at[0] = GB + STEPS * (g + 1)
                    V.load([regs[0]], turn_row[0:1, ORDER[g], (TURNS - 1) * 2 * HB + WRITE:(TURNS - 1) * 2 * HB + WRITE + 1])
                    for u in sorted(back):
                        back[u](TURNS - 1, None, V.snap(regs[0], min_val=0, max_val=SPARE + 1))

                    def skip():
                        for name, times in sems:
                            at = next(columns)
                            V.memset(carrier[:, at:at + 1], 0.0).then_inc(sem(name), BY_TURNS * times)

                    def all_of(n, *tiles):
                        if ph != "fi":
                            dve.wait_ge(sem("slot_zero"), slot_count(None, ph, n))
                        for stage in (front, back):
                            for u in sorted(stage):
                                stage[u](n, *tiles)

                    more_slots(V, regs[0], ORDER[g], all_of, skip, regs[1:3])

            V.memset(edges[:, 0:2, :], NP - 1)
            V.memset(edges[:, 2, :], 0)
            V.memset(zrows, 0.0).then_inc(sem("pads_set"), 1)
            V.memset(all_ones, 1.0).then_inc(sem("acts_hT"), FREE)
            V.memset(turn_row[:], 0)
            V.memset(carrier[:, 13:14], 0.0).then_inc(sem("slot_h"), 1)
            V.memset(carrier[:, 11:12], 0.0).then_inc(sem("slot_zero"), 1)
            V.memset(carrier[:, 8:9], 0.0).then_inc(sem("slot_hT"), 1)
            V.memset(carrier[:, 9:10], 0.0).then_inc(sem("slot_taken"), 1)
            V.memset(carrier[:, 10:11], 0.0).then_inc(sem("slot_out"), 1)
            V.memset(carrier[:, 14:15], 0.0).then_inc(sem("layer_taken"), 1)
            V.memset(carrier[:, 7:8], 0.0).then_inc(sem("s1_xout"), 1)
            V.memset(position, 0.0).then_inc(sem("taken_dve"), FREE)
            V.memset(ones[:], 1.0).then_inc(sem("mm"), U)
            V.memset(ring[:, :, D:D + 1], 1.0).then_inc(sem("summed"), GB)
            dve.wait_ge(sem("iota"), 4)
            V.tensor_scalar(ones_last[:], part[:].broadcast_to([P, P]), float(LAST), None, op0=ALU.is_lt)
            V.tensor_scalar(before, iota_row[:], part[:], None, op0=ALU.is_gt)
            V.tensor_scalar(ident[:], iota_row[:], part[:], None, op0=ALU.is_equal).then_inc(sem("consts"), 1)
            dve.wait_ge(sem("edges"), 16 * 9)
            src_sb, dst_sb, rel_sb = (edges[:, a, :] for a in range(3))

            def shifted(to, of, bits, op=ALU.logical_shift_left):
                once(V.tensor_scalar(to, of, bits, None, op0=op))

            shifted(rec_sb[BY_DST], dst_sb, NODE)
            once(V.scalar_tensor_tensor(out=rel_sb, in0=rel_sb, scalar=float(NP), in1=src_sb, op0=ALU.mult, op1=ALU.add))
            once(V.tensor_tensor(rec_sb[BY_DST], rec_sb[BY_DST], rel_sb, ALU.bitwise_or))
            shifted(rec_sb[BY_SRC], src_sb, NODE)
            once(V.tensor_tensor(rec_sb[BY_SRC], rec_sb[BY_SRC], dst_sb, ALU.bitwise_or))
            shifted(src_sb, src_sb, 7, ALU.logical_shift_right)
            V.tensor_copy(key_tile, src_sb).then_inc(sem("rec_by_dst"), 1)
            dve.wait_ge(sem("rec_by_dst"), 1)

            HC = C // 2

            def step_chunks(o):
                dve.wait_ge(sem("last_rec"), 16 * (o + 1))
                shifted(last_tile, last_rec, NODE + 7, ALU.logical_shift_right)
                V.tensor_tensor(bound_row, last_tile, chunk_row, ALU.add).then_inc(sem("bound_row"), 1)
                dve.wait_ge(sem("bound_mm"), o + 1)
                once(V.tensor_copy(bounds.rearrange("p (b c) -> p b c", b=2), psum[:, 0:2, 0:HC]))
                for s in range(SB):
                    once(V.tensor_scalar(junk, bounds, step_no[:, s:s + 1], 0.0, op0=ALU.is_le, op1=ALU.add,
                                         accum_out=chunk_f[:, s:s + 1]))
                once(V.tensor_scalar(chunk_c, chunk_f, float(C - 1), None, op0=ALU.min))
                V.tensor_copy(chunk_i, chunk_c).then_inc(sem("chunk_i"), 1)
                once(V.tensor_tensor(tile_f, step_no, chunk_c, ALU.subtract))
                V.tensor_copy(tile_i, tile_f).then_inc(sem("tile_i"), 1)
                once(V.tensor_scalar(tile_base, tile_f, float(P), None, op0=ALU.mult))

            def step_tables(o):
                dve.wait_ge(sem("edge_rows"), 16 * SB * (o + 1))
                shifted(edge_i, edge_rows, (1 << NODE) - 1, ALU.bitwise_and)
                once(V.tensor_copy(edge_f[:, 0, :, :], edge_i))
                shifted(edge_i, edge_rows, NODE, ALU.logical_shift_right)
                V.memset(junk[:, 0:1], 0.0).then_inc(sem("edge_f"), 1)
                for s in range(SB):
                    last = V.tensor_scalar(edge_f[:, 1, s, :], edge_i[:, s, :], tile_base[:, s:s + 1], None, op0=ALU.subtract)
                last.then_inc(sem("edge_f"), 1)
                dve.wait_ge(sem("edge_T_read"), 2 * o + 2)

            def turn_tables(o):
                dve.wait_ge(sem("tile_row"), 16 * (o + 1))
                halves_of = turn_row[0:1, o, :].rearrange("p (h e) -> p h e", e=HB)
                once(V.tensor_copy(halves_of[:, :, 0:HALF], tile_row[:, 0:STEPS].rearrange("p (h e) -> p h e", e=HALF)))
                n = TURNS + BY_TURNS
                come_t, done_t = come[:, 0:n], done[:, 0:n + 1]
                once(V.memset(come_t, float(BY_TURNS)))
                once(V.memset(done_t, 0.0))
                once(V.tensor_scalar(come_t[:, 0:TURNS], tile_row[:, 0:STEPS].rearrange("p (t u) -> p t u", u=U)[:, :, 0],
                                     float(BY_TURNS), None, op0=ALU.min))
                once(V.tensor_tensor_scan(done_t[:, 1:n + 1], all_ones[0:1, 0:n], come_t, 0.0, op0=ALU.add, op1=ALU.min))
                same, read = tiles_same[:, 0:n], tiles_read[:, 0:n]
                once(V.tensor_tensor(same, done_t[:, 0:n], done_t[:, 1:n + 1], ALU.is_equal))
                once(V.tensor_scalar(read, done_t[:, 0:n], -1.0, float(SPARE), op0=ALU.mult, op1=ALU.add))
                once(V.tensor_tensor(read, read, same, ALU.mult))
                once(V.tensor_tensor(read, read, done_t[:, 0:n], ALU.add))
                once(V.tensor_tensor(same, same, read, ALU.add))
                left_of = left_row[0:1, o, 0:4 * BY_TURNS].rearrange("p (m e) -> p m e", e=4)
                turns_of = turn_row[0:1, o, :].rearrange("p (t e) -> p t e", e=2 * HB)
                for e, tiles in enumerate((read, same, done_t[:, 0:n])):
                    once(V.tensor_copy(turns_of[:, :, READ + e], tiles[:, 0:TURNS]))
                    once(V.tensor_copy(left_of[:, :, e], tiles[:, TURNS:n]))
                once(V.tensor_copy(turns_of[:, 1:TURNS, WROTE], same[:, 0:TURNS - 1]))
                V.tensor_copy(left_row[0:1, o, 4 * T - 1:4 * T], done_t[:, TURNS:TURNS + 1]).then_inc(sem("turn_row"), 1)
                dve.wait_ge(sem("turn_row"), o + 1)

            step_chunks(BY_DST)
            with dve.Fori(0, T) as t:
                then(V.tensor_scalar(is_tile, key_tile, iota_row[:, bass.ds(t, 1)], 0.0, op0=ALU.is_equal, op1=ALU.add,
                                     accum_out=counts[:, bass.ds(t, 1)]), "counts", t + 1)
            dve.wait_ge(sem("count_mm"), 1)
            once(V.tensor_copy(totals, psum[:, 3, 0:T]))
            once(V.tensor_tensor_scan(ends, ones[:, 0:T], totals, 0.0, op0=ALU.mult, op1=ALU.add))
            once(V.tensor_tensor(starts, ends, totals, ALU.subtract))
            once(V.tensor_tensor(starts, starts, psum[:, 2, 0:T], ALU.add))
            with dve.Fori(0, T) as t:
                then(V.tensor_scalar(is_tile, key_tile, iota_row[:, bass.ds(t, 1)], None, op0=ALU.is_equal), "is_tile", t + 1)
                V.tensor_tensor_scan(running, all_ones, is_tile, starts[:, bass.ds(t, 1)], op0=ALU.mult, op1=ALU.add).then_inc(sem("running"), 1)
                dve.wait_ge(sem("running"), t + 1)
                V.reg_add(sort_tiles, sort_tiles, 1)
                then(V.copy_predicated(position, is_tile, running), "position", t + 1)
            dve.wait_ge(sem("position"), V.snap(sort_tiles))
            V.tensor_scalar(pos_i, position, -1.0, None, op0=ALU.add).then_inc(sem("positions"), 1)
            step_tables(BY_DST)
            turn_tables(BY_DST)
            once(V.tensor_scalar(idx_by_dst[:], idx_rel[:], float(NP), float(-NP), op0=ALU.is_ge, op1=ALU.mult))
            once(V.tensor_tensor(idx_by_dst[:], idx_by_dst[:], idx_rel[:], ALU.add))

            def own_hid(ph):
                def f(k):
                    return lambda j, ps: V.tensor_tensor(own_at(k, j), ps[:, D:2 * D], row(ph, "b_hid"), ALU.add)
                return f

            dve.wait_ge(sem("in_params"), 16 * NLOADS["in"])
            with dve.Fori(0, K) as k:
                dve.wait_ge(sem("in_x"), k * 16 + 16)
                ln_stats(k, "in")
                ln_bias(k, "in")
                take(k, "in_u", lambda j, ps: V.tensor_tensor(hbuf[:, j, :], ps[:, 0:D], row("in", "b_in"), ALU.add))
                take(k, "in_tab", own_hid("in")(k))
            step_chunks(BY_SRC)
            step_tables(BY_SRC)
            turn_tables(BY_SRC)
            once(V.memset(own[:, T:T + 2, :], 0.0))
            for g, ph in enumerate(("l0", "l1")):
                edge_pass(g, D + 1 if g == 0 else D, ph,
                          {0: slot_pre(ph, g, g == 0), 2: slot_zero(ph)}, {5: slot_own(ph, "tab", D, row(ph, "b_hid"))},
                          (("slot_pre", 1), ("slot_zero", 1), ("slot_taken", 1)) + ((("deg", 3),) if g == 0 else ()))
            edge_pass(2, D)

            dve.wait_ge(sem("l2_params"), 16 * NLOADS["l2"])
            wg = W["l2", "W_gat"]
            for a, name in enumerate(("att_src", "att_dst")):
                for q in range(Q):
                    n = a * Q + q
                    once(V.tensor_tensor(xb[:, n, :], wbuf[:, q, wg:wg + D], row("l2", name), ALU.mult))
                    V.tensor_reduce(wbuf[:, q, wg + D + a * HEADS:wg + D + (a + 1) * HEADS], heads(xb[:, n, :]),
                                    axis=AX, op=ALU.add).then_inc(sem("w_att"), 1)
            dve.wait_ge(sem("w_att"), 2 * Q)

            def logits(k):
                def f(j, ps):
                    t = bass.ds(k * B + j, 1)
                    copied(a_own[:, t, :].rearrange("p t h -> p (t h)"), ps[:, D:GW])
                    return copied(dst_tab[:, t, 0:HEADS].rearrange("p t h -> p (t h)"), ps[:, GW:GW + HEADS])
                return f

            def l2(k, more):
                dve.wait_ge(sem("l2_r"), k * 16 + 16)
                then(V.tensor_tensor(rb[:], rb[:], over_batch(row("l2", "b_out")), ALU.add), "l2_rb", k + 1)

                def stats(j):
                    if j > 0:
                        dve.wait_ge(sem("taken_dve"), FREE + count(PRODUCTS, k, "l2_u", B, j - 1))
                        tile_stats(j - 1)

                take(k, "l2_u", lambda j, ps: V.tensor_tensor(xb[:, j, :], ps[:, 0:D], rb[:, j, :], ALU.add), stats)
                stats(B)
                ln_rstd(k, "l2")
                ln_bias(k, "l2")
                dve.wait_ge(sem("l2_ln_h"), k * B + B)
                then(V.tensor_tensor(rb[:], xb[:], hbuf[:], ALU.add), "l2_res", k + 1)
                take(k, "l2_tab", logits(k), (lambda j: mean_and_own(k + 1, "l2", [j])) if more else None)

            mean_and_own(0, "l2")
            batches(dve, l2)
            dve.wait_ge(sem("taken_dve"), FREE + count(PRODUCTS, K - 1, "l2_tab", B))
            V.tensor_reduce(amax[:], a_own[:, :, :].rearrange("p t h -> p h t"), axis=AX, op=ALU.max).then_inc(sem("amax"), 1)
            dve.wait_ge(sem("amax_T"), 1)
            once(V.tensor_reduce(gmax[:], psum[0:HEADS, 0, 0:P], axis=AX, op=ALU.max))
            V.tensor_scalar(gdiag[:], ident[0:HEADS, 0:HEADS], gmax[:], None, op0=ALU.mult).then_inc(sem("gdiag"), 1)
            dve.wait_ge(sem("gmax_mm"), 1)
            once(V.tensor_copy(gmax_b[:], psum[:, 1, 0:HEADS]))
            dmax = dst_tab[:, :, HEADS:2 * HEADS]
            dlog = dst_tab[:, :, 0:HEADS]
            once(V.tensor_tensor(dmax, dlog, gmax_b[:].unsqueeze(1).broadcast_to([P, T, HEADS]), ALU.add))
            V.scalar_tensor_tensor(out=dmax, in0=dmax, scalar=SLOPE, in1=dmax, op0=ALU.mult, op1=ALU.max).then_inc(sem("dst_tab"), 1)

            g = GAT
            norms_done(g)

            def gat_logits(n, r):
                if not isinstance(n, int) or n > 0:
                    dve.wait_ge(sem("edge_w"), n)
                if r < 2:
                    for v in range(HALF):
                        dve.wait_ge(slot_sem(r, v), n * 4 + (16 * (filled(g, r) + 1) - 4 * r))
                else:
                    dve.wait_ge(slot_sem(r, 0), n * (4 * HALF) + HALF * (16 - 4 * r))
                dve.wait_ge(sem("log_mm"), n + 1)
                then(V.tensor_tensor(zlog[:], ps_log[:, :, 0:HEADS], gat_ring[r][:, :, D:GW], ALU.add), "z", n * 2 + 1)
                then(V.scalar_tensor_tensor(out=zlog2[:], in0=zlog[:], scalar=SLOPE, in1=zlog[:], op0=ALU.mult, op1=ALU.max), "z", n * 2 + 2)
                V.tensor_tensor(zlog[:], zlog2[:], ps_log[:, :, HEADS:2 * HEADS], ALU.subtract).then_inc(sem("z_less"), 1)

            def gat_half(n, r, tiles):
                first = isinstance(n, int) and n == 0
                dve.wait_ge(sem("edge_w"), n + 1)
                if not first:
                    dve.wait_ge(sem("mm"), n * HALF + (U + STEPS * g))
                for v in range(HALF):
                    if not first:
                        add_sums((n - 1) * HALF + v, g, v, tiles[v], GW, wait=False)
                    V.tensor_tensor(heads(gat_ring[r][:, v, 0:D]), heads(gat_ring[r][:, v, 0:D]),
                                    gat_ring[r][:, v, D:GW].unsqueeze(2).broadcast_to([P, HEADS, DH]), ALU.mult).then_inc(sem("msg"), 1)
                if not isinstance(n, int) or n + 1 < HALVES:
                    gat_logits(n + 1, (r + 1) % 4)
                if not isinstance(n, int) or n + 3 < HALVES:
                    make_onehots(g, (n + 3) * HALF, (r + 3) % 4 * HALF)

            for n in range(3):
                make_onehots(g, n * HALF, n * HALF)
            dve.wait_ge(sem("acc_zero"), ZEROED.index(g) + 1)
            gat_logits(0, 0)
            def last_tiles(n, count):
                if isinstance(n, int) and n == 0:
                    return [None] + step_tiles(BY_DST, 0, count - 1)
                return step_tiles(BY_DST, n - 1, count)

            by_halves(dve, gat_half, last_tiles)
            for v, tile in enumerate(step_tiles(BY_DST, HALVES - 1, 1)[0]):
                add_sums((HALVES - 1) * HALF + v, g, v, tile, GW)
            dve.wait_ge(sem("summed"), GB + STEPS * (g + 1))

            once(V.tensor_tensor(w_self[:], a_own[:], dlog, ALU.add))
            once(V.scalar_tensor_tensor(out=w_self[:], in0=w_self[:], scalar=SLOPE, in1=w_self[:], op0=ALU.mult, op1=ALU.max))
            once(V.tensor_tensor(w_self[:], w_self[:], dmax, ALU.subtract))
            V.tensor_scalar(w_self[:], w_self[:], 0.0, None, op0=ALU.min).then_inc(sem("zs_clamped"), 1)
            dve.wait_ge(sem("ga_params"), 16 * NLOADS["ga"])
            dve.wait_ge(sem("w_self"), 1)

            def by_head(ap):
                return ap.rearrange("p j (h d) -> p j h d", h=HEADS)

            def over_dim(ap):
                return ap.unsqueeze(3).broadcast_to([P, B, HEADS, DH])

            with dve.Fori(0, K) as k:
                t = bass.ds(k * B, B)
                dve.wait_ge(sem("ga_xh"), k * 16 + 16)
                then(V.tensor_tensor(by_head(xb[:]), by_head(tbuf[:, :, 0:D]), over_dim(w_self[:, t, :]), ALU.mult), "ga_own", k * 4 + 1)
                V.tensor_tensor(xb[:], xb[:], acc[:, t, 0:D], ALU.add)
                then(V.tensor_tensor(den[:], acc[:, t, D:GW], w_self[:, t, :], ALU.add), "ga_own", k * 4 + 2)
                then(V.reciprocal(den[:], den[:]), "ga_own", k * 4 + 3)
                then(V.tensor_tensor(by_head(xb[:]), by_head(xb[:]), over_dim(den[:]), ALU.mult), "ga_own", k * 4 + 4)
                V.tensor_tensor(acc[:, t, 0:D], xb[:], over_batch(row("ga", "bias")), ALU.add).then_inc(sem("bs_rows"), 1)
                dve.wait_ge(sem("bs_rows"), k + 1)
            dve.wait_ge(sem("bs_mm"), T)
            once(V.tensor_scalar(bn_mean[:], psum[:, 0, 0:D], 1.0 / N, None, op0=ALU.mult))

            def deviations(k):
                t = bass.ds(k * B, B)
                if not isinstance(k, int):
                    dve.wait_ge(sem("bv_rows"), k * B)
                V.tensor_tensor(xb[:], acc[:, t, 0:D], over_batch(bn_mean[:]), ALU.subtract).then_inc(sem("bv_dev"), 1)

            deviations(0)
            with dve.Fori(1, K) as k:
                deviations(k)
            dve.wait_ge(sem("bv_mm"), T)
            V.tensor_scalar(bn_a[:], psum[:, 1, 0:D], 1.0 / N, LN_EPS, op0=ALU.mult, op1=ALU.add).then_inc(sem("bn_ve"), 1)
            dve.wait_ge(sem("bn_sd"), 1)
            once(V.reciprocal(bn_a[:], bn_b[:]))
            once(V.tensor_tensor(bn_a[:], bn_a[:], row("ga", "gamma"), ALU.mult))
            once(V.tensor_tensor(bn_b[:], bn_mean[:], bn_a[:], ALU.mult))
            once(V.tensor_tensor(bn_b[:], row("ga", "beta"), bn_b[:], ALU.subtract))
            def ga_x2(k, j):
                n = k * B + (j + 1)
                then(V.tensor_tensor(xb[:, j, :], acc[:, bass.ds(k * B + j, 1), 0:D].rearrange("p t c -> p (t c)"), bn_a[:], ALU.mult),
                     "ga_scaled", n)
                then(V.tensor_tensor(xb[:, j, :], xb[:, j, :], rb[:, j, :], ALU.add), "ga_x2", n)
                tile_stats(j)

            def ga_residual(k):
                dve.wait_ge(sem("ga_r"), k * 16 + 16)
                then(V.tensor_tensor(rb[:], rb[:], over_batch(bn_b[:]), ALU.add), "ga_rb", k + 1)

            def ga(k, more):
                ln_rstd(k, "ga")
                ln_bias(k, "ga")

                def next_x2(j):
                    if j == 0:
                        dve.wait_ge(sem("ga_rstored"), k * 16 + 16)
                        ga_residual(k + 1)
                    ga_x2(k + 1, j)

                take(k, "ga_tab", lambda j, ps: V.tensor_tensor(own_at(k, j), ps[:, 0:D], row("ga", "b_next"), ALU.add),
                     next_x2 if more else None)

            ga_residual(0)
            for j in range(B):
                ga_x2(0, j)
            batches(dve, ga)
            edge_pass(4, D, "s0", {0: slot_pre("s0", 4), 1: both(slot_zero("s0"), slot_ln("s0", "z")),
                                   4: slot_affine("s0", "z", row("s0", "g"), row("s0", "beta"))},
                      {6: slot_own("s0", "tab", 0, row("s0", "b_next"))},
                      tuple((name, 1) for name in ("slot_pre", "slot_zero", "slot_st", "slot_mv", "slot_ve", "slot_n", "slot_taken"))
                      + (("slot_hat", 2),))

            def slot_norms_done(at):
                dve.wait_ge(sem("slot_mv"), V.snap(slot_norms))
                V.memset(carrier[:, at:at + 1], 0.0)

            slot_norms_done(12)

            def residual(n, r, w):
                dve.wait_ge(sem("slot_h"), slot_count(None, "s1", n))
                dve.wait_ge(sem("s1_silu"), n + 1)
                dve.wait_ge(sem("s1_res"), n + 1)
                dve.wait_ge(sem("s1_xout"), n + 1)
                V.tensor_tensor(xb[:, 1, :], xb[:, 0, :], rb[:, 0, :], ALU.add).then_inc(sem("s1_x3"), 1)

            def residual_norm(n, r, w):
                dve.wait_ge(sem("slot_sd"), slot_count(SLOT_LN, "s1", n, "x"))
                then(V.reciprocal(rstd[:, 1:2], sd[:, 1:2]), "s1_rstd", n + 1)
                V.scalar_tensor_tensor(out=nmr[:, 1:2], in0=mv[:, 1, 0:1], scalar=-1.0, in1=rstd[:, 1:2], op0=ALU.mult,
                                       op1=ALU.mult).then_inc(sem("s1_nmr"), 1)

            edge_pass(5, D, "s1", {3: slot_pre("s1", 5), 4: slot_zero("s1"), 5: slot_ln("s1", "z"),
                                   8: slot_affine("s1", "z", row("s1", "g"), row("s1", "beta"))},
                      {1: residual, 2: slot_ln("s1", "x"), 7: residual_norm},
                      tuple((name, 1) for name in ("slot_pre", "slot_zero", "slot_n", "s1_x3", "s1_rstd", "s1_nmr"))
                      + (("slot_st", 2), ("slot_mv", 2), ("slot_ve", 2), ("slot_hat", 2)))
            slot_norms_done(15)

            dve.wait_ge(sem("fi_params"), 16 * NLOADS["fi"])
            V.tensor_tensor(b_ih, b_ih, b_hh, ALU.add).then_inc(sem("fi_bias"), 1)

            def fi_take_sums(n, r, w):
                dve.wait_ge(sem("summed"), summed_at[0])
                copied(fi_sums, tile_of(acc, r)[:, 0:D]).then_inc(sem("fi_sums"), 1)

            def fi_cells(n, r, w):
                dve.wait_ge(sem("slot_taken"), 1 + slot_count(SLOT_P, "fi", n, "ig"))
                V.tensor_tensor(fi_cell, fi_i, fi_g, ALU.mult).then_inc(sem("fi_cell"), 1)

            def fi_states(n, r, w):
                dve.wait_ge(sem("fi_tanh"), n + 1)
                dve.wait_ge(sem("slot_taken"), 1 + slot_count(SLOT_P, "fi", n, "o"))
                V.tensor_tensor(fi_state, fi_o, fi_cell, ALU.mult).then_inc(sem("fi_state"), 1)

            def fi_result(n, r, w):
                dve.wait_ge(sem("layer_P"), layer_count(n, "3"))
                dve.wait_ge(sem("slot_out"), slot_count(None, "fi", n))
                V.tensor_tensor(fi_3, psum[:, BANK_LAYERS, 0:D], row("fi", "b3"), ALU.add).then_inc(sem("layer_taken"), 1)
                dve.wait_ge(sem("layer_taken"), 1 + layer_count(n, "3"))
                dve.wait_ge(sem("slot_res"), n + 1)
                V.tensor_tensor(tbuf[:, 0, 0:D], fi_3, rb[:, 1, :], ALU.add).then_inc(sem("fi_y"), 1)

            edge_pass(6, D, "fi", {0: fi_take_sums}, {0: fi_cells, 2: fi_states, 9: fi_result},
                      tuple((name, 1) for name in ("fi_sums", "fi_cell", "fi_state", "fi_y", "layer_taken")))


_TRANSPOSED = ("L2_gnn_W0", "L2_gnn_W1", "L3_gnn_W_rel", "L3_gnn_W_ih", "L3_gnn_W1", "L3_gnn_W2", "L3_gnn_W3")


def kernel(**inputs):
    import numpy as _np
    import concourse.bacc as _bacc
    from concourse import mybir as _mybir
    from concourse.bass_utils import run_bass_kernel_spmd as _run

    nc = _bacc.Bacc("TRN2", target_bir_lowering=False, num_devices=1)
    arrays, io = {}, {}
    for name, value in inputs.items():
        a = _np.asarray(value)
        if name in _TRANSPOSED:
            a = a.swapaxes(-1, -2)
        a = _np.ascontiguousarray(a)
        arrays["in_" + name] = a
        io[name] = nc.dram_tensor("in_" + name, a.shape, _mybir.dt.from_np(a.dtype), kind="ExternalInput").ap()
    out = nc.dram_tensor("out_x", inputs["x"].shape, _mybir.dt.float32, kind="ExternalOutput").ap()
    build(nc, io, out)
    return _run(nc, [arrays], core_ids=[0]).results[0]["out_x"]
```
